# Optimizing a Trainium2 kernel written in Bass

```python
import numpy as np
import jax
import jax.numpy as jnp

def _softmax(x, axis=-1):
    return jax.nn.softmax(x, axis=axis)

def _gelu(x):
    return jax.nn.gelu(x, approximate=True)

def _silu(x):
    return jax.nn.silu(x)

def _sigmoid(x):
    return jax.nn.sigmoid(x)

def _layernorm(x, axis=-1, eps=1e-05):
    m = jnp.mean(x, axis=axis, keepdims=True)
    v = jnp.var(x, axis=axis, keepdims=True)
    return (x - m) / jnp.sqrt(v + eps)

def _scatter_add(tgt, idx, src, axis=0):
    return tgt.at[idx].add(src)

def _segment_sum(src, seg, n):
    return jax.ops.segment_sum(src, seg, n)
kernel_name = 'mk_gps_d1_gnn_r8_4cd7d1'

def setup_inputs(seed: int=0):
    np.random.seed(seed)
    _w = jnp.asarray

    def _rec_inputs():
        import jax
        import jax.numpy as jnp
        _gk = jax.random.key(seed)
        x = -0.0002117 + 1 * jax.random.normal(jax.random.fold_in(_gk, 1), (6250, 256), jnp.float32)
        _s = jax.random.randint(jax.random.fold_in(_gk, 2), (100000,), 0, 6250, jnp.int32)
        _d = jax.random.randint(jax.random.fold_in(_gk, 3), (100000,), 0, 6250, jnp.int32)
        _loop = jnp.arange(6250, dtype=jnp.int32)
        src = jnp.concatenate([_s, _d, _loop])
        dst = jnp.concatenate([_d, _s, _loop])
        _o = jnp.argsort(dst, stable=True)
        src = src[_o]
        dst = dst[_o]
        return (x, src, dst)
    x, src, dst = _rec_inputs()

    def _L0_gnn_setup():
        import jax, jax.numpy as jnp
        import numpy as np
        N_NODES = 12500
        N_EDGES = 200000
        IN_FEATS = 256
        OUT_FEATS = 64
        NHEAD = 4
        ALPHA = 0.2
        key = jax.random.key(seed)
        k1, k2, k3, k4, k5, k6 = jax.random.split(key, 6)
        stdv_w = np.sqrt(6.0 / (IN_FEATS + OUT_FEATS * NHEAD))
        stdv_a = np.sqrt(6.0 / (NHEAD + OUT_FEATS))
        return {'x': jax.random.normal(k1, (N_NODES, IN_FEATS), dtype=jnp.float32), 'W': jax.random.uniform(k2, (IN_FEATS, OUT_FEATS * NHEAD), minval=-stdv_w, maxval=stdv_w, dtype=jnp.float32), 'a_l': jax.random.uniform(k3, (1, NHEAD, OUT_FEATS), minval=-stdv_a, maxval=stdv_a, dtype=jnp.float32), 'a_r': jax.random.uniform(k4, (1, NHEAD, OUT_FEATS), minval=-stdv_a, maxval=stdv_a, dtype=jnp.float32), 'row': jax.random.randint(k5, (N_EDGES,), 0, N_NODES, dtype=jnp.int32), 'col': jax.random.randint(k6, (N_EDGES,), 0, N_NODES, dtype=jnp.int32)}
    _L0_gnn_all = _L0_gnn_setup()
    _L0_gnn_in = {k: v for k, v in _L0_gnn_all.items() if k in ('W', 'a_l', 'a_r')}
    del _L0_gnn_all

    def _L0_mix_setup():
        import jax, jax.numpy as jnp
        import numpy as np
        DIM = 256
        HEADS = 4
        DIM_HEAD = 32
        NUM_MEM = 4
        HIDDEN = HEADS * DIM_HEAD
        SCALE = DIM_HEAD ** (-0.5)

        def rmsnorm(x, g):
            n = jnp.linalg.norm(x, axis=-1, keepdims=True)
            return x / jnp.maximum(n, 1e-12) * g * x.shape[-1] ** 0.5
        key = jax.random.key(seed)
        ks = jax.random.split(key, 8)
        B, N = (4, 2048)
        return {'x': jax.random.normal(ks[0], (B, N, DIM), jnp.float32), 't': jax.random.normal(ks[1], (B,), jnp.float32), 'w_qkv': jax.random.normal(ks[2], (DIM, 3 * HIDDEN), jnp.float32) * 0.02, 'mem_kv': jax.random.normal(ks[3], (2, HEADS, DIM_HEAD, NUM_MEM), jnp.float32), 'w_out': jax.random.normal(ks[4], (HIDDEN, DIM), jnp.float32) * 0.02, 'b_out': jnp.zeros((DIM,), jnp.float32), 'g_out': jnp.ones((DIM,), jnp.float32), 'g_pre': jnp.ones((DIM,), jnp.float32)}
    _L0_mix_all = _L0_mix_setup()
    _L0_mix_in = {k: v for k, v in _L0_mix_all.items() if k in ('t', 'w_qkv', 'mem_kv', 'w_out', 'b_out', 'g_out', 'g_pre')}
    del _L0_mix_all

    def _L0_ffn_setup():
        import jax, jax.numpy as jnp
        import numpy as np
        TOP_K = 2
        LN_EPS = 1e-05
        key = jax.random.key(seed)
        ks = jax.random.split(key, 8)
        B, S, D, E, H = (16, 1024, 256, 8, 1024)
        x = jax.random.normal(ks[0], (B, S, D), dtype=jnp.float32)
        Wr = jax.random.normal(ks[1], (D, E), dtype=jnp.float32) * 0.1
        br = jnp.zeros((E,), dtype=jnp.float32)
        ln_g = jnp.ones((E, D), dtype=jnp.float32)
        ln_b = jnp.zeros((E, D), dtype=jnp.float32)
        W1 = jax.random.normal(ks[2], (E, D, H), dtype=jnp.float32) * (1.0 / np.sqrt(D))
        b1 = jnp.zeros((E, H), dtype=jnp.float32)
        W2 = jax.random.normal(ks[3], (E, H, D), dtype=jnp.float32) * (1.0 / np.sqrt(H))
        b2 = jnp.zeros((E, D), dtype=jnp.float32)
        return {'x': x, 'Wr': Wr, 'br': br, 'ln_g': ln_g, 'ln_b': ln_b, 'W1': W1, 'b1': b1, 'W2': W2, 'b2': b2}
    _L0_ffn_all = _L0_ffn_setup()
    _L0_ffn_in = {k: v for k, v in _L0_ffn_all.items() if k in ('Wr', 'br', 'ln_g', 'ln_b', 'W1', 'b1', 'W2', 'b2')}
    del _L0_ffn_all
    return {'x': x, 'src': src, 'dst': dst, 'L0_gnn_W': _L0_gnn_in['W'], 'L0_gnn_a_l': _L0_gnn_in['a_l'], 'L0_gnn_a_r': _L0_gnn_in['a_r'], 'L0_mix_t': _L0_mix_in['t'], 'L0_mix_w_qkv': _L0_mix_in['w_qkv'], 'L0_mix_mem_kv': _L0_mix_in['mem_kv'], 'L0_mix_w_out': _L0_mix_in['w_out'], 'L0_mix_b_out': _L0_mix_in['b_out'], 'L0_mix_g_out': _L0_mix_in['g_out'], 'L0_mix_g_pre': _L0_mix_in['g_pre'], 'L0_ffn_Wr': _L0_ffn_in['Wr'], 'L0_ffn_br': _L0_ffn_in['br'], 'L0_ffn_ln_g': _L0_ffn_in['ln_g'], 'L0_ffn_ln_b': _L0_ffn_in['ln_b'], 'L0_ffn_W1': _L0_ffn_in['W1'], 'L0_ffn_b1': _L0_ffn_in['b1'], 'L0_ffn_W2': _L0_ffn_in['W2'], 'L0_ffn_b2': _L0_ffn_in['b2']}

def reference(x, src, dst, L0_gnn_W, L0_gnn_a_l, L0_gnn_a_r, L0_mix_t, L0_mix_w_qkv, L0_mix_mem_kv, L0_mix_w_out, L0_mix_b_out, L0_mix_g_out, L0_mix_g_pre, L0_ffn_Wr, L0_ffn_br, L0_ffn_ln_g, L0_ffn_ln_b, L0_ffn_W1, L0_ffn_b1, L0_ffn_W2, L0_ffn_b2):
    import jax
    import jax.numpy as jnp

    def _L0_gnn_ref(x, W, a_l, a_r, row, col):
        import jax, jax.numpy as jnp
        import numpy as np
        N_NODES = 12500
        N_EDGES = 200000
        IN_FEATS = 256
        OUT_FEATS = 64
        NHEAD = 4
        ALPHA = 0.2
        n = x.shape[0]
        h = (x @ W).reshape(n, NHEAD, OUT_FEATS)
        h = jnp.where(jnp.isnan(h), 0.0, h)
        h_l = (a_l * h).sum(-1)
        h_r = (a_r * h).sum(-1)
        e = h_l[row] + h_r[col]
        e = jnp.where(e > 0, e, ALPHA * e)
        m = jax.ops.segment_max(e, row, num_segments=n)
        m = jnp.where(jnp.isfinite(m), m, 0.0)
        ex = jnp.exp(e - m[row])
        denom = jax.ops.segment_sum(ex, row, num_segments=n)
        att = ex / (denom[row] + 1e-16)
        msg = att[:, :, None] * h[col]
        out = jax.ops.segment_sum(msg, row, num_segments=n)
        return out.reshape(n, NHEAD * OUT_FEATS)

    def _L0_mix_ref(x, t, w_qkv, mem_kv, w_out, b_out, g_out, g_pre):
        import jax, jax.numpy as jnp
        import numpy as np
        DIM = 256
        HEADS = 4
        DIM_HEAD = 32
        NUM_MEM = 4
        HIDDEN = HEADS * DIM_HEAD
        SCALE = DIM_HEAD ** (-0.5)

        def rmsnorm(x, g):
            n = jnp.linalg.norm(x, axis=-1, keepdims=True)
            return x / jnp.maximum(n, 1e-12) * g * x.shape[-1] ** 0.5
        b, n, c = x.shape
        xn = rmsnorm(x, g_pre)
        qkv = xn @ w_qkv
        q, k, v = jnp.split(qkv, 3, axis=-1)

        def to_heads(z):
            return z.reshape(b, n, HEADS, DIM_HEAD).transpose(0, 2, 3, 1)
        q, k, v = map(to_heads, (q, k, v))
        mk = jnp.broadcast_to(mem_kv[0], (b, HEADS, DIM_HEAD, NUM_MEM))
        mv = jnp.broadcast_to(mem_kv[1], (b, HEADS, DIM_HEAD, NUM_MEM))
        k = jnp.concatenate([mk, k], axis=-1)
        v = jnp.concatenate([mv, v], axis=-1)
        q = jax.nn.softmax(q, axis=-2) * SCALE
        k = jax.nn.softmax(k, axis=-1)
        context = jnp.einsum('bhdn,bhen->bhde', k, v)
        out = jnp.einsum('bhde,bhdn->bhen', context, q)
        out = out.transpose(0, 3, 1, 2).reshape(b, n, HIDDEN)
        out = rmsnorm(out @ w_out + b_out, g_out)
        return out + x

    def _L0_ffn_ref(x, Wr, br, ln_g, ln_b, W1, b1, W2, b2):
        import jax, jax.numpy as jnp
        import numpy as np
        TOP_K = 2
        LN_EPS = 1e-05
        B, S, D = x.shape
        N = B * S
        xt = x.reshape(N, D)
        logits = xt @ Wr + br
        probs = jax.nn.softmax(logits, axis=-1)
        top_p, top_idx = jax.lax.top_k(probs, TOP_K)
        weights = top_p / top_p.sum(axis=-1, keepdims=True)
        mu = xt.mean(axis=-1, keepdims=True)
        var = ((xt - mu) ** 2).mean(axis=-1, keepdims=True)
        xn = (xt - mu) * jax.lax.rsqrt(var + LN_EPS)
        xe = xn[None, :, :] * ln_g[:, None, :] + ln_b[:, None, :]
        h = jax.nn.gelu(jnp.einsum('end,edh->enh', xe, W1) + b1[:, None, :], approximate=False)
        y = jnp.einsum('enh,ehd->end', h, W2) + b2[:, None, :]
        y_tok = jnp.transpose(y, (1, 0, 2))
        sel = jnp.take_along_axis(y_tok, top_idx[:, :, None], axis=1)
        out = (weights[:, :, None] * sel).sum(axis=1)
        return out.reshape(B, S, D)
    xn = _layernorm(x, axis=-1)
    x = x + _L0_gnn_ref(xn, L0_gnn_W, L0_gnn_a_l, L0_gnn_a_r, src, dst) + _L0_mix_ref(xn[None], L0_mix_t, L0_mix_w_qkv, L0_mix_mem_kv, L0_mix_w_out, L0_mix_b_out, L0_mix_g_out, L0_mix_g_pre)[0]
    x = x + _L0_ffn_ref(_layernorm(x, axis=-1)[None], L0_ffn_Wr, L0_ffn_br, L0_ffn_ln_g, L0_ffn_ln_b, L0_ffn_W1, L0_ffn_b1, L0_ffn_W2, L0_ffn_b2)[0]
    return x

_drawn_inputs = setup_inputs


def setup_inputs(seed=0):
    import zlib

    import numpy as np

    out = dict(_drawn_inputs(seed))
    spreads = {'L0_mix_b_out': (0.0, 0.1),
     'L0_mix_g_out': (1.0, 0.2),
     'L0_mix_g_pre': (1.0, 0.6),
     'L0_ffn_br': (0.0, 0.1),
     'L0_ffn_ln_g': (1.0, 0.2),
     'L0_ffn_ln_b': (0.0, 0.347),
     'L0_ffn_b1': (0.0, 0.331),
     'L0_ffn_b2': (0.0, 0.1)}
    factors = {'L0_mix_w_qkv': 8.0, 'L0_mix_mem_kv': 8.0, 'L0_mix_w_out': 8.0}
    for name, (base, spread) in spreads.items():
        noise = np.random.default_rng([zlib.crc32(name.encode()), seed]).standard_normal(out[name].shape)
        drawn = base * np.exp(spread * noise) if base else spread * noise
        out[name] = jnp.asarray(drawn.astype(out[name].dtype))
    for name, factor in factors.items():
        out[name] = (out[name] * factor).astype(out[name].dtype)
    return out
```

```python
import concourse.bass as bass
from concourse import mybir
from contextlib import ExitStack

FP32 = mybir.dt.float32
BF16 = mybir.dt.bfloat16
I32 = mybir.dt.int32
ALU = mybir.AluOpType
ACT = mybir.ActivationFunctionType
AX = mybir.AxisListType.X


class Chain:

    def __init__(self, engine, sem):
        self.engine, self.sem, self.base, self.k, self.closed = engine, sem, 0, 0, True

    def turn(self, i, per):
        if self.closed:
            self.start, self.closed = self.base, False
        self.at, self.k, self.per = i * per + self.start, 0, per
        return self

    def straight(self):
        self.start = self.at = self.base
        self.k, self.per, self.closed = 0, None, False
        return self

    def link(self, instruction):
        self.k += 1
        instruction.then_inc(self.sem, 1)
        self.engine.wait_ge(self.sem, self.at + self.k)

    def tick(self, instruction):
        self.k += 1
        instruction.then_inc(self.sem, 1)
        return self.at + self.k

    def need(self, value):
        self.engine.wait_ge(self.sem, value)

    def publish(self, instruction, sem, count):
        instruction.then_inc(sem, 1)
        self.engine.wait_ge(sem, count)

    def done(self, turns):
        assert self.per in (None, self.k), (self.k, self.per)
        self.base, self.closed = self.start + turns * self.k, True


def first_then_rest(engine, turns, body):
    body(0)
    with engine.Fori(1, turns) as i:
        body(i)


def gps_layer_kernel(nc, x, src, dst, gnn_w, gnn_al, gnn_ar, mix_wqkv, mix_mem, mix_wout, mix_bout,
                     mix_gout, mix_gpre, wr, br, ln_g, ln_b, w1, b1, w2, b2, out):
    P = 128
    N, D = x.shape
    E = src.shape[0]
    NT = (N + P - 1) // P
    LAST = N - (NT - 1) * P
    HEADS, HD = gnn_al.shape[1], gnn_al.shape[2]
    HP = HD + 1
    KC = D // P
    EP = 125
    EC = E // EP
    assert EP * EC == E
    GT = 4
    G = GT * P
    UN = 6
    NG = (E + NT * (G - 1)) // G
    TURNS = (NG + UN - 1) // UN
    NG = TURNS * UN
    assert TURNS <= P
    NSLOT = NG * G
    COLBITS = 13
    assert NT * P <= 1 << COLBITS
    PADCOL = NT * P - 1
    PADREC = (P << COLBITS) + PADCOL
    TW = HEADS * HP + 6
    SK = 10
    STURNS = EC // SK
    assert SK * STURNS == EC
    MH, MD, MM = mix_mem.shape[1], mix_mem.shape[2], mix_mem.shape[3]
    HID = MH * MD
    QW = 3 * HID
    NE, FH = w1.shape[0], w1.shape[2]
    FC = FH // P
    FT = 4
    BIG = 1e30
    FAR = 2.0 ** 100
    LN_EPS = 1e-5

    slots = nc.dram_tensor("slots", [NSLOT, 1], I32).ap()
    table = nc.dram_tensor("table", [NT * P, TW], FP32).ap()

    top = ExitStack()

    def sem(name):
        return top.enter_context(nc.semaphore(name))

    def sb(stack, name, shape, dt=FP32):
        return stack.enter_context(nc.sbuf_tensor(name, shape, dt))

    def pb(stack, name, shape, dt=FP32):
        return stack.enter_context(nc.psum_tensor(name, shape, dt))

    with top:
        X = sb(top, "X", [P, NT, D])
        ident = sb(top, "ident", [P, P])
        identb = sb(top, "identb", [P, P], BF16)
        iota_row = sb(top, "iota_row", [P, P])
        iota_i = sb(top, "iota_i", [P, 1], I32)
        iota_p = sb(top, "iota_p", [P, 1])
        ones = sb(top, "ones", [P, P])
        hl = sb(top, "hl", [P, NT, HEADS])
        start_row = sb(top, "start_row", [P, NT])
        block_of = sb(top, "block_of", [1, NG], I32)
        acc = sb(top, "acc", [P, NT, HEADS * HP])

        binning_and_nodes(nc, locals())
        attention(nc, locals())
        experts(nc, locals())


def binning_and_nodes(nc, v):
    P, N, D, E, NT, LAST, HEADS, HD, HP, KC = (v[k] for k in ("P", "N", "D", "E", "NT", "LAST", "HEADS", "HD", "HP", "KC"))
    EP, EC, G, NG, NSLOT, COLBITS, PADREC, SK, STURNS, TW = (v[k] for k in ("EP", "EC", "G", "NG", "NSLOT", "COLBITS", "PADREC", "SK", "STURNS", "TW"))
    MH, MD, MM, HID, QW, BIG, LN_EPS = (v[k] for k in ("MH", "MD", "MM", "HID", "QW", "BIG", "LN_EPS"))
    X, ident, identb, iota_row, iota_i, iota_p, ones, hl, start_row, block_of, acc = (v[k] for k in ("X", "ident", "identb", "iota_row", "iota_i", "iota_p", "ones", "hl", "start_row", "block_of", "acc"))
    sem, sb, pb, slots, table = v["sem"], v["sb"], v["pb"], v["slots"], v["table"]
    x = v["x"]
    LG = G.bit_length() - 1
    PAIR = MM

    with ExitStack() as s:
        records = sb(s, "records", [EP, 2, EC], I32)
        qkv = sb(s, "qkv", [P, NT, QW + 1])
        lists = acc[0:EP, :, :].rearrange("p a b -> p (a b)")

        def edge_list(n, dt=FP32):
            view = lists[:, n * EC:(n + 1) * EC]
            return view if dt == FP32 else view.bitcast(dt)

        rows_i, cols_i, bins_i = (edge_list(n, I32) for n in range(3))
        bin_f, mask, scan, rank = (edge_list(n) for n in range(3, 7))
        part = edge_list(0)
        counts = sb(s, "counts", [EP, NT])
        before = sb(s, "before", [EP, NT])
        groups_i = sb(s, "groups_i", [P, NT], I32)
        groups_f = sb(s, "groups_f", [P, NT])
        zeros = sb(s, "zeros", [P, NT])
        col_i = sb(s, "col_i", [NT, 1], I32)
        col_f = sb(s, "col_f", [NT, 1])
        start_col = sb(s, "start_col", [NT, 1])
        tri = sb(s, "tri", [P, P])
        giota = sb(s, "giota", [NT, NG])
        reached = giota
        padrec = sb(s, "padrec", [P, NSLOT // P], I32)
        block_f = sb(s, "block_f", [1, NG])

        sl, sc, sd, spe, sdv, sfill = (sem(n) for n in ("edges_loaded", "constants_made", "list_chain", "counts_summed", "counts_ready", "slots_filled"))
        x_loaded = sem("x_loaded")
        with ExitStack() as s2:
            ps_before = pb(s2, "ps_before", [EP, 512])
            ps_total = pb(s2, "ps_total", [P, 512])
            ps_col = pb(s2, "ps_col", [P, 512])
            ps_block = pb(s2, "ps_block", [P, 512])
            block = s2.enter_context(nc.Block())

            @block.sync
            def _(sp):
                sp.dma_start(rows_i, v["src"].rearrange("(p c) -> p c", p=EP)).then_inc(sl, 16)
                sp.dma_start(cols_i, v["dst"].rearrange("(p c) -> p c", p=EP)).then_inc(sl, 16)
                sp.wait_ge(sc, 1)
                sp.dma_start(slots.rearrange("(p c) o -> p (c o)", p=P), padrec[:]).then_inc(sfill, 16)
                sp.wait_ge(sfill, 16)

            @block.scalar
            def _(act):
                act.wait_ge(sc, 7)
                for t0 in range(0, NT - 1, 8):
                    n = min(8, NT - 1 - t0)
                    act.dma_start(X[:, t0:t0 + n, :], x[t0 * P:(t0 + n) * P, :].rearrange("(t p) f -> p t f", p=P)).then_inc(x_loaded, 16)
                act.dma_start(X[0:LAST, NT - 1, :], x[(NT - 1) * P:N, :]).then_inc(x_loaded, 16)
                act.wait_ge(x_loaded, 16 * ((NT - 1 + 7) // 8 + 1))

            @block.gpsimd
            def _(pool):
                pool.memset(padrec[:], PADREC).then_inc(sc, 1)
                pool.iota(iota_row[:], pattern=[[1, P]], base=0, channel_multiplier=0, allow_small_or_imprecise_dtypes=True).then_inc(sc, 1)
                pool.iota(iota_i[:], pattern=[[0, 1]], base=0, channel_multiplier=1).then_inc(sc, 1)
                pool.iota(giota[:], pattern=[[1, NG]], base=0, channel_multiplier=0, allow_small_or_imprecise_dtypes=True).then_inc(sc, 1)
                pool.memset(ones[:], 1.0).then_inc(sc, 1)
                pool.memset(zeros[:], 0.0).then_inc(sc, 1)
                pool.memset(X[:, NT - 1, :], 0.0).then_inc(sc, 1)

            @block.vector
            def _(dve):
                c = Chain(dve, sd)
                dve.wait_ge(sc, 7)
                dve.wait_ge(sl, 32)
                c.straight()
                c.link(dve.tensor_copy(iota_p[:], iota_i[:]))
                c.link(dve.tensor_scalar(ident[:], iota_row[:], iota_p[:], None, ALU.is_equal))
                c.link(dve.tensor_copy(identb[:], ident[:]))
                c.link(dve.tensor_scalar(tri[:], iota_row[:], iota_p[:], None, ALU.is_gt))
                c.link(dve.tensor_single_scalar(bins_i, rows_i, 7, ALU.logical_shift_right))
                c.link(dve.tensor_copy(bin_f, bins_i))
                c.link(dve.tensor_scalar(bins_i, rows_i, P - 1, COLBITS, ALU.bitwise_and, ALU.logical_shift_left))
                c.link(dve.tensor_tensor(records[:, 1, :], bins_i, cols_i, ALU.bitwise_or))
                c.link(dve.memset(rank, 0.0))
                c.link(dve.memset(counts[:], 0.0))
                c.link(dve.memset(start_row[:], 0.0))
                c.link(dve.memset(qkv[:, :, QW:QW + 1], 1.0))
                c.done(1)
                with dve.Fori(0, NT) as b:
                    c.turn(b, 1)
                    c.link(dve.tensor_scalar(mask, bin_f, iota_row[0:EP, bass.ds(b, 1)], None, ALU.is_equal, ALU.add,
                                             accum_out=counts[:, bass.ds(b, 1)]))
                c.done(NT)
                dve.nop().then_inc(sdv, 1)
                dve.wait_ge(spe, 1)
                c.straight()
                c.link(dve.tensor_scalar(groups_i[:], ps_total[:, 0:NT], float(G - 1), None, ALU.add))
                c.link(dve.tensor_single_scalar(groups_i[:], groups_i[:], LG, ALU.logical_shift_right))
                c.link(dve.tensor_copy(groups_f[:], groups_i[:]))
                c.link(dve.tensor_tensor_scan(start_row[:], groups_f[:], zeros[:], 0.0, ALU.add, ALU.add))
                c.link(dve.tensor_tensor(start_row[:], start_row[:], groups_f[:], ALU.subtract))
                c.link(dve.scalar_tensor_tensor(before[:], start_row[0:EP, :], float(G), ps_before[:, 0:NT], ALU.mult, ALU.add))
                c.link(dve.tensor_scalar(col_i[:], ps_col[0:NT, 0:1], float(G - 1), None, ALU.add))
                c.link(dve.tensor_single_scalar(col_i[:], col_i[:], LG, ALU.logical_shift_right))
                c.publish(dve.tensor_copy(col_f[:], col_i[:]), sdv, 2)
                dve.wait_ge(spe, 2)
                c.link(dve.tensor_copy(start_col[:], ps_col[0:NT, 1:2]))
                c.done(1)
                c.straight()
                c.publish(dve.tensor_scalar(reached[:], giota[:], start_col[:], None, ALU.is_ge), sdv, 3)
                c.done(1)
                with dve.Fori(0, NT) as b:
                    c.turn(b, 4)
                    c.link(dve.tensor_scalar(mask, bin_f, iota_row[0:EP, bass.ds(b, 1)], None, ALU.is_equal))
                    c.link(dve.tensor_tensor_scan(scan, mask, mask, before[:, bass.ds(b, 1)], ALU.add, ALU.max))
                    c.link(dve.tensor_tensor(part, scan, mask, ALU.mult))
                    c.link(dve.tensor_tensor(rank, rank, part, ALU.add))
                c.done(NT)
                dve.wait_ge(spe, 3)
                c.straight()
                c.link(dve.tensor_scalar(records[:, 0, :], rank, -1.0, None, ALU.add))
                c.link(dve.tensor_scalar(block_of[:], ps_block[0:1, 0:NG], -1.0, None, ALU.add))
                c.done(1)

            @block.tensor
            def _(pe):
                pe.wait_ge(sdv, 1)
                pe.matmul(ps_before[:, 0:NT], tri[0:EP, 0:EP], counts[:], start=True, stop=True)
                pe.matmul(ps_total[:, 0:NT], ones[0:EP, :], counts[:], start=True, stop=True)
                pe.matmul(ps_col[0:NT, 0:1], counts[:], ones[0:EP, 0:1], start=True, stop=True).then_inc(spe, 1)
                pe.wait_ge(sdv, 2)
                pe.matmul(ps_col[0:NT, 1:2], tri[0:NT, 0:NT], col_f[:], start=True, stop=True).then_inc(spe, 1)
                pe.wait_ge(sdv, 3)
                pe.matmul(ps_block[0:1, 0:NG], ones[0:NT, 0:1], reached[:], start=True, stop=True).then_inc(spe, 1)

        nodes(nc, {**v, **locals()})


def nodes(nc, v):
    P, N, D, E, NT, LAST, HEADS, HD, HP, KC = (v[k] for k in ("P", "N", "D", "E", "NT", "LAST", "HEADS", "HD", "HP", "KC"))
    EP, EC, G, NG, NSLOT, COLBITS, PADREC, SK, STURNS, TW = (v[k] for k in ("EP", "EC", "G", "NG", "NSLOT", "COLBITS", "PADREC", "SK", "STURNS", "TW"))
    MH, MD, MM, HID, QW, BIG, LN_EPS = (v[k] for k in ("MH", "MD", "MM", "HID", "QW", "BIG", "LN_EPS"))
    X, ident, identb, iota_row, iota_i, iota_p, ones, hl, acc = (v[k] for k in ("X", "ident", "identb", "iota_row", "iota_i", "iota_p", "ones", "hl", "acc"))
    sem, sb, pb, slots, table, records, qkv = (v[k] for k in ("sem", "sb", "pb", "slots", "table", "records", "qkv"))
    GW = HEADS * HD

    with ExitStack() as s:
        scratch = acc[:, :, :].rearrange("p a b -> p (a b)")
        used = [0]

        def carve(width):
            at = used[0]
            used[0] += width
            assert used[0] <= NT * HEADS * HP
            return scratch[:, at:at + width]

        w_all = carve(KC * (GW + QW)).rearrange("p (k c) -> p k c", k=KC)
        a_both = carve(2 * GW)
        gpre = carve(KC)
        stats = carve(NT * 6).rearrange("p (t c) -> p t c", t=NT)
        mean = carve(NT)
        var = carve(NT)
        rstd = carve(NT)
        sig = carve(NT)
        rms = carve(NT)
        xn = carve(2 * D).rearrange("p (b c) -> p b c", b=2)
        xnt = carve(2 * D).rearrange("p (b k c) -> p b k c", b=2, k=KC)
        row_tile = carve(2 * HEADS * HP).rearrange("p (b h c) -> p b h c", b=2, h=HEADS)
        prod = carve(2 * GW)
        nanmask = carve(GW)
        h_raw = carve(2 * GW).rearrange("p (b c) -> p b c", b=2)
        hr = carve(NT * HEADS)
        res = carve(NT * HEADS)
        split = carve(NT * 6)
        kcol = carve(HID)
        kmax = carve(4)
        kdiag = carve(HID)
        krow = carve(HID)
        qstat = carve(NT * MH)
        qsum = carve(NT * MH)
        mem_k = carve(MM)
        mem_v = carve(MM)
        mem_e = carve(MM)
        memkt = carve(HID)
        memvt = carve(HID + 1)
        ctx_r = carve(1)
        ctx_n = carve(HID)
        ctx_t = carve(HID)
        blockm = carve(HID)
        wout = carve(D)
        wc = carve(D)
        bout = carve(D)
        gout = carve(D)
        p5 = carve(1)
        p5i = carve(1).bitcast(I32)
        padneg = carve(1)
        ktile = carve(2 * HID).rearrange("p (b c) -> p b c", b=2)
        qt = carve(2 * HID).rearrange("p (b c) -> p b c", b=2)
        qs = carve(2 * HID).rearrange("p (b c) -> p b c", b=2)
        n2 = carve(NT)
        junk = carve(D)
        staged = sb(s, "staged", [EP, 2, 2, SK], I32)

        ps_t = [pb(s, f"ps_t{i}", [P, KC, P]) for i in range(2)]
        ps_g = [pb(s, f"ps_g{i}", [P, 512]) for i in range(2)]
        ps_q = [pb(s, f"ps_q{i}", [P, 512]) for i in range(2)]
        ps_c = pb(s, "ps_c", [P, 512])
        ps_m = pb(s, "ps_m", [P, 512])

        names = ("weights_loaded", "moments_done", "sigma_ready", "act_chain", "dve_chain", "normed", "transposed", "xnt_ready",
                 "projected", "h_copied", "qkv_kept", "heads_kept", "row_ready0", "row_ready1", "rows_stored0", "rows_stored1", "consts2", "records_staged0",
                 "records_staged1", "scattered0", "scattered1", "split_ready", "split_stored", "k_column", "k_column_t", "k_diag", "k_row",
                 "k_shifted", "k_exp", "q_shifted", "q_exp", "k_used", "mem_ready", "mem_t", "mem_t_kept", "context", "context_n", "context_t", "context_t_kept", "wc_done", "wc_kept",
                 "q_scaled", "q_t", "q_t_kept", "mask_made", "records_taken", "mixed", "mix_kept", "mix_sigma", "mix_sigma_done", "gnn_kept")
        S = {n: sem(n) for n in names}
        table_rows = table[:, 0:HEADS * HP].rearrange("(t p) c -> p t c", p=P)
        block = s.enter_context(nc.Block())

        @block.sync
        def _(sp):
            def turn(i, u):
                if not isinstance(i, int) or i > 0:
                    sp.wait_ge(S[f"scattered{u}"], i * 16 * SK)
                j = i * 2 + u
                sp.dma_start(staged[:, u, :, :], records[:, :, bass.ds(j * SK, SK)]).then_inc(S[f"records_staged{u}"], 16)

            def both(i):
                turn(i, 0)
                turn(i, 1)

            with nc.allow_non_contiguous_dma(reason="records of 4 bytes"):
                first_then_rest(sp, STURNS // 2, both)
                if STURNS % 2:
                    turn(STURNS // 2, 0)

        @block.gpsimd
        def _(pool):
            def turn(i, u):
                pool.wait_ge(S[f"records_staged{u}"], (i + 1) * 16)
                pool.sem_inc(S["records_taken"], 1)
                for k in range(SK):
                    pool.indirect_dma_start(slots, bass.IndirectOffsetOnAxis(staged[:, u, 0, k:k + 1], 0),
                                            staged[:, u, 1, k:k + 1], None).then_inc(S[f"scattered{u}"], 16)

            with pool.Fori(0, STURNS // 2) as i:
                turn(i, 0)
                turn(i, 1)
            if STURNS % 2:
                turn(STURNS // 2, 0)
            pool.wait_ge(S["scattered0"], 16 * SK * ((STURNS + 1) // 2))
            pool.wait_ge(S["scattered1"], 16 * SK * (STURNS // 2))

        @block.scalar
        def _(act):
            c = Chain(act, S["act_chain"])
            ld = S["weights_loaded"]
            for dst_, src_ in (
                (w_all[:, :, 0:GW], v["gnn_w"].rearrange("(k p) c -> p k c", p=P)),
                (w_all[:, :, GW:GW + QW], v["mix_wqkv"].rearrange("(k p) c -> p k c", p=P)),
                (a_both[:, 0:GW], v["gnn_ar"].rearrange("a h c -> a (h c)").to_broadcast([P, GW])),
                (a_both[:, GW:2 * GW], v["gnn_al"].rearrange("a h c -> a (h c)").to_broadcast([P, GW])),
                (mem_k, v["mix_mem"][0].rearrange("h d m -> (h d) m")),
                (mem_v, v["mix_mem"][1].rearrange("h d m -> (h d) m")),
                (wout, v["mix_wout"]),
                (bout[0:1, :], v["mix_bout"].rearrange("(a c) -> a c", a=1)),
                (gout, v["mix_gout"].rearrange("(a c) -> a c", a=1).to_broadcast([P, D])),
            ):
                act.dma_start(dst_, src_).then_inc(ld, 16)
            with nc.allow_non_contiguous_dma(reason="a column of scales"):
                act.dma_start(gpre, v["mix_gpre"].rearrange("(k p) -> p k", p=P)).then_inc(ld, 16)
            act.wait_ge(S["moments_done"], 1)
            act.activation(sig, rstd, ACT.Sqrt).then_inc(S["sigma_ready"], 1)
            act.activation(rms, var, ACT.Sqrt).then_inc(S["sigma_ready"], 1)

            def store_row(i, u):
                act.wait_ge(S[f"row_ready{u}"], i + 1)
                act.dma_start(table_rows[:, bass.ds(i * 2 + u, 1), :].rearrange("p a c -> p (a c)"),
                              row_tile[:, u, :, :].rearrange("p h c -> p (h c)")).then_inc(S[f"rows_stored{u}"], 16)

            def tile(i, u):
                t = i * 2 + u
                later = not isinstance(i, int) or i > 0
                if later or u:
                    store_row(i if u else i - 1, 1 - u)
                act.wait_ge(S["transposed"], t + 1)
                if later:
                    act.wait_ge(S["projected"], t - 1)
                act.activation(xnt[:, u, :, :], ps_t[u][:], ACT.Copy).then_inc(S["xnt_ready"], 1)
                act.wait_ge(S["projected"], t + 1)
                if later:
                    act.wait_ge(S["heads_kept"], t - 1)
                act.activation(h_raw[:, u, :], ps_g[u][:, 0:GW], ACT.Copy).then_inc(S["h_copied"], 1)
                act.activation(qkv[:, bass.ds(t, 1), 0:QW].rearrange("p a c -> p (a c)"), ps_q[u][:, 0:QW], ACT.Copy,
                               scale=rms[:, bass.ds(t, 1)]).then_inc(S["qkv_kept"], 1)

            def pair(i):
                tile(i, 0)
                tile(i, 1)

            act.wait_ge(S["normed"], 1)
            first_then_rest(act, NT // 2, pair)
            tile(NT // 2, 0)
            store_row(NT // 2, 0)
            act.wait_ge(S["q_shifted"], 1)
            act.activation(qkv[:, :, 0:HID], qkv[:, :, 0:HID], ACT.Exp).then_inc(S["q_exp"], 1)
            act.wait_ge(S["k_shifted"], 1)
            act.activation(mem_e, mem_k, ACT.Exp, bias=kmax[:, 1:2]).then_inc(S["mem_ready"], 1)

            def ktile_exp(i, u):
                t = i * 2 + u
                if not isinstance(i, int) or i > 0:
                    act.wait_ge(S["k_used"], t - 1)
                act.activation(ktile[:, u, :], qkv[:, bass.ds(t, 1), HID:2 * HID].rearrange("p a c -> p (a c)"), ACT.Exp).then_inc(S["k_exp"], 1)

            def kpair(i):
                ktile_exp(i, 0)
                ktile_exp(i, 1)

            first_then_rest(act, NT // 2, kpair)
            ktile_exp(NT // 2, 0)

            def mix_tile(i, u):
                t = i * 2 + u
                act.wait_ge(S["q_t"], t + 1)
                if not isinstance(i, int) or i > 0:
                    act.wait_ge(S["mixed"], t - 1)
                act.activation(qt[:, u, :], ps_t[u][:, 0, :], ACT.Copy).then_inc(S["q_t_kept"], 1)
                act.wait_ge(S["mixed"], t + 1)
                act.activation(junk, ps_g[u][:, 0:D], ACT.Square, accum_out=n2[:, bass.ds(t, 1)]).then_inc(S["act_chain"], 1)
                act.activation(qkv[:, bass.ds(t, 1), HID:HID + D].rearrange("p a c -> p (a c)"), ps_g[u][:, 0:D], ACT.Copy).then_inc(S["mix_kept"], 1)
                act.wait_ge(S["act_chain"], t + 1)

            def mix_pair(i):
                mix_tile(i, 0)
                mix_tile(i, 1)

            first_then_rest(act, NT // 2, mix_pair)
            mix_tile(NT // 2, 0)
            act.wait_ge(S["mix_kept"], NT)
            act.activation(n2, n2, ACT.Sqrt).then_inc(S["mix_sigma"], 1)
            act.wait_ge(S["split_ready"], 1)
            with nc.allow_non_contiguous_dma(reason="24 bytes of each row"):
                act.dma_start(table[:, HEADS * HP:TW].rearrange("(t p) c -> p t c", p=P),
                              split.rearrange("p (t c) -> p t c", t=NT)).then_inc(S["split_stored"], 16)
            act.wait_ge(S["split_stored"], 16)
            act.wait_ge(S["rows_stored0"], 16 * ((NT + 1) // 2))
            act.wait_ge(S["rows_stored1"], 16 * (NT // 2))

        @block.vector
        def _(dve):
            c = Chain(dve, S["dve_chain"])
            with dve.Fori(0, NT) as t:
                c.turn(t, 1)
                c.link(dve.bn_stats(stats[:, bass.ds(t, 1), :].rearrange("p a c -> p (a c)"), X[:, bass.ds(t, 1), :].rearrange("p a c -> p (a c)")))
            c.done(NT)
            c.straight()
            c.link(dve.tensor_tensor(mean, stats[:, :, 1], stats[:, :, 4], ALU.add))
            c.link(dve.tensor_tensor(var, stats[:, :, 1], stats[:, :, 4], ALU.subtract))
            c.link(dve.tensor_tensor(rms, stats[:, :, 2], stats[:, :, 5], ALU.add))
            c.link(dve.tensor_scalar(mean, mean, 0.5, None, ALU.mult))
            c.link(dve.scalar_tensor_tensor(var, var, 0.25, var, ALU.mult, ALU.mult))
            c.link(dve.scalar_tensor_tensor(var, rms, 1.0 / D, var, ALU.mult, ALU.add))
            c.publish(dve.tensor_scalar(rstd, var, LN_EPS, None, ALU.add), S["moments_done"], 1)
            dve.wait_ge(S["sigma_ready"], 2)
            c.link(dve.reciprocal(rstd, sig))
            c.done(1)
            c.straight()
            c.link(dve.tensor_tensor(rms, rms, rstd, ALU.mult))
            c.link(dve.tensor_scalar(rms, rms, float(D) ** 0.5, 1e-12, ALU.mult, ALU.max))
            c.link(dve.reciprocal(rms, rms))
            c.link(dve.tensor_scalar(rms, rms, float(D) ** 0.5, None, ALU.mult))
            dve.wait_ge(S["weights_loaded"], 160)
            for k in range(KC):
                c.link(dve.tensor_scalar(w_all[:, k, GW:GW + QW], w_all[:, k, GW:GW + QW], gpre[:, k:k + 1], None, ALU.mult))
            c.link(dve.tensor_scalar(gout, gout, float(D) ** 0.5, None, ALU.mult))
            c.link(dve.tensor_single_scalar(p5i, iota_i[:], MD.bit_length() - 1, ALU.logical_shift_right))
            c.link(dve.tensor_copy(p5, p5i))
            for h in range(MH):
                ins = dve.tensor_scalar(blockm[:, h * MD:(h + 1) * MD], p5.to_broadcast([P, MD]), float(h), MD ** -0.5, ALU.is_equal, ALU.mult)
            c.link(ins)
            c.link(dve.tensor_scalar(padneg, iota_p[:], float(LAST), -BIG, ALU.is_ge, ALU.mult))
            c.done(1)

            def tile(i, u):
                t = i * 2 + u
                later = not isinstance(i, int) or i > 0
                tt = bass.ds(t, 1)
                c.turn(t, 6)
                if later:
                    dve.wait_ge(S["transposed"], t - 1)
                c.publish(dve.tensor_scalar(xn[:, u, :], X[:, tt, :].rearrange("p a c -> p (a c)"), mean[:, tt], rstd[:, tt], ALU.subtract, ALU.mult), S["normed"], t + 1)
                c.link(dve.tensor_tensor(X[:, tt, :].rearrange("p a c -> p (a c)"), X[:, tt, :].rearrange("p a c -> p (a c)"), xn[:, u, :], ALU.add))
                if later:
                    dve.wait_ge(S[f"rows_stored{u}"], 16 * i)
                c.link(dve.memset(row_tile[:, u, :, 0:HD], 0.0))
                dve.wait_ge(S["h_copied"], t + 1)
                c.link(dve.tensor_tensor(nanmask, h_raw[:, u, :], ps_g[u][:, 0:GW], ALU.is_equal))
                dve.sem_inc(S["mask_made"], 1)
                c.publish(dve.copy_predicated(row_tile[:, u, :, 0:HD], nanmask.bitcast(I32).rearrange("p (h c) -> p h c", h=HEADS),
                                           ps_g[u][:, 0:GW].rearrange("p (h c) -> p h c", h=HEADS)), S["heads_kept"], t + 1)
                for n in range(2):
                    ins = dve.tensor_tensor(prod[:, n * GW:(n + 1) * GW].rearrange("p (h c) -> p h c", h=HEADS), row_tile[:, u, :, 0:HD],
                                            a_both[:, n * GW:(n + 1) * GW].rearrange("p (h c) -> p h c", h=HEADS), ALU.mult)
                    c.link(ins)
                dve.tensor_reduce(hl[:, tt, :].rearrange("p a h -> p (a h)"), prod[:, GW:2 * GW].rearrange("p (h c) -> p h c", h=HEADS), AX, ALU.add)
                c.link(dve.tensor_reduce(hr[:, bass.ds(t * HEADS, HEADS)], prod[:, 0:GW].rearrange("p (h c) -> p h c", h=HEADS), AX, ALU.add))
                c.publish(dve.tensor_scalar(row_tile[:, u, :, HD], hr[:, bass.ds(t * HEADS, HEADS)], 1.0, None, ALU.mult), S[f"row_ready{u}"], i + 1)

            def pair(i):
                tile(i, 0)
                tile(i, 1)

            first_then_rest(dve, NT // 2, pair)
            tile(NT // 2, 0)
            c.done(NT)
            dve.wait_ge(S["qkv_kept"], NT)
            c.straight()
            q = qkv[:, :, 0:HID].rearrange("p t (h d) -> p t h d", h=MH)

            def per_head(a):
                return a.rearrange("p (t h) -> p t h", h=MH).unsqueeze(3).broadcast_to([P, NT, MH, MD])

            c.link(dve.tensor_reduce(qstat.rearrange("p (t h) -> p t h", h=MH), q, AX, ALU.max))
            c.publish(dve.tensor_tensor(q, q, per_head(qstat), ALU.subtract), S["q_shifted"], 1)
            k_all = qkv[:, :, HID:2 * HID]
            c.link(dve.tensor_scalar(k_all[:, NT - 1, :], k_all[:, NT - 1, :], padneg, None, ALU.add))
            c.publish(dve.tensor_reduce(kcol, k_all.rearrange("p t c -> p c t"), AX, ALU.max), S["k_column"], 1)
            dve.wait_ge(S["k_column_t"], 1)
            c.link(dve.tensor_reduce(kmax[:, 0:1], ps_m[:, 0:P], AX, ALU.max))
            c.link(dve.tensor_reduce(kmax[:, 1:2], mem_k, AX, ALU.max))
            c.link(dve.tensor_tensor(kmax[:, 0:1], kmax[:, 0:1], kmax[:, 1:2], ALU.max))
            c.link(dve.tensor_scalar(kmax[:, 1:2], kmax[:, 0:1], -1.0, None, ALU.mult))
            c.publish(dve.tensor_scalar(kdiag, ident[:], kmax[:, 0:1], None, ALU.mult), S["k_diag"], 1)
            dve.wait_ge(S["k_row"], 1)
            c.link(dve.tensor_copy(krow, ps_m[:, P:2 * P]))
            c.publish(dve.tensor_tensor(k_all, k_all, krow.unsqueeze(1).broadcast_to([P, NT, HID]), ALU.subtract), S["k_shifted"], 1)
            dve.wait_ge(S["q_exp"], 1)
            c.link(dve.tensor_reduce(qsum.rearrange("p (t h) -> p t h", h=MH), q, AX, ALU.add))
            c.link(dve.reciprocal(qsum, qsum))
            dve.wait_ge(S["mem_t"], 1)
            dve.memset(memvt[:, HID:HID + 1], 1.0)
            dve.tensor_copy(memkt[0:MM, :], ps_m[0:MM, 256:256 + HID])
            c.publish(dve.tensor_copy(memvt[0:MM, 0:HID], ps_m[0:MM, 384:384 + HID]), S["mem_t_kept"], 1)
            parts = split.rearrange("p (t c) -> p t c", t=NT).bitcast(BF16)
            hr3 = hr.rearrange("p (t h) -> p t h", h=HEADS)
            res3 = res.rearrange("p (t h) -> p t h", h=HEADS)
            c.link(dve.tensor_copy(parts[:, :, 0:4], hr3))
            c.link(dve.tensor_tensor(res3, hr3, parts[:, :, 0:4], ALU.subtract))
            c.link(dve.tensor_copy(parts[:, :, 4:8], res3))
            c.link(dve.tensor_tensor(res3, res3, parts[:, :, 4:8], ALU.subtract))
            c.publish(dve.tensor_copy(parts[:, :, 8:12], res3), S["split_ready"], 1)
            dve.wait_ge(S["context"], 1)
            c.link(dve.reciprocal(ctx_r, ps_c[:, HID:HID + 1]))
            c.publish(dve.scalar_tensor_tensor(ctx_n, ps_c[:, 0:HID], ctx_r, blockm, ALU.mult, ALU.mult), S["context_n"], 1)
            c.done(1)
            c.straight()
            dve.wait_ge(S["context_t"], 1)
            c.publish(dve.tensor_copy(ctx_t, ps_m[:, 0:P]), S["context_t_kept"], 1)
            dve.wait_ge(S["wc_done"], 1)
            c.publish(dve.tensor_copy(wc, ps_m[:, 0:D]), S["wc_kept"], 1)

            def q_tile(i, u):
                t = i * 2 + u
                if not isinstance(i, int) or i > 0:
                    dve.wait_ge(S["q_t"], t - 1)
                sums = qsum[:, bass.ds(t * MH, MH)].unsqueeze(2).broadcast_to([P, MH, MD])
                dve.tensor_tensor(qs[:, u, :].rearrange("p (h d) -> p h d", h=MH),
                                  qkv[:, bass.ds(t, 1), 0:HID].rearrange("p a (h d) -> p (a h) d", h=MH), sums, ALU.mult).then_inc(S["q_scaled"], 1)

            def q_pair(i):
                q_tile(i, 0)
                q_tile(i, 1)

            first_then_rest(dve, NT // 2, q_pair)
            q_tile(NT // 2, 0)
            dve.wait_ge(S["mix_sigma"], 1)
            c.link(dve.tensor_scalar(n2, n2, 1e-12, None, ALU.max))
            c.link(dve.reciprocal(n2, n2))
            c.done(1)
            with dve.Fori(0, NT) as t:
                c.turn(t, 2)
                y = qkv[:, bass.ds(t, 1), HID:HID + D].rearrange("p a c -> p (a c)")
                xt = X[:, bass.ds(t, 1), :].rearrange("p a c -> p (a c)")
                c.link(dve.scalar_tensor_tensor(y, y, n2[:, bass.ds(t, 1)], gout, ALU.mult, ALU.mult))
                c.link(dve.tensor_tensor(xt, xt, y, ALU.add))
            c.done(NT)

        @block.tensor
        def _(pe):
            def transposes(t, u):
                pe.wait_ge(S["normed"], t + 1)
                for k in range(KC):
                    ins = pe.transpose(ps_t[u][:, k, :], xn[:, u, k * P:(k + 1) * P], ident[:])
                ins.then_inc(S["transposed"], 1)

            def products(t, u):
                pe.wait_ge(S["xnt_ready"], t + 1)
                for k in range(KC):
                    pe.matmul(ps_g[u][:, 0:GW], xnt[:, u, k, :], w_all[:, k, 0:GW], start=(k == 0), stop=(k == KC - 1))
                for k in range(KC):
                    ins = pe.matmul(ps_q[u][:, 0:QW], xnt[:, u, k, :], w_all[:, k, GW:GW + QW], start=(k == 0), stop=(k == KC - 1))
                ins.then_inc(S["projected"], 1)

            def tile(i, u):
                t = i * 2 + u
                if not isinstance(i, int) or i > 0:
                    pe.wait_ge(S["heads_kept"], t - 1)
                    pe.wait_ge(S["qkv_kept"], t - 1)
                transposes(t, u)
                products(t, u)

            def pair(i):
                tile(i, 0)
                tile(i, 1)

            first_then_rest(pe, NT // 2, pair)
            tile(NT // 2, 0)
            pe.wait_ge(S["k_column"], 1)
            pe.transpose(ps_m[:, 0:P], kcol, ident[:]).then_inc(S["k_column_t"], 1)
            pe.wait_ge(S["k_diag"], 1)
            pe.matmul(ps_m[:, P:2 * P], ones[:], kdiag, start=True, stop=True).then_inc(S["k_row"], 1)
            pe.wait_ge(S["mem_ready"], 1)
            pe.transpose(ps_m[0:MM, 256:256 + P], mem_e, ident[:])
            pe.transpose(ps_m[0:MM, 384:384 + P], mem_v, ident[:]).then_inc(S["mem_t"], 1)
            pe.wait_ge(S["mem_t_kept"], 1)
            pe.matmul(ps_c[:, 0:HID + 1], memkt[0:MM, :], memvt[0:MM, :], start=True, stop=False)

            def context(i, u):
                t = i * 2 + u
                pe.wait_ge(S["k_exp"], t + 1)
                pe.matmul(ps_c[:, 0:HID + 1], ktile[:, u, :], qkv[:, bass.ds(t, 1), 2 * HID:3 * HID + 1].rearrange("p a c -> p (a c)"),
                          start=False, stop=isinstance(i, int) and t == NT - 1).then_inc(S["k_used"], 1)

            with pe.Fori(0, NT // 2) as i:
                context(i, 0)
                context(i, 1)
            context(NT // 2, 0)
            pe.wait_ge(S["k_used"], NT)
            pe.nop().then_inc(S["context"], 1)
            pe.wait_ge(S["context_n"], 1)
            pe.transpose(ps_m[:, 0:P], ctx_n, ident[:]).then_inc(S["context_t"], 1)
            pe.wait_ge(S["context_t_kept"], 1)
            pe.matmul(ps_m[:, 0:D], ctx_t, wout, start=True, stop=True).then_inc(S["wc_done"], 1)
            pe.wait_ge(S["wc_kept"], 1)

            def mix_tile(i, u):
                t = i * 2 + u
                if not isinstance(i, int) or i > 0:
                    pe.wait_ge(S["q_t_kept"], t - 1)
                    pe.wait_ge(S["mix_kept"], t - 1)
                pe.wait_ge(S["q_scaled"], t + 1)
                pe.transpose(ps_t[u][:, 0, :], qs[:, u, :], ident[:]).then_inc(S["q_t"], 1)
                pe.wait_ge(S["q_t_kept"], t + 1)
                pe.matmul(ps_g[u][:, 0:D], qt[:, u, :], wc, start=True, stop=False)
                pe.matmul(ps_g[u][:, 0:D], ones[0:1, :], bout[0:1, :], start=False, stop=True).then_inc(S["mixed"], 1)

            def mix_pair(i):
                mix_tile(i, 0)
                mix_tile(i, 1)

            first_then_rest(pe, NT // 2, mix_pair)
            mix_tile(NT // 2, 0)


def attention(nc, v):
    P, N, D, NT, HEADS, HD, HP, G, GT, NG, UN, TURNS, COLBITS, TW, BIG, FAR = (v[k] for k in (
        "P", "N", "D", "NT", "HEADS", "HD", "HP", "G", "GT", "NG", "UN", "TURNS", "COLBITS", "TW", "BIG", "FAR"))
    X, ident, identb, iota_row, iota_i, iota_p, ones, hl, block_of, acc = (v[k] for k in (
        "X", "ident", "identb", "iota_row", "iota_i", "iota_p", "ones", "hl", "block_of", "acc"))
    sem, sb, pb, slots, table = v["sem"], v["sb"], v["pb"], v["slots"], v["table"]
    TILES = UN * GT
    MAIN = TURNS // 16 * 16

    with ExitStack() as s:
        rank_t = sb(s, "rank_t", [TURNS, UN * G], BF16)
        columns = sb(s, "columns", [P, TURNS, TILES], I32)
        rank_e = sb(s, "rank_e", [P, TURNS, TILES])
        maxima = sb(s, "maxima", [P, NT, HEADS])
        left_parts = sb(s, "left_parts", [P, NT, 3, HEADS], BF16)
        pick = sb(s, "pick", [3 * HEADS, HEADS, P], BF16)

        with ExitStack() as s2:
            packed = sb(s2, "packed", [TURNS, UN * G], I32)
            packed_f = sb(s2, "packed_f", [TURNS, UN * G])
            shifted = sb(s2, "shifted", [TURNS, UN * G], I32)
            flat = sb(s2, "flat", [P, TURNS, TILES], I32)
            head_no = sb(s2, "head_no", [3 * HEADS, HEADS, P])
            part_i = sb(s2, "part_i", [P, 1], I32)
            part_f = sb(s2, "part_f", [P, 1])
            left_rest = sb(s2, "left_rest", [P, NT, HEADS])
            ps = [pb(s2, f"ps_slots{i}", [P, 512]) for i in range(UN)]
            loaded, ready, turned, chain, made = (sem(n) for n in ("slots_loaded", "packed_ready", "slots_turned", "slot_chain", "head_numbers"))
            block = s2.enter_context(nc.Block())

            @block.sync
            def _(sp):
                view = slots.rearrange("(i c) o -> i (c o)", i=TURNS)
                sp.dma_start(packed[0:MAIN, :], view[0:MAIN, :]).then_inc(loaded, 16)
                sp.dma_start(packed[MAIN:TURNS, :], view[MAIN:TURNS, :]).then_inc(loaded, 16)

            @block.gpsimd
            def _(pool):
                pool.iota(head_no[:], pattern=[[1, HEADS], [0, P]], base=0, channel_multiplier=0, allow_small_or_imprecise_dtypes=True).then_inc(made, 1)
                pool.memset(maxima[:], -BIG)
                pool.memset(acc[:], 0.0).then_inc(made, 1)

            @block.vector
            def _(dve):
                c = Chain(dve, chain)
                c.straight()
                c.link(dve.tensor_single_scalar(part_i[:], iota_i[:], HEADS - 1, ALU.bitwise_and))
                c.link(dve.tensor_copy(part_f[:], part_i[:]))
                dve.wait_ge(made, 1)
                c.link(dve.tensor_scalar(pick[:], head_no[:], part_f[0:3 * HEADS, :], None, ALU.is_equal))
                c.link(dve.tensor_copy(left_parts[:, :, 0, :], hl[:]))
                c.link(dve.tensor_tensor(left_rest[:], hl[:], left_parts[:, :, 0, :], ALU.subtract))
                c.link(dve.tensor_copy(left_parts[:, :, 1, :], left_rest[:]))
                c.link(dve.tensor_tensor(left_parts[:, :, 2, :], left_rest[:], left_parts[:, :, 1, :], ALU.subtract))
                dve.wait_ge(loaded, 32)
                dve.tensor_copy(packed_f[:], packed[:]).then_inc(ready, 1)
                c.link(dve.tensor_single_scalar(shifted[:], packed[:], COLBITS, ALU.logical_shift_right))
                c.link(dve.tensor_copy(rank_t[:], shifted[:]))
                for u in range(UN):
                    dve.wait_ge(turned, u + 1)
                    c.link(dve.tensor_copy(flat[:, :, u * GT:(u + 1) * GT].rearrange("p i k -> p k i"),
                                           ps[u][:, 0:GT * TURNS].rearrange("p (k i) -> p k i", k=GT)))
                c.link(dve.tensor_single_scalar(columns[:], flat[:], (1 << COLBITS) - 1, ALU.bitwise_and))
                c.link(dve.tensor_single_scalar(flat[:], flat[:], COLBITS, ALU.logical_shift_right))
                c.link(dve.tensor_copy(rank_e[:], flat[:]))
                c.done(1)

            @block.tensor
            def _(pe):
                pe.wait_ge(ready, 1)
                for u in range(UN):
                    for k in range(GT):
                        ins = pe.transpose(ps[u][:, k * TURNS:(k + 1) * TURNS], packed_f[:, (u * GT + k) * P:(u * GT + k + 1) * P],
                                           ident[0:TURNS, 0:TURNS])
                    ins.then_inc(turned, 1)

        with ExitStack() as s2:
            indices = sb(s2, "indices", [P, UN, GT], I32)
            rows = sb(s2, "rows", [P, UN, GT, TW])
            far = sb(s2, "far", [P, 2, G], BF16)
            in_row_t = sb(s2, "in_row_t", [P, 2, G], BF16)
            in_row = sb(s2, "in_row", [P, 2, GT, P])
            logits_t = sb(s2, "logits_t", [3 * HEADS, 2, G], BF16)
            masked = sb(s2, "masked", [P, HEADS, G], BF16)
            largest = sb(s2, "largest", [P, HEADS])
            bound = sb(s2, "bound", [P, HEADS])
            new_max = sb(s2, "new_max", [P, 2, HEADS])
            row_side = sb(s2, "row_side", [P, 2, 3, 2, HEADS], BF16)
            edge_side = sb(s2, "edge_side", [P, GT, 2, HEADS])
            delta = sb(s2, "delta", [P, 3, HEADS])
            scale = sb(s2, "scale", [P, 3, HEADS])
            logit = sb(s2, "logit", [P, GT, HEADS])
            far_off = sb(s2, "far_off", [P, 1])
            ps_pick = pb(s2, "ps_pick", [P, HEADS, G])
            ps_rank = pb(s2, "ps_rank", [P, G])
            ps_sum = pb(s2, "ps_sum", [P, 512])
            ps_turned = pb(s2, "ps_turned", [3 * HEADS, 2 * G], BF16)
            ps_row_side = pb(s2, "ps_row_side", [P, 512])
            ps_lt, ps_edge = ps_turned[:, 0:G], ps_row_side[:, 0:GT * 6 * HEADS]
            names = ([f"indices_staged{u}" for u in range(UN)] + [f"gathered{u}" for u in range(UN)] +
                     ["indices_taken", "staging_passed", "far_off_made", "maximum_passed", "rank_broadcast", "far_made", "in_row_t_made", "in_row_made",
                      "logits_turned", "logits_t_kept", "picked", "largest_found", "edge_chain", "row_chain", "finish_chain", "row_side_made", "delta_made",
                      "scale_made", "edge_side_done", "logit_made", "exp_made", "messages_made", "last_messages_made", "parts_cleared", "summed", "acc_scaled", "acc_added"])
            S = {n: sem(n) for n in names}
            block = s2.enter_context(nc.Block())

            def wait(engine, name, value):
                if not isinstance(value, int) or value > 0:
                    engine.wait_ge(S[name], value)

            def turns(engine, step, ahead):
                def turn(i):
                    for u in range(UN):
                        step(i, u)
                for u in range(-ahead, 0):
                    step(0, u)
                turn(0)
                with engine.Fori(1, TURNS - 1) as i:
                    turn(i)
                turn(TURNS - 1)

            def exists(g):
                return not isinstance(g, int) or 0 <= g < NG

            def later(i, u, n):
                return i + (u + n) // UN, (u + n) % UN

            @block.sync
            def _(sp):
                def step(i, u):
                    wait(sp, f"gathered{u}", i * 16 * GT)
                    sp.sem_inc(S["staging_passed"], 1)
                    sp.dma_start(indices[:, u, :], columns[:, bass.ds(i, 1), u * GT:(u + 1) * GT].rearrange("p a k -> p (a k)")).then_inc(S[f"indices_staged{u}"], 16)
                turns(sp, step, 0)

            @block.gpsimd
            def _(pool):
                def step(i, u):
                    wait(pool, f"indices_staged{u}", i * 16 + 16)
                    wait(pool, "summed", (i - 1) * UN + u + 1)
                    pool.sem_inc(S["indices_taken"], 1)
                    for k in range(GT):
                        pool.indirect_dma_start(rows[:, u, k, :], None, table, bass.IndirectOffsetOnAxis(indices[:, u, k:k + 1], 0)).then_inc(S[f"gathered{u}"], 16)
                turns(pool, step, 0)

            @block.scalar
            def _(act):
                def keep_logits(g, u):
                    wait(act, "logits_turned", g + 1)
                    wait(act, "picked", (g - 1) * HEADS)
                    act.activation(logits_t[:, u % 2, :], ps_lt, ACT.Copy).then_inc(S["logits_t_kept"], 1)

                def row_masks(g, u):
                    wait(act, "rank_broadcast", g + 1)
                    wait(act, "largest_found", (g - 1) * HEADS)
                    act.activation(far[:, u % 2, :], ps_rank[:], ACT.Abs, bias=far_off[:], scale=FAR).then_inc(S["far_made"], 1)
                    wait(act, "far_made", g + 1)
                    wait(act, "edge_side_done", g - 1)
                    act.activation(in_row_t[:, u % 2, :], far[:, u % 2, :], ACT.Relu, bias=1.0, scale=-1.0).then_inc(S["in_row_t_made"], 1)

                act.wait_ge(S["far_off_made"], 1)

                def step(i, u):
                    g = i * UN + u
                    if exists(g):
                        wait(act, "logit_made", g + 1)
                        heads = rows[:, u, :, 0:HEADS * HP].rearrange("p k (h c) -> p k h c", h=HEADS)
                        act.activation(heads[:, :, :, HD], logit[:], ACT.Exp).then_inc(S["exp_made"], 1)
                        wait(act, "exp_made", g + 1)
                        for h in range(HEADS):
                            act.activation(heads[:, GT - 1, h, 0:HD], heads[:, GT - 1, h, 0:HD], ACT.Copy,
                                           scale=heads[:, GT - 1, h, HD:HP]).then_inc(S["last_messages_made"], 1)
                    if exists(g + 1):
                        wait(act, "delta_made", g + 2)
                        wait(act, "acc_scaled", g - 1)
                        act.activation(scale[:, (u + 1) % 3, :], delta[:, (u + 1) % 3, :], ACT.Exp).then_inc(S["scale_made"], 1)
                    if exists(g + 3):
                        keep_logits(g + 3, u + 3)
                        row_masks(g + 3, u + 3)
                turns(act, step, 3)

            @block.vector
            def _(dve):
                e = Chain(dve, S["edge_chain"])
                r = Chain(dve, S["row_chain"])
                dve.memset(row_side[:], 0.0).then_inc(S["parts_cleared"], 1)
                dve.wait_ge(S["parts_cleared"], 1)
                dve.tensor_scalar(far_off[:], iota_p[:], -FAR, None, ALU.mult).then_inc(S["far_off_made"], 1)

                def maximum(g, u, b):
                    for h in range(HEADS):
                        wait(dve, "picked", g * HEADS + h + 1)
                        if h == 0:
                            wait(dve, "far_made", g + 1)
                        dve.sem_inc(S["maximum_passed"], 1)
                        dve.tensor_tensor_reduce(masked[:, h, :], ps_pick[:, h, :], far[:, u % 2, :], 1.0, -BIG, ALU.subtract, ALU.max,
                                                 largest[:, h:h + 1]).then_inc(S["largest_found"], 1)

                def row_steps(g, u, b):
                    left = hl[:, bass.ds(b, 1), :].rearrange("p a h -> p (a h)")
                    parts = left_parts[:, bass.ds(b, 1), :, :].rearrange("p a t h -> p (a t) h")
                    so_far = maxima[:, bass.ds(b, 1), :].rearrange("p a h -> p (a h)")
                    new, side = new_max[:, u % 2, :], row_side[:, u % 2]
                    r.turn(g, 6)
                    wait(dve, "edge_side_done", g - 1)
                    dve.tensor_scalar(side[:, :, 0, :], parts, 1.0, None, ALU.mult)
                    wait(dve, "largest_found", (g + 1) * HEADS)
                    n = r.tick(dve.tensor_tensor(bound[:], largest[:], left, ALU.add))
                    yield
                    r.need(n)
                    n = r.tick(dve.scalar_tensor_tensor(bound[:], bound[:], 0.2, bound[:], ALU.mult, ALU.max))
                    yield
                    r.need(n)
                    n = r.tick(dve.tensor_tensor(new, bound[:], so_far, ALU.max))
                    yield
                    r.need(n)
                    n = r.tick(dve.tensor_copy(side[:, 0, 1, :], new))
                    yield
                    r.need(n)
                    dve.tensor_tensor(side[:, 1, 1, :], new, side[:, 0, 1, :], ALU.subtract).then_inc(S["row_side_made"], 1)
                    yield
                    wait(dve, "row_side_made", g + 1)
                    n = r.tick(dve.tensor_tensor(new, side[:, 0, 1, :], side[:, 1, 1, :], ALU.add))
                    yield
                    r.need(n)
                    wait(dve, "scale_made", g - 2)
                    dve.tensor_tensor(delta[:, u % 3, :], so_far, new, ALU.subtract).then_inc(S["delta_made"], 1)
                    yield
                    wait(dve, "delta_made", g + 1)
                    r.tick(dve.tensor_scalar(so_far, new, 1.0, None, ALU.mult))
                    yield

                def edge_steps(g, u):
                    heads = rows[:, u, :, 0:HEADS * HP].rearrange("p k (h c) -> p k h c", h=HEADS)
                    e.turn(g, 3)
                    wait(dve, "edge_side_done", g + 1)
                    n = e.tick(dve.tensor_reduce(edge_side[:].rearrange("p k v h -> p k (v h)"),
                                                 ps_edge.rearrange("p (k t c) -> p k c t", k=GT, t=3), AX, ALU.add))
                    yield
                    e.need(n)
                    wait(dve, "exp_made", g)
                    n = e.tick(dve.tensor_tensor(logit[:], heads[:, :, :, HD], edge_side[:, :, 0, :], ALU.add))
                    yield
                    e.need(n)
                    n = e.tick(dve.scalar_tensor_tensor(logit[:], logit[:], 0.2, logit[:], ALU.mult, ALU.max))
                    yield
                    e.need(n)
                    dve.tensor_tensor(logit[:], logit[:], edge_side[:, :, 1, :], ALU.subtract).then_inc(S["logit_made"], 1)
                    yield

                def edge_mask(i, u):
                    wait(dve, "summed", i * UN + u - 1)
                    rank = rank_e[:, bass.ds(i, 1), u * GT:(u + 1) * GT].rearrange("p a k -> p (a k)").unsqueeze(2).broadcast_to([P, GT, P])
                    dve.tensor_tensor(in_row[:, u % 2, :, :], iota_row[:].unsqueeze(1).broadcast_to([P, GT, P]), rank, ALU.is_equal).then_inc(S["in_row_made"], 1)

                def messages(g, u):
                    heads = rows[:, u, :, 0:HEADS * HP].rearrange("p k (h c) -> p k h c", h=HEADS)
                    wait(dve, "exp_made", g + 1)
                    dve.tensor_tensor(heads[:, 0:GT - 1, :, 0:HD], heads[:, 0:GT - 1, :, 0:HD],
                                      heads[:, 0:GT - 1, :, HD:HP].broadcast_to([P, GT - 1, HEADS, HD]), ALU.mult).then_inc(S["messages_made"], 1)

                def scale_sums(g, u, b):
                    a4 = acc[:, bass.ds(b, 1), :].rearrange("p a (h c) -> p (a h) c", h=HEADS)
                    wait(dve, "scale_made", g + 1)
                    wait(dve, "acc_added", g)
                    dve.tensor_tensor(a4, a4, scale[:, u % 3, :].unsqueeze(2).broadcast_to([P, HEADS, HP]), ALU.mult).then_inc(S["acc_scaled"], 1)

                def add_sums(g, u, b):
                    a = acc[:, bass.ds(b, 1), :].rearrange("p a c -> p (a c)")
                    wait(dve, "acc_scaled", g + 1)
                    wait(dve, "summed", g + 1)
                    dve.tensor_tensor(a, a, ps_sum[:, 0:HEADS * HP], ALU.add).then_inc(S["acc_added"], 1)

                def block_number(g):
                    return dve.value_load(block_of[0:1, bass.ds(g, 1)], min_val=0, max_val=NT - 1)

                blocks = {n: block_number(n) for n in range(2)}
                passed = [dve.alloc_register(f"passed_block{n}") for n in (-1, 0, 1)]

                def step(i, u):
                    g = i * UN + u
                    if u == 0 and (not isinstance(g, int) or g > 0):
                        for n in (-1, 0, 1):
                            blocks[n] = dve.snap(passed[n + 1], min_val=0, max_val=NT - 1)
                    if exists(g + 1):
                        maximum(g + 1, u + 1, blocks[u + 1])
                    if exists(g):
                        rows_of, edges_of = (row_steps(g + 1, u + 1, blocks[u + 1]) if exists(g + 1) else iter(())), edge_steps(g, u)
                        for _ in range(4):
                            next(edges_of)
                            next(rows_of, None)
                        next(rows_of, None)
                        edge_mask(i, u)
                        next(rows_of, None)
                        if exists(g - 1):
                            scale_sums(g - 1, u - 1, blocks[u - 1])
                        next(rows_of, None)
                        if exists(g - 1):
                            add_sums(g - 1, u - 1, blocks[u - 1])
                        messages(g, u)
                        if exists(g + 2):
                            blocks[u + 2] = block_number(g + 2)
                        next(rows_of, None)
                        if u == UN - 1:
                            for n in (-1, 0, 1):
                                if exists(g + 1 + n):
                                    dve.reg_mov(passed[n + 1], blocks[UN + n])
                    else:
                        for _ in row_steps(g + 1, u + 1, blocks[u + 1]):
                            pass
                turns(dve, step, 1)
                scale_sums(NG - 1, UN - 1, blocks[UN - 1])
                add_sums(NG - 1, UN - 1, blocks[UN - 1])
                wait(dve, "acc_added", NG)
                c = Chain(dve, S["finish_chain"])
                c.straight()
                den = maxima[:]
                a4 = acc[:, :, :].rearrange("p t (h c) -> p t h c", h=HEADS)
                c.link(dve.tensor_scalar(den, a4[:, :, :, HD], 1e-16, None, ALU.add))
                c.link(dve.reciprocal(den, den))
                c.link(dve.tensor_tensor(a4[:, :, :, 0:HD], a4[:, :, :, 0:HD], den.unsqueeze(3).broadcast_to([P, NT, HEADS, HD]), ALU.mult))
                x4 = X[:, :, :].rearrange("p t (h c) -> p t h c", h=HEADS)
                c.link(dve.tensor_tensor(x4, x4, a4[:, :, :, 0:HD], ALU.add))

            @block.tensor
            def _(pe):
                def broadcast_rank(i, u):
                    wait(pe, "far_made", i * UN + u)
                    pe.matmul(ps_rank[:], identb[0:TURNS, bass.ds(i, 1)].broadcast_to([TURNS, P]), rank_t[:, u * G:(u + 1) * G],
                              start=True, stop=True).then_inc(S["rank_broadcast"], 1)

                def turn_logits(i, u):
                    g = i * UN + u
                    wait(pe, f"gathered{u}", i * 16 * GT + 16 * GT)
                    wait(pe, "logits_t_kept", g)
                    for k in range(GT):
                        ins = pe.transpose(ps_lt[:, k * P:(k + 1) * P], rows[:, u, k, HEADS * HP:TW].bitcast(BF16), identb[:])
                    ins.then_inc(S["logits_turned"], 1)

                def pick_logits(g, u):
                    wait(pe, "logits_t_kept", g + 1)
                    for h in range(HEADS):
                        wait(pe, "largest_found", (g - 1) * HEADS + h + 1)
                        pe.matmul(ps_pick[:, h, :], pick[:, h, :], logits_t[:, u % 2, :], start=True, stop=True).then_inc(S["picked"], 1)

                def row_to_edge(g, u):
                    wait(pe, "row_side_made", g + 1)
                    wait(pe, "in_row_t_made", g + 1)
                    wait(pe, "logit_made", g)
                    for k in range(GT):
                        ins = pe.matmul(ps_edge[:, k * 6 * HEADS:(k + 1) * 6 * HEADS], in_row_t[:, u % 2, k * P:(k + 1) * P],
                                        row_side[:, u % 2].rearrange("p t v h -> p (t v h)"),
                                        start=True, stop=True)
                    ins.then_inc(S["edge_side_done"], 1)

                def sum_rows(g, u):
                    wait(pe, "messages_made", g + 1)
                    wait(pe, "last_messages_made", (g + 1) * HEADS)
                    wait(pe, "acc_added", g)
                    for k in range(GT):
                        ins = pe.matmul(ps_sum[:, 0:HEADS * HP], in_row[:, u % 2, k, :], rows[:, u, k, 0:HEADS * HP],
                                        start=(k == 0), stop=(k == GT - 1))
                    ins.then_inc(S["summed"], 1)

                def step(i, u):
                    g = i * UN + u
                    if exists(g + 2):
                        pick_logits(g + 2, u + 2)
                    if exists(g + 3):
                        turn_logits(*later(i, u, 3))
                        broadcast_rank(*later(i, u, 3))
                    if exists(g + 1):
                        row_to_edge(g + 1, u + 1)
                    if exists(g):
                        sum_rows(g, u)
                turns(pe, step, 3)


def experts(nc, v):
    P, N, D, NT, LAST, KC, NE, FH, FC, LN_EPS = (v[k] for k in ("P", "N", "D", "NT", "LAST", "KC", "NE", "FH", "FC", "LN_EPS"))
    X, ident, identb, iota_row, iota_i, iota_p, ones = (v[k] for k in ("X", "ident", "identb", "iota_row", "iota_i", "iota_p", "ones"))
    sem, sb, pb = v["sem"], v["sb"], v["pb"]
    w1, w2, wr, br, b1, b2, ln_g, ln_b, out = (v[k] for k in ("w1", "w2", "wr", "br", "b1", "b2", "ln_g", "ln_b", "out"))
    SG = 256
    ST = SG // P
    EG = (2 * NT * P + NE * (SG - 1)) // SG
    EG += EG % 2
    in_slots = nc.dram_tensor("in_slots", [EG * SG, D], FP32).ap()
    out_slots = nc.dram_tensor("out_slots", [EG * SG, D], FP32).ap()

    with ExitStack() as s:
        mean1, rstd1, mean2, rstd2 = (sb(s, n, [P, NT]) for n in ("mean1", "rstd1", "mean2", "rstd2"))
        slot_of = sb(s, "slot_of", [P, NT, 2])
        weight = sb(s, "weight", [P, NT, 2])
        expert_of = sb(s, "expert_of", [1, EG], I32)
        gains = sb(s, "gains", [P, 2, NE * KC])
        b1t = sb(s, "b1t", [P, NE * FC])
        b2row = sb(s, "b2row", [1, NE * D])

        with ExitStack() as s2:
            stats = sb(s2, "f_stats", [P, NT, 6])
            tmp, sig = (sb(s2, n, [P, NT]) for n in ("f_tmp", "f_sig"))
            u_tile = sb(s2, "u_tile", [P, 2, D])
            ut = sb(s2, "ut", [P, 2, KC, P])
            wr_sb = sb(s2, "wr_sb", [P, KC, NE])
            br_sb = sb(s2, "br_sb", [1, NE])
            prob, sel, sel2, rest, pos = (sb(s2, n, [P, NT, NE]) for n in ("prob", "sel", "sel2", "rest", "pos"))
            red = sb(s2, "red", [P, NT])
            order = sb(s2, "order", [P, NE])
            tri = sb(s2, "f_tri", [P, P])
            count, before, start, groups_f = (sb(s2, n, [P, NE]) for n in ("f_count", "f_before", "f_start", "f_groups"))
            zero8 = sb(s2, "zero8", [P, NE])
            groups_i = sb(s2, "f_groups_i", [P, NE], I32)
            reached = sb(s2, "f_reached", [1, EG, NE])
            gno = sb(s2, "gno", [1, EG, NE])
            expert_f = sb(s2, "expert_f", [1, EG])
            zero = sb(s2, "zero", [P, 14, D])
            gb_rows = sb(s2, "gb_rows", [NE * KC, 2, P])
            b1_rows = sb(s2, "b1_rows", [NE * FC, P])
            ps_u = [pb(s2, f"ps_u{i}", [P, 512]) for i in range(2)]
            ps_l = [pb(s2, f"ps_l{i}", [P, 512]) for i in range(2)]
            ps_w = pb(s2, "ps_w", [P, 512])
            ps_s = pb(s2, "ps_s", [P, 512])
            names = ("f_loaded", "zeroed", "slots_cleared", "f_chain", "f_moments", "f_sigma", "u_made", "u_turned", "ut_kept", "logits_done",
                     "logits_kept", "logits_shifted", "prob_made", "counted", "count_summed", "weights_turned", "r_made", "router_misc")
            S = {n: sem(n) for n in names}
            block = s2.enter_context(nc.Block())
            FILL = 14 * P

            @block.sync
            def _(sp):
                ld = S["f_loaded"]
                sp.dma_start(wr_sb[:], wr.rearrange("(k p) e -> p k e", p=P)).then_inc(ld, 16)
                sp.dma_start(br_sb[:], br.rearrange("(a e) -> a e", a=1)).then_inc(ld, 16)
                sp.dma_start(b2row[:], b2.rearrange("e c -> (e c)").rearrange("(a c) -> a c", a=1)).then_inc(ld, 16)
                sp.dma_start(gb_rows[:, 0, :], ln_g.rearrange("e (k p) -> (e k) p", p=P)).then_inc(ld, 16)
                sp.dma_start(gb_rows[:, 1, :], ln_b.rearrange("e (k p) -> (e k) p", p=P)).then_inc(ld, 16)
                sp.dma_start(b1_rows[:], b1.rearrange("e (k p) -> (e k) p", p=P)).then_inc(ld, 16)
                sp.wait_ge(S["zeroed"], 1)
                rows = in_slots.shape[0]
                assert rows % P == 0
                n = 0
                for r in range(0, rows, FILL):
                    m = min(FILL, rows - r)
                    sp.dma_start(in_slots[r:r + m, :].rearrange("(p t) c -> p t c", p=P), zero[:, 0:m // P, :]).then_inc(S["slots_cleared"], 16)
                    n += 16
                sp.wait_ge(S["slots_cleared"], n)

            @block.gpsimd
            def _(pool):
                pool.memset(zero[:], 0.0).then_inc(S["zeroed"], 1)
                pool.iota(order[:], pattern=[[-1, NE]], base=NE, channel_multiplier=0, allow_small_or_imprecise_dtypes=True).then_inc(S["zeroed"], 1)
                pool.iota(gno[:], pattern=[[1, EG], [0, NE]], base=0, channel_multiplier=0, allow_small_or_imprecise_dtypes=True).then_inc(S["zeroed"], 1)
                pool.memset(zero8[:], 0.0).then_inc(S["zeroed"], 1)

            @block.scalar
            def _(act):
                def sigma(n):
                    act.wait_ge(S["f_moments"], n)
                    act.activation(sig[:], tmp[:], ACT.Sqrt).then_inc(S["f_sigma"], 1)

                sigma(1)

                def tile(i, u):
                    t = i * 2 + u
                    act.wait_ge(S["u_turned"], t + 1)
                    if not isinstance(i, int) or i > 0:
                        act.wait_ge(S["logits_done"], t - 1)
                    act.activation(ut[:, u, :, :], ps_u[u][:, 0:D].rearrange("p (k c) -> p k c", k=KC), ACT.Copy).then_inc(S["ut_kept"], 1)

                def pair(i):
                    tile(i, 0)
                    tile(i, 1)

                first_then_rest(act, NT // 2, pair)
                tile(NT // 2, 0)
                sigma(2)
                act.wait_ge(S["logits_shifted"], 1)
                act.activation(prob[:], prob[:], ACT.Exp).then_inc(S["prob_made"], 1)

            @block.vector
            def _(dve):
                c = Chain(dve, S["f_chain"])

                def moments(mean, rstd, n):
                    c.link(dve.tensor_tensor(mean, stats[:, :, 1], stats[:, :, 4], ALU.add))
                    c.link(dve.tensor_tensor(rstd, stats[:, :, 1], stats[:, :, 4], ALU.subtract))
                    c.link(dve.tensor_tensor(tmp[:], stats[:, :, 2], stats[:, :, 5], ALU.add))
                    c.link(dve.tensor_scalar(mean, mean, 0.5, None, ALU.mult))
                    c.link(dve.scalar_tensor_tensor(rstd, rstd, 0.25, rstd, ALU.mult, ALU.mult))
                    c.link(dve.scalar_tensor_tensor(tmp[:], tmp[:], 1.0 / D, rstd, ALU.mult, ALU.add))
                    c.publish(dve.tensor_scalar(tmp[:], tmp[:], LN_EPS, None, ALU.add), S["f_moments"], n)
                    dve.wait_ge(S["f_sigma"], n)
                    c.link(dve.reciprocal(rstd, sig[:]))

                with dve.Fori(0, NT) as t:
                    c.turn(t, 1)
                    c.link(dve.bn_stats(stats[:, bass.ds(t, 1), :].rearrange("p a c -> p (a c)"), X[:, bass.ds(t, 1), :].rearrange("p a c -> p (a c)")))
                c.done(NT)
                c.straight()
                moments(mean1[:], rstd1[:], 1)
                c.link(dve.tensor_scalar(tri[:], iota_row[:], iota_p[:], None, ALU.is_gt))
                c.done(1)

                def tile(i, u):
                    t = i * 2 + u
                    later = not isinstance(i, int) or i > 0
                    tt = bass.ds(t, 1)
                    if later:
                        dve.wait_ge(S["u_turned"], t - 1)
                    c.turn(t, 1)
                    c.publish(dve.tensor_scalar(u_tile[:, u, :], X[:, tt, :].rearrange("p a c -> p (a c)"), mean1[:, tt], rstd1[:, tt],
                                               ALU.subtract, ALU.mult), S["u_made"], t + 1)
                    c.link(dve.bn_stats(stats[:, tt, :].rearrange("p a c -> p (a c)"), u_tile[:, u, :]))
                    dve.wait_ge(S["logits_done"], t + 1)
                    dve.tensor_scalar(prob[:, tt, :].rearrange("p a c -> p (a c)"), ps_l[u][:, 0:NE], 1.0, None, ALU.mult).then_inc(S["logits_kept"], 1)

                def pair(i):
                    tile(i, 0)
                    tile(i, 1)

                first_then_rest(dve, NT // 2, pair)
                tile(NT // 2, 0)
                c.done(NT)
                dve.wait_ge(S["logits_kept"], NT)
                c.straight()
                moments(mean2[:], rstd2[:], 2)

                def each(a):
                    return a.unsqueeze(2).broadcast_to([P, NT, NE])

                orders = order[:].unsqueeze(1).broadcast_to([P, NT, NE])
                c.link(dve.tensor_reduce(red[:], prob[:], AX, ALU.max))
                c.publish(dve.tensor_tensor(prob[:], prob[:], each(red[:]), ALU.subtract), S["logits_shifted"], 1)
                dve.wait_ge(S["prob_made"], 1)
                dve.wait_ge(S["zeroed"], 4)

                def choose(values, chosen, top):
                    c.link(dve.tensor_reduce(top, values, AX, ALU.max))
                    c.link(dve.tensor_tensor(chosen, values, each(top), ALU.is_equal))
                    c.link(dve.tensor_tensor(chosen, chosen, orders, ALU.mult))
                    c.link(dve.tensor_reduce(red[:], chosen, AX, ALU.max))
                    c.link(dve.tensor_tensor(chosen, each(red[:]), orders, ALU.is_equal))

                choose(prob[:], sel[:], weight[:, :, 0])
                c.link(dve.scalar_tensor_tensor(rest[:], sel[:], -2.0, prob[:], ALU.mult, ALU.add))
                choose(rest[:], sel2[:], weight[:, :, 1])
                c.link(dve.tensor_tensor(red[:], weight[:, :, 0], weight[:, :, 1], ALU.add))
                c.link(dve.reciprocal(red[:], red[:]))
                c.link(dve.tensor_tensor(weight[:], weight[:], red[:].unsqueeze(2).broadcast_to([P, NT, 2]), ALU.mult))
                c.link(dve.tensor_tensor(rest[:], sel[:], sel2[:], ALU.add))
                c.publish(dve.tensor_reduce(count[:], rest[:].rearrange("p t e -> p e t"), AX, ALU.add), S["counted"], 1)
                dve.wait_ge(S["count_summed"], 1)
                c.link(dve.tensor_scalar(groups_i[:], ps_s[:, 16:16 + NE], float(SG - 1), None, ALU.add))
                c.link(dve.tensor_single_scalar(groups_i[:], groups_i[:], SG.bit_length() - 1, ALU.logical_shift_right))
                c.link(dve.tensor_copy(groups_f[:], groups_i[:]))
                c.link(dve.tensor_tensor_scan(start[:], groups_f[:], zero8[:], 0.0, ALU.add, ALU.add))
                c.link(dve.tensor_tensor(start[:], start[:], groups_f[:], ALU.subtract))
                c.link(dve.scalar_tensor_tensor(before[:], start[:], float(SG), ps_s[:, 0:NE], ALU.mult, ALU.add))
                for e in range(NE):
                    ins = dve.tensor_tensor_scan(pos[:, :, e], rest[:, :, e], rest[:, :, e], before[:, e:e + 1], ALU.add, ALU.max)
                c.link(ins)
                for n, chosen in enumerate((sel, sel2)):
                    c.link(dve.tensor_tensor(chosen[:], chosen[:], pos[:], ALU.mult))
                    c.link(dve.tensor_reduce(slot_of[:, :, n], chosen[:], AX, ALU.add))
                c.link(dve.tensor_scalar(slot_of[:], slot_of[:], -1.0, None, ALU.add))
                c.link(dve.tensor_tensor(reached[:], gno[:], start[0:1, :].unsqueeze(1).broadcast_to([1, EG, NE]), ALU.is_ge))
                c.link(dve.tensor_reduce(expert_f[:], reached[:], AX, ALU.add))
                c.link(dve.tensor_scalar(expert_of[:], expert_f[:], -1.0, None, ALU.add))
                dve.wait_ge(S["weights_turned"], 1)
                dve.tensor_copy(gains[:].rearrange("p a c -> p (a c)"), ps_w[:, 0:2 * NE * KC])
                c.link(dve.tensor_copy(b1t[:], ps_w[:, 128:128 + NE * FC]))
                c.done(1)

            @block.tensor
            def _(pe):
                pe.wait_ge(S["f_loaded"], 96)
                for n in range(2):
                    pe.transpose(ps_w[:, n * NE * KC:(n + 1) * NE * KC], gb_rows[:, n, :], ident[0:NE * KC, 0:NE * KC])
                pe.transpose(ps_w[:, 128:128 + NE * FC], b1_rows[:], ident[0:NE * FC, 0:NE * FC]).then_inc(S["weights_turned"], 1)

                def tile(i, u):
                    t = i * 2 + u
                    pe.wait_ge(S["u_made"], t + 1)
                    if not isinstance(i, int) or i > 0:
                        pe.wait_ge(S["logits_kept"], t - 1)
                    for k in range(KC):
                        ins = pe.transpose(ps_u[u][:, k * P:(k + 1) * P], u_tile[:, u, k * P:(k + 1) * P], ident[:])
                    ins.then_inc(S["u_turned"], 1)
                    pe.wait_ge(S["ut_kept"], t + 1)
                    for k in range(KC):
                        pe.matmul(ps_l[u][:, 0:NE], ut[:, u, k, :], wr_sb[:, k, :], start=(k == 0), stop=False)
                    pe.matmul(ps_l[u][:, 0:NE], ones[0:1, :], br_sb[:], start=False, stop=True).then_inc(S["logits_done"], 1)

                def pair(i):
                    tile(i, 0)
                    tile(i, 1)

                first_then_rest(pe, NT // 2, pair)
                tile(NT // 2, 0)
                pe.wait_ge(S["counted"], 1)
                pe.matmul(ps_s[:, 0:NE], tri[:], count[:], start=True, stop=True)
                pe.matmul(ps_s[:, 16:16 + NE], ones[:], count[:], start=True, stop=True).then_inc(S["count_summed"], 1)

        with ExitStack() as s2:
            u_tile = sb(s2, "d_u", [P, 2, D])
            v_tile = sb(s2, "d_v", [P, 2, D])
            slot_tile = sb(s2, "d_slot", [P, 2, 2], I32)
            S = {n: sem(n) for n in ("d_normed", "d_ready", "d_taken", "dispatched0", "dispatched1")}
            block = s2.enter_context(nc.Block())

            @block.vector
            def _(dve):
                def tile(i, u):
                    t = i * 2 + u
                    tt = bass.ds(t, 1)
                    if not isinstance(i, int) or i > 0:
                        dve.wait_ge(S["d_ready"], t - 1)
                    dve.tensor_scalar(u_tile[:, u, :], X[:, tt, :].rearrange("p a c -> p (a c)"), mean1[:, tt], rstd1[:, tt],
                                      ALU.subtract, ALU.mult).then_inc(S["d_normed"], 1)
                    if not isinstance(i, int) or i > 0:
                        dve.wait_ge(S[f"dispatched{u}"], i * 32)
                    dve.tensor_scalar(slot_tile[:, u, :], slot_of[:, tt, :].rearrange("p a c -> p (a c)"), 1.0, None, ALU.mult)
                    dve.wait_ge(S["d_normed"], t + 1)
                    dve.tensor_scalar(v_tile[:, u, :], u_tile[:, u, :], mean2[:, tt], rstd2[:, tt], ALU.subtract, ALU.mult).then_inc(S["d_ready"], 1)

                def pair(i):
                    tile(i, 0)
                    tile(i, 1)

                first_then_rest(dve, NT // 2, pair)
                tile(NT // 2, 0)

            @block.gpsimd
            def _(pool):
                def tile(i, u):
                    pool.wait_ge(S["d_ready"], i * 2 + u + 1)
                    pool.sem_inc(S["d_taken"], 1)
                    for n in range(2):
                        pool.indirect_dma_start(in_slots, bass.IndirectOffsetOnAxis(slot_tile[:, u, n:n + 1], 0), v_tile[:, u, :],
                                                None).then_inc(S[f"dispatched{u}"], 16)

                with pool.Fori(0, NT // 2) as i:
                    tile(i, 0)
                    tile(i, 1)
                tile(NT // 2, 0)
                pool.wait_ge(S["dispatched0"], 32 * ((NT + 1) // 2))
                pool.wait_ge(S["dispatched1"], 32 * (NT // 2))

        with ExitStack() as s2:
            w1_sb = sb(s2, "w1_sb", [P, 2, KC, FH])
            w2_sb = sb(s2, "w2_sb", [P, 2, FC, D])
            slot_in = sb(s2, "slot_in", [P, 2, ST, D])
            xt = sb(s2, "xt", [P, 2, KC, SG])
            hid = sb(s2, "hid", [P, 2, FC, SG])
            slot_out = sb(s2, "slot_out", [P, 2, ST, D])
            ps_x = [pb(s2, f"ps_x{i}", [P, KC, SG]) for i in range(2)]
            ps_h = [pb(s2, f"ps_h{i}", [P, 512]) for i in range(2)]
            ps_y = [pb(s2, f"ps_y{i}", [P, ST, D]) for i in range(2)]
            S = {n: sem(n) for n in ("w1_in0", "w1_in1", "w2_in0", "w2_in1", "slots_in0", "slots_in1", "sp_passed", "x_turned", "xt_made", "hidden_done",
                                     "gelu_done", "out_done", "out_kept", "slots_out0", "slots_out1")}
            block = s2.enter_context(nc.Block())

            def turns(engine, step):
                def turn(i):
                    step(i, 0)
                    step(i, 1)
                turn(0)
                with engine.Fori(1, EG // 2 - 1) as i:
                    turn(i)
                turn(EG // 2 - 1)

            def wait(engine, name, value):
                if not isinstance(value, int) or value > 0:
                    engine.wait_ge(S[name], value)

            in_view = in_slots.rearrange("(g j p) c -> p g j c", j=ST, p=P)
            out_view = out_slots.rearrange("(g j p) c -> p g j c", j=ST, p=P)
            w1_view = w1.rearrange("e (k p) f -> p e k f", p=P)
            w2_view = w2.rearrange("e (k p) c -> p e k c", p=P)

            @block.sync
            def _(sp):
                def step(i, u):
                    g = i * 2 + u
                    e = sp.value_load(expert_of[0:1, bass.ds(g, 1)], min_val=0, max_val=NE - 1)
                    wait(sp, "x_turned", g - 1)
                    sp.sem_inc(S["sp_passed"], 1)
                    sp.dma_start(slot_in[:, u, :, :], in_view[:, bass.ds(g, 1), :, :].rearrange("p a j c -> p (a j) c")).then_inc(S[f"slots_in{u}"], 16)
                    wait(sp, "hidden_done", (g - 1) * FC)
                    sp.sem_inc(S["sp_passed"], 1)
                    sp.dma_start(w1_sb[:, u, :, :], w1_view[:, bass.ds(e, 1), :, :].rearrange("p a k f -> p (a k) f")).then_inc(S[f"w1_in{u}"], 16)
                    wait(sp, "out_done", g - 1)
                    sp.sem_inc(S["sp_passed"], 1)
                    sp.dma_start(w2_sb[:, u, :, :], w2_view[:, bass.ds(e, 1), :, :].rearrange("p a k c -> p (a k) c")).then_inc(S[f"w2_in{u}"], 16)
                turns(sp, step)

            @block.scalar
            def _(act):
                def step(i, u):
                    g = i * 2 + u
                    e = act.value_load(expert_of[0:1, bass.ds(g, 1)], min_val=0, max_val=NE - 1)
                    wait(act, "x_turned", g + 1)
                    wait(act, "hidden_done", (g - 1) * FC)
                    for k in range(KC):
                        ins = act.activation(xt[:, u, k, :], ps_x[u][:, k, :], ACT.Identity, bias=gains[:, 1, bass.ds(e * KC + k, 1)],
                                             scale=gains[:, 0, bass.ds(e * KC + k, 1)])
                    ins.then_inc(S["xt_made"], 1)
                    wait(act, "out_done", g - 1)
                    for f in range(FC):
                        wait(act, "hidden_done", g * FC + f + 1)
                        act.activation(hid[:, u, f, :], ps_h[f % 2][:, 0:SG], ACT.Gelu, bias=b1t[:, bass.ds(e * FC + f, 1)]).then_inc(S["gelu_done"], 1)
                turns(act, step)

            @block.vector
            def _(dve):
                def step(i, u):
                    g = i * 2 + u
                    wait(dve, f"slots_out{u}", i * 16)
                    wait(dve, "out_done", g + 1)
                    dve.tensor_scalar(slot_out[:, u, :, :], ps_y[u][:], 1.0, None, ALU.mult).then_inc(S["out_kept"], 1)
                turns(dve, step)

            @block.gpsimd
            def _(pool):
                def step(i, u):
                    g = i * 2 + u
                    wait(pool, "out_kept", g + 1)
                    pool.dma_start(out_view[:, bass.ds(g, 1), :, :].rearrange("p a j c -> p (a j) c"), slot_out[:, u, :, :]).then_inc(S[f"slots_out{u}"], 16)
                turns(pool, step)
                for u in range(2):
                    pool.wait_ge(S[f"slots_out{u}"], 16 * (EG // 2))

            @block.tensor
            def _(pe):
                def turn_slots(i, u):
                    wait(pe, f"slots_in{u}", i * 16 + 16)
                    wait(pe, "xt_made", i * 2 + u - 1)
                    for k in range(KC):
                        for j in range(ST):
                            ins = pe.transpose(ps_x[u][:, k, j * P:(j + 1) * P], slot_in[:, u, j, k * P:(k + 1) * P], ident[:])
                    ins.then_inc(S["x_turned"], 1)

                turn_slots(0, 0)

                def step(i, u):
                    g = i * 2 + u
                    e = pe.value_load(expert_of[0:1, bass.ds(g, 1)], min_val=0, max_val=NE - 1)
                    wait(pe, f"w1_in{u}", i * 16 + 16)
                    wait(pe, "xt_made", g + 1)
                    for f in range(FC):
                        wait(pe, "gelu_done", g * FC + f - 1)
                        for k in range(KC):
                            ins = pe.matmul(ps_h[f % 2][:, 0:SG], w1_sb[:, u, k, f * P:(f + 1) * P], xt[:, u, k, :], start=(k == 0), stop=(k == KC - 1))
                        ins.then_inc(S["hidden_done"], 1)
                    if not isinstance(g, int) or g + 1 < EG:
                        turn_slots(i + (u + 1) // 2, (u + 1) % 2)
                    wait(pe, f"w2_in{u}", i * 16 + 16)
                    wait(pe, "out_kept", g - 1)
                    wait(pe, "gelu_done", g * FC + FC)
                    for j in range(ST):
                        for f in range(FC):
                            pe.matmul(ps_y[u][:, j, :], hid[:, u, f, j * P:(j + 1) * P], w2_sb[:, u, f, :], start=(f == 0), stop=False)
                        ins = pe.matmul(ps_y[u][:, j, :], ones[0:1, :], b2row[0:1, bass.ds(e * D, D)], start=False, stop=True)
                    ins.then_inc(S["out_done"], 1)
                turns(pe, step)

        with ExitStack() as s2:
            CB = 4
            slot_all = sb(s2, "c_slot", [P, NT, 2], I32)
            slot_tile = sb(s2, "c_slots", [P, CB, 2], I32)
            y = sb(s2, "c_y", [P, CB, 2, D])
            S = {n: sem(n) for n in ["c_chain", "c_taken", "combined", "c_ready", "stored"] + [f"c_staged{u}" for u in range(CB)] + [f"c_in{u}" for u in range(CB)]}
            block = s2.enter_context(nc.Block())
            TURNS = NT // CB

            def wait(engine, name, value):
                if not isinstance(value, int) or value > 0:
                    engine.wait_ge(S[name], value)

            def turns(engine, step):
                def turn(i):
                    for u in range(CB):
                        step(i, u)
                first_then_rest(engine, TURNS, turn)
                for u in range(NT - TURNS * CB):
                    step(TURNS, u)

            @block.scalar
            def _(act):
                def step(i, u):
                    wait(act, f"c_in{u}", i * 32)
                    act.activation(slot_tile[:, u, :], slot_of[:, bass.ds(i * CB + u, 1), :].rearrange("p a c -> p (a c)"), ACT.Copy).then_inc(S[f"c_staged{u}"], 1)
                turns(act, step)

            @block.gpsimd
            def _(pool):
                def step(i, u):
                    wait(pool, f"c_staged{u}", i + 1)
                    wait(pool, "combined", (i - 1) * CB + u + 1)
                    pool.sem_inc(S["c_taken"], 1)
                    for n in range(2):
                        pool.indirect_dma_start(y[:, u, n, :], None, out_slots, bass.IndirectOffsetOnAxis(slot_tile[:, u, n:n + 1], 0)).then_inc(S[f"c_in{u}"], 16)
                turns(pool, step)

            @block.vector
            def _(dve):
                def step(i, u):
                    t = i * CB + u
                    xt_ = X[:, bass.ds(t, 1), :].rearrange("p a c -> p (a c)")
                    wait(dve, f"c_in{u}", i * 32 + 32)
                    dve.scalar_tensor_tensor(xt_, y[:, u, 0, :], weight[:, bass.ds(t, 1), 0], xt_, ALU.mult, ALU.add).then_inc(S["c_chain"], 1)
                    dve.wait_ge(S["c_chain"], t + 1)
                    dve.scalar_tensor_tensor(xt_, y[:, u, 1, :], weight[:, bass.ds(t, 1), 1], xt_, ALU.mult, ALU.add).then_inc(S["combined"], 1)
                turns(dve, step)

            @block.sync
            def _(sp):
                n = 0
                for t0 in range(0, NT - 1, 8):
                    m = min(8, NT - 1 - t0)
                    sp.wait_ge(S["combined"], t0 + m)
                    sp.dma_start(out[t0 * P:(t0 + m) * P, :].rearrange("(t p) f -> p t f", p=P), X[:, t0:t0 + m, :]).then_inc(S["stored"], 16)
                    n += 16
                sp.wait_ge(S["combined"], NT)
                sp.dma_start(out[(NT - 1) * P:N, :], X[0:LAST, NT - 1, :]).then_inc(S["stored"], 16)
                sp.wait_ge(S["stored"], n + 16)


_INS = ["x", "src", "dst", "L0_gnn_W", "L0_gnn_a_l", "L0_gnn_a_r", "L0_mix_w_qkv", "L0_mix_mem_kv", "L0_mix_w_out", "L0_mix_b_out",
        "L0_mix_g_out", "L0_mix_g_pre", "L0_ffn_Wr", "L0_ffn_br", "L0_ffn_ln_g", "L0_ffn_ln_b", "L0_ffn_W1", "L0_ffn_b1", "L0_ffn_W2",
        "L0_ffn_b2"]
_OUTS = [((6250, 256), "float32")]


def kernel(**inputs):
    import numpy as _np
    import concourse.bacc as _bacc
    from concourse import mybir as _mybir
    from concourse.bass_utils import run_bass_kernel_spmd as _run

    nc = _bacc.Bacc("TRN2", target_bir_lowering=False, num_devices=1)
    arrays, args = {}, []
    for name in _INS:
        a = _np.ascontiguousarray(inputs[name])
        arrays[f"in_{name}_dram"] = a
        args.append(nc.dram_tensor(f"in_{name}_dram", a.shape, _mybir.dt.from_np(a.dtype), kind="ExternalInput").ap())
    for i, (shape, dtype) in enumerate(_OUTS):
        dt = _mybir.dt.from_np(_np.dtype(dtype))
        args.append(nc.dram_tensor(f"out_{i}_dram", shape, dt, kind="ExternalOutput").ap())
    gps_layer_kernel(nc, *args)
    r = _run(nc, [arrays], core_ids=[0])
    return r.results[0]["out_0_dram"]
```

```python
import concourse.bass as bass
from concourse import mybir
from contextlib import ExitStack

FP32 = mybir.dt.float32
FP32R = mybir.dt.float32r
BF16 = mybir.dt.bfloat16
FP16 = mybir.dt.float16
I32 = mybir.dt.int32
ALU = mybir.AluOpType
ACT = mybir.ActivationFunctionType
AX = mybir.AxisListType.X


class Chain:

    def __init__(self, engine, sem):
        self.engine, self.sem, self.base, self.k, self.closed = engine, sem, 0, 0, True

    def turn(self, i, per):
        if self.closed:
            self.start, self.closed = self.base, False
        self.at, self.k, self.per = i * per + self.start, 0, per
        return self

    def straight(self):
        self.start = self.at = self.base
        self.k, self.per, self.closed = 0, None, False
        return self

    def link(self, instruction):
        self.k += 1
        instruction.then_inc(self.sem, 1)
        self.engine.wait_ge(self.sem, self.at + self.k)

    def tick(self, instruction):
        self.k += 1
        instruction.then_inc(self.sem, 1)
        return self.at + self.k

    def need(self, value):
        self.engine.wait_ge(self.sem, value)

    def publish(self, instruction, sem, count):
        instruction.then_inc(sem, 1)
        self.engine.wait_ge(sem, count)

    def done(self, turns):
        assert self.per in (None, self.k), (self.k, self.per)
        self.base, self.closed = self.start + turns * self.k, True


def first_then_rest(engine, turns, body):
    body(0)
    with engine.Fori(1, turns) as i:
        body(i)


def gps_layer_kernel(nc, x, src, dst, gnn_w, gnn_al, gnn_ar, mix_wqkv, mix_mem, mix_wout, mix_bout,
                     mix_gout, mix_gpre, wr, br, ln_g, ln_b, w1, b1, w2, b2, out):
    P = 128
    N, D = x.shape
    E = src.shape[0]
    NT = (N + P - 1) // P
    LAST = N - (NT - 1) * P
    HEADS, HD = gnn_al.shape[1], gnn_al.shape[2]
    HP = HD + 1
    KC = D // P
    EP = 125
    EC = E // EP
    assert EP * EC == E
    GT = 4
    G = GT * P
    UN = 6
    NG = (E + NT * (G - 1)) // G
    TURNS = (NG + UN - 1) // UN
    NG = TURNS * UN
    assert TURNS <= P
    NSLOT = NG * G
    COLBITS = 13
    assert NT * P <= 1 << COLBITS
    PADCOL = NT * P - 1
    PADREC = (P << COLBITS) + PADCOL
    TW = HEADS * HP + 6
    SK = 10
    STURNS = EC // SK
    assert SK * STURNS == EC
    MH, MD, MM = mix_mem.shape[1], mix_mem.shape[2], mix_mem.shape[3]
    HID = MH * MD
    QW = 3 * HID
    NE, FH = w1.shape[0], w1.shape[2]
    FC = FH // P
    FT = 4
    BIG = 1e30
    FAR = 2.0 ** 100
    LN_EPS = 1e-5

    slots = nc.dram_tensor("slots", [NSLOT, 1], I32).ap()
    table = nc.dram_tensor("table", [NT * P, TW], FP32).ap()

    top = ExitStack()

    def sem(name):
        return top.enter_context(nc.semaphore(name))

    def sb(stack, name, shape, dt=FP32):
        return stack.enter_context(nc.sbuf_tensor(name, shape, dt))

    def pb(stack, name, shape, dt=FP32):
        return stack.enter_context(nc.psum_tensor(name, shape, dt))

    with top:
        waits_passed = sem("waits_passed")
        X = sb(top, "X", [P, NT, D])
        ident = sb(top, "ident", [P, P])
        identb = sb(top, "identb", [P, P], BF16)
        iota_row = sb(top, "iota_row", [P, P])
        iota_i = sb(top, "iota_i", [P, 1], I32)
        iota_p = sb(top, "iota_p", [P, 1])
        ones = sb(top, "ones", [P, P])
        hl = sb(top, "hl", [P, NT, HEADS])
        start_row = sb(top, "start_row", [P, NT])
        block_of = sb(top, "block_of", [1, NG], I32)
        acc = sb(top, "acc", [P, NT, HEADS * HP])

        binning_and_nodes(nc, locals())
        attention(nc, locals())
        experts(nc, locals())


def binning_and_nodes(nc, v):
    P, N, D, E, NT, LAST, HEADS, HD, HP, KC = (v[k] for k in ("P", "N", "D", "E", "NT", "LAST", "HEADS", "HD", "HP", "KC"))
    EP, EC, G, NG, NSLOT, COLBITS, PADREC, SK, STURNS, TW = (v[k] for k in ("EP", "EC", "G", "NG", "NSLOT", "COLBITS", "PADREC", "SK", "STURNS", "TW"))
    MH, MD, MM, HID, QW, BIG, LN_EPS = (v[k] for k in ("MH", "MD", "MM", "HID", "QW", "BIG", "LN_EPS"))
    X, ident, identb, iota_row, iota_i, iota_p, ones, hl, start_row, block_of, acc = (v[k] for k in ("X", "ident", "identb", "iota_row", "iota_i", "iota_p", "ones", "hl", "start_row", "block_of", "acc"))
    sem, sb, pb, slots, table, waits_passed = v["sem"], v["sb"], v["pb"], v["slots"], v["table"], v["waits_passed"]
    x = v["x"]
    LG = G.bit_length() - 1
    PAIR = MM

    with ExitStack() as s:
        records = sb(s, "records", [EP, 2, EC], I32)
        qkv = sb(s, "qkv", [P, NT, QW + 1])
        lists = acc[0:EP, :, :].rearrange("p a b -> p (a b)")

        def edge_list(n, dt):
            view = lists[:, n * EC:(n + 1) * EC].bitcast(dt)
            return view if dt == I32 else view.rearrange("p (u e) -> p u e", u=2)

        rows_i, cols_i, bins_i = (edge_list(n, I32) for n in range(3))
        masks, parts, scan_and_bin = (edge_list(n, FP16) for n in range(3, 6))
        his = edge_list(0, FP16)
        scan, bin_h = scan_and_bin[:, 0, :], scan_and_bin[:, 1, :]
        assert EC <= 2048 and NT < P
        HALF = 512
        assert NSLOT // HALF <= 2048
        counts = sb(s, "counts", [EP, NT])
        before = sb(s, "before", [EP, NT])
        before_i, half_i = (sb(s, n, [EP, NT], I32) for n in ("before_i", "half_i"))
        before_hi, before_lo = (sb(s, n, [EP, NT]) for n in ("before_hi", "before_lo"))
        ident_h, ident_half = (sb(s, n, [EP, EP], FP16) for n in ("ident_h", "ident_half"))
        groups_i = sb(s, "groups_i", [P, NT], I32)
        groups_f = sb(s, "groups_f", [P, NT])
        zeros = sb(s, "zeros", [P, NT])
        col_i = sb(s, "col_i", [NT, 1], I32)
        col_f = sb(s, "col_f", [NT, 1])
        start_col = sb(s, "start_col", [NT, 1])
        tri = sb(s, "tri", [P, P])
        giota = sb(s, "giota", [NT, NG])
        reached = giota
        padrec = sb(s, "padrec", [P, NSLOT // P], I32)
        block_f = sb(s, "block_f", [1, NG])

        sl, sc, sd, spe, sdv, sfill = (sem(n) for n in ("edges_loaded", "constants_made", "list_chain", "counts_summed", "counts_ready", "slots_filled"))
        parts_made, parts_added, bases_made, bases_added = (sem(n) for n in ("parts_made", "parts_added", "bases_made", "bases_added"))
        x_loaded = sem("x_loaded")
        with ExitStack() as s2:
            ps_before = pb(s2, "ps_before", [EP, 512])
            ps_total = pb(s2, "ps_total", [P, 512])
            ps_col = pb(s2, "ps_col", [P, 512])
            ps_block = pb(s2, "ps_block", [P, 512])
            ps_slot = pb(s2, "ps_slot", [EP, 2048])
            block = s2.enter_context(nc.Block())

            @block.sync
            def _(sp):
                sp.dma_start(rows_i, v["src"].rearrange("(p c) -> p c", p=EP)).then_inc(sl, 16)
                sp.dma_start(cols_i, v["dst"].rearrange("(p c) -> p c", p=EP)).then_inc(sl, 16)
                sp.wait_ge(sc, 1)
                sp.dma_start(slots.rearrange("(p c) o -> p (c o)", p=P), padrec[:]).then_inc(sfill, 16)
                sp.wait_ge(sfill, 16)

            @block.scalar
            def _(act):
                act.wait_ge(sc, 7)
                for t0 in range(0, NT - 1, 8):
                    n = min(8, NT - 1 - t0)
                    act.dma_start(X[:, t0:t0 + n, :], x[t0 * P:(t0 + n) * P, :].rearrange("(t p) f -> p t f", p=P)).then_inc(x_loaded, 16)
                act.dma_start(X[0:LAST, NT - 1, :], x[(NT - 1) * P:N, :]).then_inc(x_loaded, 16)
                act.wait_ge(x_loaded, 16 * ((NT - 1 + 7) // 8 + 1))

            @block.gpsimd
            def _(pool):
                pool.memset(padrec[:], PADREC).then_inc(sc, 1)
                pool.iota(iota_row[:], pattern=[[1, P]], base=0, channel_multiplier=0, allow_small_or_imprecise_dtypes=True).then_inc(sc, 1)
                pool.iota(iota_i[:], pattern=[[0, 1]], base=0, channel_multiplier=1).then_inc(sc, 1)
                pool.iota(giota[:], pattern=[[1, NG]], base=0, channel_multiplier=0, allow_small_or_imprecise_dtypes=True).then_inc(sc, 1)
                pool.memset(ones[:], 1.0).then_inc(sc, 1)
                pool.memset(zeros[:], 0.0).then_inc(sc, 1)
                pool.memset(X[:, NT - 1, :], 0.0).then_inc(sc, 1)

            @block.vector
            def _(dve):
                c = Chain(dve, sd)
                dve.wait_ge(sc, 7)
                dve.wait_ge(sl, 32)
                c.straight()
                c.link(dve.tensor_copy(iota_p[:], iota_i[:]))
                c.link(dve.tensor_scalar(ident[:], iota_row[:], iota_p[:], None, ALU.is_equal))
                c.link(dve.tensor_copy(identb[:], ident[:]))
                c.link(dve.tensor_scalar(tri[:], iota_row[:], iota_p[:], None, ALU.is_gt))
                c.link(dve.tensor_single_scalar(bins_i, rows_i, 7, ALU.logical_shift_right))
                c.link(dve.tensor_copy(bin_h, bins_i))
                c.link(dve.tensor_copy(ident_h[:], ident[0:EP, 0:EP]))
                c.link(dve.tensor_scalar(ident_half[:], ident[0:EP, 0:EP], float(HALF), None, ALU.mult))
                c.link(dve.tensor_scalar(bins_i, rows_i, P - 1, COLBITS, ALU.bitwise_and, ALU.logical_shift_left))
                c.link(dve.tensor_tensor(records[:, 1, :], bins_i, cols_i, ALU.bitwise_or))
                c.link(dve.memset(start_row[:], 0.0))
                c.link(dve.memset(qkv[:, :, QW:QW + 1], 1.0))
                c.done(1)
                c.straight()
                c.link(dve.tensor_scalar(masks[:, 0, :], bin_h, iota_row[0:EP, 0:1], None, ALU.is_equal))
                c.done(1)

                def rank_edges(b, u):
                    c.turn(b, 3)
                    counted = c.tick(dve.tensor_tensor_scan(scan, masks[:, u, :], masks[:, u, :], 0.0, ALU.add, ALU.max))
                    c.tick(dve.tensor_scalar(masks[:, 1 - u, :], bin_h, iota_row[0:EP, bass.ds(b + 1, 1)], None, ALU.is_equal))
                    c.need(counted)
                    if not isinstance(b, int) or b >= 2:
                        dve.wait_ge(parts_added, b - 1)
                    dve.tensor_tensor(parts[:, u, :], scan, masks[:, u, :], ALU.mult).then_inc(parts_made, 1)
                    c.link(dve.tensor_scalar(counts[:, bass.ds(b, 1)], scan[:, EC - 1:EC], 1.0, None, ALU.mult))

                rank_edges(0, 0)
                rank_edges(1, 1)
                with dve.Fori(1, NT // 2) as i:
                    rank_edges(i * 2, 0)
                    rank_edges(i * 2 + 1, 1)
                rank_edges(NT - 1, 0)
                c.done(NT)
                dve.nop().then_inc(sdv, 1)
                dve.wait_ge(spe, 1)
                c.straight()
                c.link(dve.tensor_scalar(groups_i[:], ps_total[:, 0:NT], float(G - 1), None, ALU.add))
                c.link(dve.tensor_single_scalar(groups_i[:], groups_i[:], LG, ALU.logical_shift_right))
                c.link(dve.tensor_copy(groups_f[:], groups_i[:]))
                c.link(dve.tensor_tensor_scan(start_row[:], groups_f[:], zeros[:], 0.0, ALU.add, ALU.add))
                c.link(dve.tensor_tensor(start_row[:], start_row[:], groups_f[:], ALU.subtract))
                c.link(dve.scalar_tensor_tensor(before[:], start_row[0:EP, :], float(G), ps_before[:, 0:NT], ALU.mult, ALU.add))
                c.link(dve.tensor_scalar(col_i[:], ps_col[0:NT, 0:1], float(G - 1), None, ALU.add))
                c.link(dve.tensor_single_scalar(col_i[:], col_i[:], LG, ALU.logical_shift_right))
                c.publish(dve.tensor_copy(col_f[:], col_i[:]), sdv, 2)
                dve.wait_ge(spe, 2)
                c.link(dve.tensor_copy(start_col[:], ps_col[0:NT, 1:2]))
                c.done(1)
                c.straight()
                c.publish(dve.tensor_scalar(reached[:], giota[:], start_col[:], None, ALU.is_ge), sdv, 3)
                c.done(1)
                c.straight()
                c.link(dve.tensor_copy(before_i[:], before[:]))
                c.link(dve.tensor_single_scalar(half_i[:], before_i[:], HALF.bit_length() - 1, ALU.logical_shift_right))
                c.link(dve.tensor_copy(before_hi[:], half_i[:]))
                c.link(dve.tensor_single_scalar(half_i[:], before_i[:], HALF - 1, ALU.bitwise_and))
                c.link(dve.tensor_copy(before_lo[:], half_i[:]))
                dve.wait_ge(parts_added, NT)

                def spread_base(b, u):
                    if not isinstance(b, int) or b >= 2:
                        dve.wait_ge(bases_added, b - 1)
                    at = bass.ds(b, 1)
                    dve.tensor_scalar(his[:, u, :], bin_h, iota_row[0:EP, at], before_hi[:, at], ALU.is_equal, ALU.mult)
                    dve.tensor_scalar(masks[:, u, :], bin_h, iota_row[0:EP, at], before_lo[:, at], ALU.is_equal, ALU.mult).then_inc(bases_made, 1)

                spread_base(0, 0)
                spread_base(1, 1)
                with dve.Fori(1, NT // 2) as i:
                    spread_base(i * 2, 0)
                    spread_base(i * 2 + 1, 1)
                spread_base(NT - 1, 0)
                c.done(1)
                dve.wait_ge(spe, 3)
                c.straight()
                dve.wait_ge(bases_added, NT)
                c.link(dve.tensor_scalar(records[:, 0, :], ps_slot[:, 0:EC], -1.0, None, ALU.add))
                c.link(dve.tensor_scalar(block_of[:], ps_block[0:1, 0:NG], -1.0, None, ALU.add))
                c.done(1)

            @block.tensor
            def _(pe):
                def add(weights, values, start, stop):
                    for c0 in range(0, EC, 512):
                        c1 = min(c0 + 512, EC)
                        ins = pe.matmul(ps_slot[:, c0:c1], weights, values[:, c0:c1], start=start, stop=stop)
                    return ins

                def add_rank(b, u, start=False):
                    pe.wait_ge(parts_made, b + 1)
                    add(ident_h[:], parts[:, u, :], start, False).then_inc(parts_added, 1)

                add_rank(0, 0, start=True)
                add_rank(1, 1)
                with pe.Fori(1, NT // 2) as i:
                    add_rank(i * 2, 0)
                    add_rank(i * 2 + 1, 1)
                add_rank(NT - 1, 0)
                pe.wait_ge(sdv, 1)
                pe.matmul(ps_before[:, 0:NT], tri[0:EP, 0:EP], counts[:], start=True, stop=True)
                pe.matmul(ps_total[:, 0:NT], ones[0:EP, :], counts[:], start=True, stop=True)
                pe.matmul(ps_col[0:NT, 0:1], counts[:], ones[0:EP, 0:1], start=True, stop=True).then_inc(spe, 1)
                pe.wait_ge(sdv, 2)
                pe.matmul(ps_col[0:NT, 1:2], tri[0:NT, 0:NT], col_f[:], start=True, stop=True).then_inc(spe, 1)
                pe.wait_ge(sdv, 3)
                pe.matmul(ps_block[0:1, 0:NG], ones[0:NT, 0:1], reached[:], start=True, stop=True).then_inc(spe, 1)

                def add_base(b, u, stop=False):
                    pe.wait_ge(bases_made, b + 1)
                    add(ident_half[:], his[:, u, :], False, False)
                    add(ident_h[:], masks[:, u, :], False, stop).then_inc(bases_added, 1)

                add_base(0, 0)
                add_base(1, 1)
                with pe.Fori(1, NT // 2) as i:
                    add_base(i * 2, 0)
                    add_base(i * 2 + 1, 1)
                add_base(NT - 1, 0, stop=True)

        nodes(nc, {**v, **locals()})


def nodes(nc, v):
    P, N, D, E, NT, LAST, HEADS, HD, HP, KC = (v[k] for k in ("P", "N", "D", "E", "NT", "LAST", "HEADS", "HD", "HP", "KC"))
    EP, EC, G, NG, NSLOT, COLBITS, PADREC, SK, STURNS, TW = (v[k] for k in ("EP", "EC", "G", "NG", "NSLOT", "COLBITS", "PADREC", "SK", "STURNS", "TW"))
    MH, MD, MM, HID, QW, BIG, LN_EPS = (v[k] for k in ("MH", "MD", "MM", "HID", "QW", "BIG", "LN_EPS"))
    X, ident, identb, iota_row, iota_i, iota_p, ones, hl, acc = (v[k] for k in ("X", "ident", "identb", "iota_row", "iota_i", "iota_p", "ones", "hl", "acc"))
    sem, sb, pb, slots, table, records, qkv = (v[k] for k in ("sem", "sb", "pb", "slots", "table", "records", "qkv"))
    GW = HEADS * HD

    with ExitStack() as s:
        scratch = acc[:, :, :].rearrange("p a b -> p (a b)")
        used = [0]

        def carve(width):
            at = used[0]
            used[0] += width
            assert used[0] <= NT * HEADS * HP
            return scratch[:, at:at + width]

        w_all = carve(KC * (GW + QW)).rearrange("p (k c) -> p k c", k=KC)
        a_both = carve(2 * GW)
        gpre = carve(KC)
        stats = carve(NT * 6).rearrange("p (t c) -> p t c", t=NT)
        mean = carve(NT)
        var = carve(NT)
        rstd = carve(NT)
        sig = carve(NT)
        rms = carve(NT)
        xn = carve(2 * D).rearrange("p (b c) -> p b c", b=2)
        xnt = carve(2 * D).rearrange("p (b k c) -> p b k c", b=2, k=KC)
        row_tile = carve(2 * HEADS * HP).rearrange("p (b h c) -> p b h c", b=2, h=HEADS)
        prod = carve(2 * GW)
        nanmask = carve(GW)
        h_raw = carve(2 * GW).rearrange("p (b c) -> p b c", b=2)
        hr = carve(NT * HEADS)
        res = carve(NT * HEADS)
        split = carve(NT * 6)
        kcol = carve(HID)
        kmax = carve(4)
        kdiag = carve(HID)
        krow = carve(HID)
        qstat = carve(NT * MH)
        qsum = carve(NT * MH)
        mem_k = carve(MM)
        mem_v = carve(MM)
        mem_e = carve(MM)
        memkt = carve(HID)
        memvt = carve(HID + 1)
        ctx_r = carve(1)
        ctx_n = carve(HID)
        ctx_t = carve(HID)
        blockm = carve(HID)
        wout = carve(D)
        wc = carve(D)
        bout = carve(D)
        gout = carve(D)
        p5 = carve(1)
        p5i = carve(1).bitcast(I32)
        padneg = carve(1)
        ktile = carve(2 * HID).rearrange("p (b c) -> p b c", b=2)
        qt = carve(2 * HID).rearrange("p (b c) -> p b c", b=2)
        qs = carve(2 * HID).rearrange("p (b c) -> p b c", b=2)
        n2 = carve(NT)
        junk = carve(D)
        staged = sb(s, "staged", [EP, 2, 2, SK], I32)

        ps_t = [pb(s, f"ps_t{i}", [P, KC, P]) for i in range(2)]
        ps_g = [pb(s, f"ps_g{i}", [P, 512]) for i in range(2)]
        ps_q = [pb(s, f"ps_q{i}", [P, 512]) for i in range(2)]
        ps_c = pb(s, "ps_c", [P, 512])
        ps_m = pb(s, "ps_m", [P, 512])

        names = ("weights_loaded", "moments_done", "sigma_ready", "act_chain", "dve_chain", "normed", "transposed", "xnt_ready",
                 "projected", "h_copied", "qkv_kept", "heads_kept", "row_ready0", "row_ready1", "rows_stored0", "rows_stored1", "consts2", "records_staged0",
                 "records_staged1", "scattered0", "scattered1", "split_ready", "split_stored", "k_column", "k_column_t", "k_diag", "k_row",
                 "k_shifted", "k_exp", "q_shifted", "q_exp", "k_used", "mem_ready", "mem_t", "mem_t_kept", "context", "context_n", "context_t", "context_t_kept", "wc_done", "wc_kept",
                 "q_scaled", "q_t", "q_t_kept", "mask_made", "records_taken", "mixed", "mix_kept", "mix_sigma")
        S = {n: sem(n) for n in names}
        table_rows = table[:, 0:HEADS * HP].rearrange("(t p) c -> p t c", p=P)
        block = s.enter_context(nc.Block())

        @block.sync
        def _(sp):
            def turn(i, u):
                if not isinstance(i, int) or i > 0:
                    sp.wait_ge(S[f"scattered{u}"], i * 16 * SK)
                j = i * 2 + u
                sp.dma_start(staged[:, u, :, :], records[:, :, bass.ds(j * SK, SK)]).then_inc(S[f"records_staged{u}"], 16)

            def both(i):
                turn(i, 0)
                turn(i, 1)

            with nc.allow_non_contiguous_dma(reason="records of 4 bytes"):
                first_then_rest(sp, STURNS // 2, both)
                if STURNS % 2:
                    turn(STURNS // 2, 0)

        @block.gpsimd
        def _(pool):
            def turn(i, u):
                pool.wait_ge(S[f"records_staged{u}"], (i + 1) * 16)
                pool.sem_inc(S["records_taken"], 1)
                for k in range(SK):
                    pool.indirect_dma_start(slots, bass.IndirectOffsetOnAxis(staged[:, u, 0, k:k + 1], 0),
                                            staged[:, u, 1, k:k + 1], None).then_inc(S[f"scattered{u}"], 16)

            with pool.Fori(0, STURNS // 2) as i:
                turn(i, 0)
                turn(i, 1)
            if STURNS % 2:
                turn(STURNS // 2, 0)
            pool.wait_ge(S["scattered0"], 16 * SK * ((STURNS + 1) // 2))
            pool.wait_ge(S["scattered1"], 16 * SK * (STURNS // 2))

        @block.scalar
        def _(act):
            c = Chain(act, S["act_chain"])
            ld = S["weights_loaded"]
            for dst_, src_ in (
                (w_all[:, :, 0:GW], v["gnn_w"].rearrange("(k p) c -> p k c", p=P)),
                (w_all[:, :, GW:GW + QW], v["mix_wqkv"].rearrange("(k p) c -> p k c", p=P)),
                (a_both[:, 0:GW], v["gnn_ar"].rearrange("a h c -> a (h c)").to_broadcast([P, GW])),
                (a_both[:, GW:2 * GW], v["gnn_al"].rearrange("a h c -> a (h c)").to_broadcast([P, GW])),
                (mem_k, v["mix_mem"][0].rearrange("h d m -> (h d) m")),
                (mem_v, v["mix_mem"][1].rearrange("h d m -> (h d) m")),
                (wout, v["mix_wout"]),
                (bout[0:1, :], v["mix_bout"].rearrange("(a c) -> a c", a=1)),
                (gout, v["mix_gout"].rearrange("(a c) -> a c", a=1).to_broadcast([P, D])),
            ):
                act.dma_start(dst_, src_).then_inc(ld, 16)
            with nc.allow_non_contiguous_dma(reason="a column of scales"):
                act.dma_start(gpre, v["mix_gpre"].rearrange("(k p) -> p k", p=P)).then_inc(ld, 16)
            act.wait_ge(S["moments_done"], 1)
            act.activation(sig, rstd, ACT.Sqrt).then_inc(S["sigma_ready"], 1)
            act.activation(rms, var, ACT.Sqrt).then_inc(S["sigma_ready"], 1)

            def store_row(i, u):
                act.wait_ge(S[f"row_ready{u}"], i + 1)
                act.dma_start(table_rows[:, bass.ds(i * 2 + u, 1), :].rearrange("p a c -> p (a c)"),
                              row_tile[:, u, :, :].rearrange("p h c -> p (h c)")).then_inc(S[f"rows_stored{u}"], 16)

            def tile(i, u):
                t = i * 2 + u
                later = not isinstance(i, int) or i > 0
                if later or u:
                    store_row(i if u else i - 1, 1 - u)
                act.wait_ge(S["transposed"], t + 1)
                if later:
                    act.wait_ge(S["projected"], t - 1)
                act.activation(xnt[:, u, :, :], ps_t[u][:], ACT.Copy).then_inc(S["xnt_ready"], 1)
                act.wait_ge(S["projected"], t + 1)
                if later:
                    act.wait_ge(S["heads_kept"], t - 1)
                act.activation(h_raw[:, u, :], ps_g[u][:, 0:GW], ACT.Copy).then_inc(S["h_copied"], 1)
                act.activation(qkv[:, bass.ds(t, 1), 0:QW].rearrange("p a c -> p (a c)"), ps_q[u][:, 0:QW], ACT.Copy,
                               scale=rms[:, bass.ds(t, 1)]).then_inc(S["qkv_kept"], 1)

            def pair(i):
                tile(i, 0)
                tile(i, 1)

            act.wait_ge(S["normed"], 1)
            first_then_rest(act, NT // 2, pair)
            tile(NT // 2, 0)
            store_row(NT // 2, 0)
            act.wait_ge(S["q_shifted"], 1)
            act.activation(qkv[:, :, 0:HID], qkv[:, :, 0:HID], ACT.Exp).then_inc(S["q_exp"], 1)
            act.wait_ge(S["k_shifted"], 1)
            act.activation(mem_e, mem_k, ACT.Exp, bias=kmax[:, 1:2]).then_inc(S["mem_ready"], 1)

            def ktile_exp(i, u):
                t = i * 2 + u
                if not isinstance(i, int) or i > 0:
                    act.wait_ge(S["k_used"], t - 1)
                act.activation(ktile[:, u, :], qkv[:, bass.ds(t, 1), HID:2 * HID].rearrange("p a c -> p (a c)"), ACT.Exp).then_inc(S["k_exp"], 1)

            def kpair(i):
                ktile_exp(i, 0)
                ktile_exp(i, 1)

            first_then_rest(act, NT // 2, kpair)
            ktile_exp(NT // 2, 0)

            def mix_tile(i, u):
                t = i * 2 + u
                act.wait_ge(S["q_t"], t + 1)
                if not isinstance(i, int) or i > 0:
                    act.wait_ge(S["mixed"], t - 1)
                act.activation(qt[:, u, :], ps_t[u][:, 0, :], ACT.Copy).then_inc(S["q_t_kept"], 1)
                act.wait_ge(S["mixed"], t + 1)
                act.activation(junk, ps_g[u][:, 0:D], ACT.Square, accum_out=n2[:, bass.ds(t, 1)]).then_inc(S["act_chain"], 1)
                act.activation(qkv[:, bass.ds(t, 1), HID:HID + D].rearrange("p a c -> p (a c)"), ps_g[u][:, 0:D], ACT.Copy).then_inc(S["mix_kept"], 1)
                act.wait_ge(S["act_chain"], t + 1)

            def mix_pair(i):
                mix_tile(i, 0)
                mix_tile(i, 1)

            first_then_rest(act, NT // 2, mix_pair)
            mix_tile(NT // 2, 0)
            act.wait_ge(S["mix_kept"], NT)
            act.activation(n2, n2, ACT.Sqrt).then_inc(S["mix_sigma"], 1)
            act.wait_ge(S["split_ready"], 1)
            with nc.allow_non_contiguous_dma(reason="24 bytes of each row"):
                act.dma_start(table[:, HEADS * HP:TW].rearrange("(t p) c -> p t c", p=P),
                              split.rearrange("p (t c) -> p t c", t=NT)).then_inc(S["split_stored"], 16)
            act.wait_ge(S["split_stored"], 16)
            act.wait_ge(S["rows_stored0"], 16 * ((NT + 1) // 2))
            act.wait_ge(S["rows_stored1"], 16 * (NT // 2))

        @block.vector
        def _(dve):
            c = Chain(dve, S["dve_chain"])
            with dve.Fori(0, NT) as t:
                c.turn(t, 1)
                c.link(dve.bn_stats(stats[:, bass.ds(t, 1), :].rearrange("p a c -> p (a c)"), X[:, bass.ds(t, 1), :].rearrange("p a c -> p (a c)")))
            c.done(NT)
            c.straight()
            c.link(dve.tensor_tensor(mean, stats[:, :, 1], stats[:, :, 4], ALU.add))
            c.link(dve.tensor_tensor(var, stats[:, :, 1], stats[:, :, 4], ALU.subtract))
            c.link(dve.tensor_tensor(rms, stats[:, :, 2], stats[:, :, 5], ALU.add))
            c.link(dve.tensor_scalar(mean, mean, 0.5, None, ALU.mult))
            c.link(dve.scalar_tensor_tensor(var, var, 0.25, var, ALU.mult, ALU.mult))
            c.link(dve.scalar_tensor_tensor(var, rms, 1.0 / D, var, ALU.mult, ALU.add))
            c.publish(dve.tensor_scalar(rstd, var, LN_EPS, None, ALU.add), S["moments_done"], 1)
            dve.wait_ge(S["sigma_ready"], 2)
            c.link(dve.reciprocal(rstd, sig))
            c.done(1)
            c.straight()
            c.link(dve.tensor_tensor(rms, rms, rstd, ALU.mult))
            c.link(dve.tensor_scalar(rms, rms, float(D) ** 0.5, 1e-12, ALU.mult, ALU.max))
            c.link(dve.reciprocal(rms, rms))
            c.link(dve.tensor_scalar(rms, rms, float(D) ** 0.5, None, ALU.mult))
            dve.wait_ge(S["weights_loaded"], 160)
            for k in range(KC):
                c.link(dve.tensor_scalar(w_all[:, k, GW:GW + QW], w_all[:, k, GW:GW + QW], gpre[:, k:k + 1], None, ALU.mult))
            c.link(dve.tensor_scalar(gout, gout, float(D) ** 0.5, None, ALU.mult))
            c.link(dve.tensor_single_scalar(p5i, iota_i[:], MD.bit_length() - 1, ALU.logical_shift_right))
            c.link(dve.tensor_copy(p5, p5i))
            for h in range(MH):
                ins = dve.tensor_scalar(blockm[:, h * MD:(h + 1) * MD], p5.to_broadcast([P, MD]), float(h), MD ** -0.5, ALU.is_equal, ALU.mult)
            c.link(ins)
            c.link(dve.tensor_scalar(padneg, iota_p[:], float(LAST), -BIG, ALU.is_ge, ALU.mult))
            c.done(1)

            def tile(i, u):
                t = i * 2 + u
                later = not isinstance(i, int) or i > 0
                tt = bass.ds(t, 1)
                c.turn(t, 6)
                if later:
                    dve.wait_ge(S["transposed"], t - 1)
                c.publish(dve.tensor_scalar(xn[:, u, :], X[:, tt, :].rearrange("p a c -> p (a c)"), mean[:, tt], rstd[:, tt], ALU.subtract, ALU.mult), S["normed"], t + 1)
                c.link(dve.tensor_tensor(X[:, tt, :].rearrange("p a c -> p (a c)"), X[:, tt, :].rearrange("p a c -> p (a c)"), xn[:, u, :], ALU.add))
                if later:
                    dve.wait_ge(S[f"rows_stored{u}"], 16 * i)
                c.link(dve.memset(row_tile[:, u, :, 0:HD], 0.0))
                dve.wait_ge(S["h_copied"], t + 1)
                c.link(dve.tensor_tensor(nanmask, h_raw[:, u, :], ps_g[u][:, 0:GW], ALU.is_equal))
                dve.sem_inc(S["mask_made"], 1)
                c.publish(dve.copy_predicated(row_tile[:, u, :, 0:HD], nanmask.bitcast(I32).rearrange("p (h c) -> p h c", h=HEADS),
                                           ps_g[u][:, 0:GW].rearrange("p (h c) -> p h c", h=HEADS)), S["heads_kept"], t + 1)
                for n in range(2):
                    ins = dve.tensor_tensor(prod[:, n * GW:(n + 1) * GW].rearrange("p (h c) -> p h c", h=HEADS), row_tile[:, u, :, 0:HD],
                                            a_both[:, n * GW:(n + 1) * GW].rearrange("p (h c) -> p h c", h=HEADS), ALU.mult)
                    c.link(ins)
                dve.tensor_reduce(hl[:, tt, :].rearrange("p a h -> p (a h)"), prod[:, GW:2 * GW].rearrange("p (h c) -> p h c", h=HEADS), AX, ALU.add)
                c.link(dve.tensor_reduce(hr[:, bass.ds(t * HEADS, HEADS)], prod[:, 0:GW].rearrange("p (h c) -> p h c", h=HEADS), AX, ALU.add))
                c.publish(dve.tensor_scalar(row_tile[:, u, :, HD], hr[:, bass.ds(t * HEADS, HEADS)], 1.0, None, ALU.mult), S[f"row_ready{u}"], i + 1)

            def pair(i):
                tile(i, 0)
                tile(i, 1)

            first_then_rest(dve, NT // 2, pair)
            tile(NT // 2, 0)
            c.done(NT)
            dve.wait_ge(S["qkv_kept"], NT)
            c.straight()
            q = qkv[:, :, 0:HID].rearrange("p t (h d) -> p t h d", h=MH)

            def per_head(a):
                return a.rearrange("p (t h) -> p t h", h=MH).unsqueeze(3).broadcast_to([P, NT, MH, MD])

            c.link(dve.tensor_reduce(qstat.rearrange("p (t h) -> p t h", h=MH), q, AX, ALU.max))
            c.publish(dve.tensor_tensor(q, q, per_head(qstat), ALU.subtract), S["q_shifted"], 1)
            k_all = qkv[:, :, HID:2 * HID]
            c.link(dve.tensor_scalar(k_all[:, NT - 1, :], k_all[:, NT - 1, :], padneg, None, ALU.add))
            c.publish(dve.tensor_reduce(kcol, k_all.rearrange("p t c -> p c t"), AX, ALU.max), S["k_column"], 1)
            dve.wait_ge(S["k_column_t"], 1)
            c.link(dve.tensor_reduce(kmax[:, 0:1], ps_m[:, 0:P], AX, ALU.max))
            c.link(dve.tensor_reduce(kmax[:, 1:2], mem_k, AX, ALU.max))
            c.link(dve.tensor_tensor(kmax[:, 0:1], kmax[:, 0:1], kmax[:, 1:2], ALU.max))
            c.link(dve.tensor_scalar(kmax[:, 1:2], kmax[:, 0:1], -1.0, None, ALU.mult))
            c.publish(dve.tensor_scalar(kdiag, ident[:], kmax[:, 0:1], None, ALU.mult), S["k_diag"], 1)
            dve.wait_ge(S["k_row"], 1)
            c.link(dve.tensor_copy(krow, ps_m[:, P:2 * P]))
            c.publish(dve.tensor_tensor(k_all, k_all, krow.unsqueeze(1).broadcast_to([P, NT, HID]), ALU.subtract), S["k_shifted"], 1)
            dve.wait_ge(S["q_exp"], 1)
            c.link(dve.tensor_reduce(qsum.rearrange("p (t h) -> p t h", h=MH), q, AX, ALU.add))
            c.link(dve.reciprocal(qsum, qsum))
            dve.wait_ge(S["mem_t"], 1)
            dve.memset(memvt[:, HID:HID + 1], 1.0)
            dve.tensor_copy(memkt[0:MM, :], ps_m[0:MM, 256:256 + HID])
            c.publish(dve.tensor_copy(memvt[0:MM, 0:HID], ps_m[0:MM, 384:384 + HID]), S["mem_t_kept"], 1)
            parts = split.rearrange("p (t c) -> p t c", t=NT).bitcast(BF16)
            hr3 = hr.rearrange("p (t h) -> p t h", h=HEADS)
            res3 = res.rearrange("p (t h) -> p t h", h=HEADS)
            c.link(dve.tensor_copy(parts[:, :, 0:4], hr3))
            c.link(dve.tensor_tensor(res3, hr3, parts[:, :, 0:4], ALU.subtract))
            c.link(dve.tensor_copy(parts[:, :, 4:8], res3))
            c.link(dve.tensor_tensor(res3, res3, parts[:, :, 4:8], ALU.subtract))
            c.publish(dve.tensor_copy(parts[:, :, 8:12], res3), S["split_ready"], 1)
            dve.wait_ge(S["context"], 1)
            c.link(dve.reciprocal(ctx_r, ps_c[:, HID:HID + 1]))
            c.publish(dve.scalar_tensor_tensor(ctx_n, ps_c[:, 0:HID], ctx_r, blockm, ALU.mult, ALU.mult), S["context_n"], 1)
            c.done(1)
            c.straight()
            dve.wait_ge(S["context_t"], 1)
            c.publish(dve.tensor_copy(ctx_t, ps_m[:, 0:P]), S["context_t_kept"], 1)
            dve.wait_ge(S["wc_done"], 1)
            c.publish(dve.tensor_copy(wc, ps_m[:, 0:D]), S["wc_kept"], 1)

            def q_tile(i, u):
                t = i * 2 + u
                if not isinstance(i, int) or i > 0:
                    dve.wait_ge(S["q_t"], t - 1)
                sums = qsum[:, bass.ds(t * MH, MH)].unsqueeze(2).broadcast_to([P, MH, MD])
                dve.tensor_tensor(qs[:, u, :].rearrange("p (h d) -> p h d", h=MH),
                                  qkv[:, bass.ds(t, 1), 0:HID].rearrange("p a (h d) -> p (a h) d", h=MH), sums, ALU.mult).then_inc(S["q_scaled"], 1)

            def q_pair(i):
                q_tile(i, 0)
                q_tile(i, 1)

            first_then_rest(dve, NT // 2, q_pair)
            q_tile(NT // 2, 0)
            dve.wait_ge(S["mix_sigma"], 1)
            c.link(dve.tensor_scalar(n2, n2, 1e-12, None, ALU.max))
            c.link(dve.reciprocal(n2, n2))
            c.done(1)
            with dve.Fori(0, NT) as t:
                c.turn(t, 2)
                y = qkv[:, bass.ds(t, 1), HID:HID + D].rearrange("p a c -> p (a c)")
                xt = X[:, bass.ds(t, 1), :].rearrange("p a c -> p (a c)")
                c.link(dve.scalar_tensor_tensor(y, y, n2[:, bass.ds(t, 1)], gout, ALU.mult, ALU.mult))
                c.link(dve.tensor_tensor(xt, xt, y, ALU.add))
            c.done(NT)

        @block.tensor
        def _(pe):
            def transposes(t, u):
                pe.wait_ge(S["normed"], t + 1)
                for k in range(KC):
                    ins = pe.transpose(ps_t[u][:, k, :], xn[:, u, k * P:(k + 1) * P], ident[:])
                ins.then_inc(S["transposed"], 1)

            def products(t, u):
                pe.wait_ge(S["xnt_ready"], t + 1)
                for k in range(KC):
                    pe.matmul(ps_g[u][:, 0:GW], xnt[:, u, k, :], w_all[:, k, 0:GW], start=(k == 0), stop=(k == KC - 1))
                for k in range(KC):
                    ins = pe.matmul(ps_q[u][:, 0:QW], xnt[:, u, k, :], w_all[:, k, GW:GW + QW], start=(k == 0), stop=(k == KC - 1))
                ins.then_inc(S["projected"], 1)

            def tile(i, u):
                t = i * 2 + u
                if not isinstance(i, int) or i > 0:
                    pe.wait_ge(S["heads_kept"], t - 1)
                    pe.wait_ge(S["qkv_kept"], t - 1)
                transposes(t, u)
                products(t, u)

            def pair(i):
                tile(i, 0)
                tile(i, 1)

            first_then_rest(pe, NT // 2, pair)
            tile(NT // 2, 0)
            pe.wait_ge(S["k_column"], 1)
            pe.transpose(ps_m[:, 0:P], kcol, ident[:]).then_inc(S["k_column_t"], 1)
            pe.wait_ge(S["k_diag"], 1)
            pe.matmul(ps_m[:, P:2 * P], ones[:], kdiag, start=True, stop=True).then_inc(S["k_row"], 1)
            pe.wait_ge(S["mem_ready"], 1)
            pe.transpose(ps_m[0:MM, 256:256 + P], mem_e, ident[:])
            pe.transpose(ps_m[0:MM, 384:384 + P], mem_v, ident[:]).then_inc(S["mem_t"], 1)
            pe.wait_ge(S["mem_t_kept"], 1)
            pe.matmul(ps_c[:, 0:HID + 1], memkt[0:MM, :], memvt[0:MM, :], start=True, stop=False)

            def context(i, u):
                t = i * 2 + u
                pe.wait_ge(S["k_exp"], t + 1)
                pe.matmul(ps_c[:, 0:HID + 1], ktile[:, u, :], qkv[:, bass.ds(t, 1), 2 * HID:3 * HID + 1].rearrange("p a c -> p (a c)"),
                          start=False, stop=isinstance(i, int) and t == NT - 1).then_inc(S["k_used"], 1)

            with pe.Fori(0, NT // 2) as i:
                context(i, 0)
                context(i, 1)
            context(NT // 2, 0)
            pe.wait_ge(S["k_used"], NT)
            pe.nop().then_inc(S["context"], 1)
            pe.wait_ge(S["context_n"], 1)
            pe.transpose(ps_m[:, 0:P], ctx_n, ident[:]).then_inc(S["context_t"], 1)
            pe.wait_ge(S["context_t_kept"], 1)
            pe.matmul(ps_m[:, 0:D], ctx_t, wout, start=True, stop=True).then_inc(S["wc_done"], 1)
            pe.wait_ge(S["wc_kept"], 1)

            def mix_tile(i, u):
                t = i * 2 + u
                if not isinstance(i, int) or i > 0:
                    pe.wait_ge(S["q_t_kept"], t - 1)
                    pe.wait_ge(S["mix_kept"], t - 1)
                pe.wait_ge(S["q_scaled"], t + 1)
                pe.transpose(ps_t[u][:, 0, :], qs[:, u, :], ident[:]).then_inc(S["q_t"], 1)
                pe.wait_ge(S["q_t_kept"], t + 1)
                pe.matmul(ps_g[u][:, 0:D], qt[:, u, :], wc, start=True, stop=False)
                pe.matmul(ps_g[u][:, 0:D], ones[0:1, :], bout[0:1, :], start=False, stop=True).then_inc(S["mixed"], 1)

            def mix_pair(i):
                mix_tile(i, 0)
                mix_tile(i, 1)

            first_then_rest(pe, NT // 2, mix_pair)
            mix_tile(NT // 2, 0)


def attention(nc, v):
    P, N, D, NT, HEADS, HD, HP, G, GT, NG, UN, TURNS, COLBITS, TW, BIG, FAR = (v[k] for k in (
        "P", "N", "D", "NT", "HEADS", "HD", "HP", "G", "GT", "NG", "UN", "TURNS", "COLBITS", "TW", "BIG", "FAR"))
    X, ident, identb, iota_row, iota_i, iota_p, ones, hl, block_of, acc = (v[k] for k in (
        "X", "ident", "identb", "iota_row", "iota_i", "iota_p", "ones", "hl", "block_of", "acc"))
    sem, sb, pb, slots, table, waits_passed = v["sem"], v["sb"], v["pb"], v["slots"], v["table"], v["waits_passed"]
    TILES = UN * GT
    VT = GT // 2
    MAIN = TURNS // 16 * 16

    with ExitStack() as s:
        rank_t = sb(s, "rank_t", [TURNS, UN * G], BF16)
        columns = sb(s, "columns", [P, TURNS, TILES], I32)
        maxima = sb(s, "maxima", [P, NT, HEADS])
        left_parts = sb(s, "left_parts", [P, NT, 3, HEADS], BF16)
        pick = sb(s, "pick", [3 * HEADS, HEADS, P], BF16)

        with ExitStack() as s2:
            packed = sb(s2, "packed", [TURNS, UN * G], I32)
            packed_f = sb(s2, "packed_f", [TURNS, UN * G])
            shifted = sb(s2, "shifted", [TURNS, UN * G], I32)
            flat = sb(s2, "flat", [P, TURNS, TILES], I32)
            head_no = sb(s2, "head_no", [3 * HEADS, HEADS, P])
            part_i = sb(s2, "part_i", [P, 1], I32)
            part_f = sb(s2, "part_f", [P, 1])
            left_rest = sb(s2, "left_rest", [P, NT, HEADS])
            ps = [pb(s2, f"ps_slots{i}", [P, 512]) for i in range(UN)]
            loaded, ready, turned, chain, made = (sem(n) for n in ("slots_loaded", "packed_ready", "slots_turned", "slot_chain", "head_numbers"))
            block = s2.enter_context(nc.Block())

            @block.sync
            def _(sp):
                view = slots.rearrange("(i c) o -> i (c o)", i=TURNS)
                sp.dma_start(packed[0:MAIN, :], view[0:MAIN, :]).then_inc(loaded, 16)
                sp.dma_start(packed[MAIN:TURNS, :], view[MAIN:TURNS, :]).then_inc(loaded, 16)

            @block.gpsimd
            def _(pool):
                pool.iota(head_no[:], pattern=[[1, HEADS], [0, P]], base=0, channel_multiplier=0, allow_small_or_imprecise_dtypes=True).then_inc(made, 1)
                pool.memset(maxima[:], -BIG)
                pool.memset(acc[:], 0.0).then_inc(made, 1)

            @block.vector
            def _(dve):
                c = Chain(dve, chain)
                c.straight()
                c.link(dve.tensor_single_scalar(part_i[:], iota_i[:], HEADS - 1, ALU.bitwise_and))
                c.link(dve.tensor_copy(part_f[:], part_i[:]))
                dve.wait_ge(made, 1)
                c.link(dve.tensor_scalar(pick[:], head_no[:], part_f[0:3 * HEADS, :], None, ALU.is_equal))
                c.link(dve.tensor_copy(left_parts[:, :, 0, :], hl[:]))
                c.link(dve.tensor_tensor(left_rest[:], hl[:], left_parts[:, :, 0, :], ALU.subtract))
                c.link(dve.tensor_copy(left_parts[:, :, 1, :], left_rest[:]))
                c.link(dve.tensor_tensor(left_parts[:, :, 2, :], left_rest[:], left_parts[:, :, 1, :], ALU.subtract))
                dve.wait_ge(loaded, 32)
                dve.tensor_copy(packed_f[:], packed[:]).then_inc(ready, 1)
                c.link(dve.tensor_single_scalar(shifted[:], packed[:], COLBITS, ALU.logical_shift_right))
                c.link(dve.tensor_copy(rank_t[:], shifted[:]))
                for u in range(UN):
                    dve.wait_ge(turned, u + 1)
                    c.link(dve.tensor_copy(flat[:, :, u * GT:(u + 1) * GT].rearrange("p i k -> p k i"),
                                           ps[u][:, 0:GT * TURNS].rearrange("p (k i) -> p k i", k=GT)))
                c.link(dve.tensor_single_scalar(columns[:], flat[:], (1 << COLBITS) - 1, ALU.bitwise_and))
                c.done(1)

            @block.tensor
            def _(pe):
                pe.wait_ge(ready, 1)
                for u in range(UN):
                    for k in range(GT):
                        ins = pe.transpose(ps[u][:, k * TURNS:(k + 1) * TURNS], packed_f[:, (u * GT + k) * P:(u * GT + k + 1) * P],
                                           ident[0:TURNS, 0:TURNS])
                    ins.then_inc(turned, 1)

        with ExitStack() as s2:
            indices = sb(s2, "indices", [P, UN, GT], I32)
            rows = sb(s2, "rows", [P, UN, GT, TW])
            far = sb(s2, "far", [P, 2, G], BF16)
            in_row_t = sb(s2, "in_row_t", [P, 2, G], BF16)
            in_row = sb(s2, "in_row", [P, 3, GT, P])
            logits_t = sb(s2, "logits_t", [3 * HEADS, 2, G], BF16)
            masked = sb(s2, "masked", [P, HEADS, G], BF16)
            largest = sb(s2, "largest", [P, HEADS])
            bound = sb(s2, "bound", [P, HEADS])
            new_max = sb(s2, "new_max", [P, 2, HEADS])
            row_side = sb(s2, "row_side", [P, 2, 3, 2, HEADS], BF16)
            delta = sb(s2, "delta", [P, 3, HEADS])
            scale = sb(s2, "scale", [P, 3, HEADS])
            logit = sb(s2, "logit", [P, GT, HEADS])
            far_off = sb(s2, "far_off", [P, 1])
            ps_pick = pb(s2, "ps_pick", [P, HEADS, G])
            ps_rank = pb(s2, "ps_rank", [P, G])
            ps_sum = pb(s2, "ps_sum", [P, 512])
            ps_turned = pb(s2, "ps_turned", [P, 2 * G], BF16)
            ps_row_side = pb(s2, "ps_row_side", [P, 512])
            ps_lt, ps_in_row, ps_edge = ps_turned[0:3 * HEADS, 0:G], ps_turned[:, G:2 * G], ps_row_side[:, 0:GT * 2 * HEADS]
            names = ([f"indices_staged{u}" for u in range(UN)] + [f"gathered{u}" for u in range(UN)] +
                     ["far_off_made", "rank_broadcast", "far_made", "in_row_t_made", "in_row_turned", "in_row_kept",
                      "logits_turned", "logits_t_kept", "picked", "largest_found", "edge_chain", "row_chain", "maximum_chain", "finish_chain", "row_side_made", "delta_made",
                      "scale_made", "edge_side_done", "logit_made", "exp_made", "messages_made", "last_messages_made", "parts_cleared", "summed", "acc_scaled", "acc_added"])
            S = {n: sem(n) for n in names}
            block = s2.enter_context(nc.Block())

            def wait(engine, name, value):
                if not isinstance(value, int) or value > 0:
                    engine.wait_ge(S[name], value)

            def turns(engine, step, ahead):
                def turn(i):
                    for u in range(UN):
                        step(i, u)
                for u in range(-ahead, 0):
                    step(0, u)
                turn(0)
                with engine.Fori(1, TURNS - 1) as i:
                    turn(i)
                turn(TURNS - 1)

            def exists(g):
                return not isinstance(g, int) or 0 <= g < NG

            def later(i, u, n):
                return i + (u + n) // UN, (u + n) % UN

            @block.sync
            def _(sp):
                def step(i, u):
                    wait(sp, f"gathered{u}", i * 16 * GT)
                    sp.sem_inc(waits_passed, 1)
                    sp.dma_start(indices[:, u, :], columns[:, bass.ds(i, 1), u * GT:(u + 1) * GT].rearrange("p a k -> p (a k)")).then_inc(S[f"indices_staged{u}"], 16)
                turns(sp, step, 0)

            @block.gpsimd
            def _(pool):
                def step(i, u):
                    wait(pool, f"indices_staged{u}", i * 16 + 16)
                    wait(pool, "summed", (i - 1) * UN + u + 1)
                    pool.sem_inc(waits_passed, 1)
                    for k in range(GT):
                        pool.indirect_dma_start(rows[:, u, k, :], None, table, bass.IndirectOffsetOnAxis(indices[:, u, k:k + 1], 0)).then_inc(S[f"gathered{u}"], 16)
                turns(pool, step, 0)

            @block.scalar
            def _(act):
                def keep_logits(g, u):
                    wait(act, "logits_turned", g + 1)
                    wait(act, "picked", (g - 1) * HEADS)
                    act.activation(logits_t[:, u % 2, :], ps_lt, ACT.Copy).then_inc(S["logits_t_kept"], 1)

                def keep_in_row(g, u):
                    wait(act, "in_row_turned", g + 1)
                    wait(act, "summed", g - 2)
                    act.activation(in_row[:, u % 3, :, :].rearrange("p k r -> p (k r)"), ps_in_row, ACT.Copy).then_inc(S["in_row_kept"], 1)

                def row_masks(g, u):
                    wait(act, "rank_broadcast", g + 1)
                    wait(act, "largest_found", (g - 1) * HEADS)
                    act.activation(far[:, u % 2, :], ps_rank[:], ACT.Abs, bias=far_off[:], scale=FAR).then_inc(S["far_made"], 1)
                    wait(act, "far_made", g + 1)
                    wait(act, "edge_side_done", g - 1)
                    act.activation(in_row_t[:, u % 2, :], far[:, u % 2, :], ACT.Relu, bias=1.0, scale=-1.0).then_inc(S["in_row_t_made"], 1)

                act.wait_ge(S["far_off_made"], 1)

                def step(i, u):
                    g = i * UN + u
                    if exists(g):
                        wait(act, "logit_made", g + 1)
                        heads = rows[:, u, :, 0:HEADS * HP].rearrange("p k (h c) -> p k h c", h=HEADS)
                        act.activation(heads[:, :, :, HD], logit[:], ACT.Exp).then_inc(S["exp_made"], 1)
                        wait(act, "exp_made", g + 1)
                        for k in range(VT, GT):
                            for h in range(HEADS):
                                act.activation(heads[:, k, h, 0:HD], heads[:, k, h, 0:HD], ACT.Copy,
                                               scale=heads[:, k, h, HD:HP]).then_inc(S["last_messages_made"], 1)
                    if exists(g):
                        wait(act, "delta_made", g + 1)
                        wait(act, "acc_scaled", g - 2)
                        act.activation(scale[:, u % 3, :], delta[:, u % 3, :], ACT.Exp).then_inc(S["scale_made"], 1)
                    if exists(g + 3):
                        keep_logits(g + 3, u + 3)
                    if exists(g + 2):
                        keep_in_row(g + 2, u + 2)
                    if exists(g + 3):
                        row_masks(g + 3, u + 3)
                turns(act, step, 3)

            @block.vector
            def _(dve):
                e = Chain(dve, S["edge_chain"])
                r = Chain(dve, S["row_chain"])
                m = Chain(dve, S["maximum_chain"])
                dve.memset(row_side[:], 0.0).then_inc(S["parts_cleared"], 1)
                dve.wait_ge(S["parts_cleared"], 1)
                dve.tensor_scalar(far_off[:], iota_p[:], -FAR, None, ALU.mult).then_inc(S["far_off_made"], 1)

                def largest_of(g, u, h):
                    wait(dve, "picked", g * HEADS + h + 1)
                    if h == 0:
                        wait(dve, "far_made", g + 1)
                    dve.sem_inc(waits_passed, 1)
                    dve.tensor_tensor_reduce(masked[:, h, :], ps_pick[:, h, :], far[:, u % 2, :], 1.0, -BIG, ALU.subtract, ALU.max,
                                             largest[:, h:h + 1]).then_inc(S["largest_found"], 1)

                def copy_left(g, u, b):
                    parts = left_parts[:, bass.ds(b, 1), :, :].rearrange("p a t h -> p (a t) h")
                    wait(dve, "edge_side_done", g - 1)
                    dve.tensor_scalar(row_side[:, u % 2, :, 0, :], parts, 1.0, None, ALU.mult)

                def row_steps(g, u, b):
                    left = hl[:, bass.ds(b, 1), :].rearrange("p a h -> p (a h)")
                    so_far = maxima[:, bass.ds(b, 1), :].rearrange("p a h -> p (a h)")
                    new, side = new_max[:, u % 2, :], row_side[:, u % 2]
                    r.turn(g, 4)
                    wait(dve, "largest_found", (g + 1) * HEADS)
                    n = r.tick(dve.tensor_tensor(bound[:], largest[:], left, ALU.add))
                    yield
                    r.need(n)
                    n = r.tick(dve.scalar_tensor_tensor(bound[:], bound[:], 0.2, bound[:], ALU.mult, ALU.max))
                    yield
                    r.need(n)
                    n = r.tick(dve.tensor_tensor(new, bound[:], so_far, ALU.max))
                    yield
                    r.need(n)
                    n = r.tick(dve.tensor_copy(side[:, 0, 1, :], new))
                    yield
                    r.need(n)
                    dve.tensor_tensor(side[:, 1, 1, :], new, side[:, 0, 1, :], ALU.subtract).then_inc(S["row_side_made"], 1)
                    yield

                def maximum_steps(g, u, b):
                    so_far = maxima[:, bass.ds(b, 1), :].rearrange("p a h -> p (a h)")
                    new, side = new_max[:, u % 2, :], row_side[:, u % 2]
                    m.turn(g, 2)
                    wait(dve, "row_side_made", g + 1)
                    n = m.tick(dve.tensor_tensor(new, side[:, 0, 1, :], side[:, 1, 1, :], ALU.add))
                    yield
                    m.need(n)
                    wait(dve, "scale_made", g - 2)
                    dve.tensor_tensor(delta[:, u % 3, :], so_far, new, ALU.subtract).then_inc(S["delta_made"], 1)
                    yield
                    wait(dve, "delta_made", g + 1)
                    m.tick(dve.tensor_scalar(so_far, new, 1.0, None, ALU.mult))
                    yield

                def edge_steps(g, u):
                    heads = rows[:, u, :, 0:HEADS * HP].rearrange("p k (h c) -> p k h c", h=HEADS)
                    edge_side = ps_edge.rearrange("p (k v h) -> p k v h", k=GT, v=2)
                    e.turn(g, 2)
                    wait(dve, "edge_side_done", g + 1)
                    wait(dve, "exp_made", g)
                    n = e.tick(dve.tensor_tensor(logit[:], heads[:, :, :, HD], edge_side[:, :, 0, :], ALU.add))
                    yield
                    e.need(n)
                    n = e.tick(dve.scalar_tensor_tensor(logit[:], logit[:], 0.2, logit[:], ALU.mult, ALU.max))
                    yield
                    e.need(n)
                    dve.tensor_tensor(logit[:], logit[:], edge_side[:, :, 1, :], ALU.subtract).then_inc(S["logit_made"], 1)
                    yield

                def messages(g, u):
                    heads = rows[:, u, :, 0:HEADS * HP].rearrange("p k (h c) -> p k h c", h=HEADS)
                    wait(dve, "exp_made", g + 1)
                    dve.tensor_tensor(heads[:, 0:VT, :, 0:HD], heads[:, 0:VT, :, 0:HD],
                                      heads[:, 0:VT, :, HD:HP].broadcast_to([P, VT, HEADS, HD]), ALU.mult).then_inc(S["messages_made"], 1)

                def scale_sums(g, u, b):
                    a4 = acc[:, bass.ds(b, 1), :].rearrange("p a (h c) -> p (a h) c", h=HEADS)
                    wait(dve, "scale_made", g + 1)
                    wait(dve, "acc_added", g)
                    dve.tensor_tensor(a4, a4, scale[:, u % 3, :].unsqueeze(2).broadcast_to([P, HEADS, HP]), ALU.mult).then_inc(S["acc_scaled"], 1)

                def add_sums(g, u, b):
                    a = acc[:, bass.ds(b, 1), :].rearrange("p a c -> p (a c)")
                    wait(dve, "acc_scaled", g + 1)
                    wait(dve, "summed", g + 1)
                    dve.tensor_tensor(a, a, ps_sum[:, 0:HEADS * HP], ALU.add).then_inc(S["acc_added"], 1)

                def block_number(g):
                    return dve.value_load(block_of[0:1, bass.ds(g, 1)], min_val=0, max_val=NT - 1)

                blocks = {n: block_number(n) for n in range(2)}
                passed = [dve.alloc_register(f"passed_block{n}") for n in (-1, 0, 1)]

                def step(i, u):
                    g = i * UN + u
                    if u == 0 and (not isinstance(g, int) or g > 0):
                        for n in (-1, 0, 1):
                            blocks[n] = dve.snap(passed[n + 1], min_val=0, max_val=NT - 1)
                    none = iter(())
                    edges = edge_steps(g, u) if exists(g) else none
                    maxima_of = maximum_steps(g, u, blocks[u]) if exists(g) else none
                    rows_of = row_steps(g + 1, u + 1, blocks[u + 1]) if exists(g + 1) else none
                    for h in range(HEADS):
                        if exists(g + 1):
                            largest_of(g + 1, u + 1, h)
                        next(edges, None)
                        next(maxima_of, None)
                    if exists(g - 1):
                        scale_sums(g - 1, u - 1, blocks[u - 1])
                    next(rows_of, None)
                    if exists(g - 1):
                        add_sums(g - 1, u - 1, blocks[u - 1])
                    next(rows_of, None)
                    if exists(g + 1):
                        copy_left(g + 1, u + 1, blocks[u + 1])
                    next(rows_of, None)
                    if exists(g):
                        messages(g, u)
                        if exists(g + 2):
                            blocks[u + 2] = block_number(g + 2)
                    next(rows_of, None)
                    next(rows_of, None)
                    if u == UN - 1:
                        for n in (-1, 0, 1):
                            if exists(g + 1 + n):
                                dve.reg_mov(passed[n + 1], blocks[UN + n])
                turns(dve, step, 1)
                scale_sums(NG - 1, UN - 1, blocks[UN - 1])
                add_sums(NG - 1, UN - 1, blocks[UN - 1])
                wait(dve, "acc_added", NG)
                c = Chain(dve, S["finish_chain"])
                c.straight()
                den = maxima[:]
                a4 = acc[:, :, :].rearrange("p t (h c) -> p t h c", h=HEADS)
                c.link(dve.tensor_scalar(den, a4[:, :, :, HD], 1e-16, None, ALU.add))
                c.link(dve.reciprocal(den, den))
                c.link(dve.tensor_tensor(a4[:, :, :, 0:HD], a4[:, :, :, 0:HD], den.unsqueeze(3).broadcast_to([P, NT, HEADS, HD]), ALU.mult))
                x4 = X[:, :, :].rearrange("p t (h c) -> p t h c", h=HEADS)
                c.link(dve.tensor_tensor(x4, x4, a4[:, :, :, 0:HD], ALU.add))

            @block.tensor
            def _(pe):
                def broadcast_rank(i, u):
                    wait(pe, "far_made", i * UN + u)
                    pe.matmul(ps_rank[:], identb[0:TURNS, bass.ds(i, 1)].broadcast_to([TURNS, P]), rank_t[:, u * G:(u + 1) * G],
                              start=True, stop=True).then_inc(S["rank_broadcast"], 1)

                def turn_logits(i, u):
                    g = i * UN + u
                    wait(pe, f"gathered{u}", i * 16 * GT + 16 * GT)
                    wait(pe, "logits_t_kept", g)
                    wait(pe, "in_row_kept", g - 1)
                    for k in range(GT):
                        ins = pe.transpose(ps_lt[:, k * P:(k + 1) * P], rows[:, u, k, HEADS * HP:TW].bitcast(BF16), identb[:])
                    ins.then_inc(S["logits_turned"], 1)

                def turn_in_row(g, u):
                    wait(pe, "in_row_t_made", g + 1)
                    wait(pe, "in_row_kept", g)
                    wait(pe, "logits_t_kept", g + 1)
                    for k in range(GT):
                        ins = pe.transpose(ps_in_row[:, k * P:(k + 1) * P], in_row_t[:, u % 2, k * P:(k + 1) * P], identb[:])
                    ins.then_inc(S["in_row_turned"], 1)

                def pick_logits(g, u):
                    wait(pe, "logits_t_kept", g + 1)
                    for h in range(HEADS):
                        wait(pe, "largest_found", (g - 1) * HEADS + h + 1)
                        pe.matmul(ps_pick[:, h, :], pick[:, h, :], logits_t[:, u % 2, :], start=True, stop=True).then_inc(S["picked"], 1)

                def row_to_edge(g, u):
                    wait(pe, "row_side_made", g + 1)
                    wait(pe, "in_row_t_made", g + 1)
                    wait(pe, "logit_made", g)
                    for k in range(GT):
                        for t in range(3):
                            ins = pe.matmul(ps_edge[:, k * 2 * HEADS:(k + 1) * 2 * HEADS], in_row_t[:, u % 2, k * P:(k + 1) * P],
                                            row_side[:, u % 2, t].rearrange("p v h -> p (v h)"), start=(t == 0), stop=(t == 2))
                    ins.then_inc(S["edge_side_done"], 1)

                def sum_rows(g, u):
                    wait(pe, "messages_made", g + 1)
                    wait(pe, "in_row_kept", g + 1)
                    wait(pe, "last_messages_made", (g + 1) * HEADS * (GT - VT))
                    wait(pe, "acc_added", g)
                    for k in range(GT):
                        ins = pe.matmul(ps_sum[:, 0:HEADS * HP], in_row[:, u % 3, k, :], rows[:, u, k, 0:HEADS * HP],
                                        start=(k == 0), stop=(k == GT - 1))
                    ins.then_inc(S["summed"], 1)

                def step(i, u):
                    g = i * UN + u
                    if exists(g + 2):
                        pick_logits(g + 2, u + 2)
                    if exists(g + 2):
                        turn_in_row(g + 2, u + 2)
                    if exists(g + 3):
                        turn_logits(*later(i, u, 3))
                        broadcast_rank(*later(i, u, 3))
                    if exists(g + 1):
                        row_to_edge(g + 1, u + 1)
                    if exists(g):
                        sum_rows(g, u)
                turns(pe, step, 3)


def experts(nc, v):
    P, N, D, NT, LAST, KC, NE, FH, FC, LN_EPS = (v[k] for k in ("P", "N", "D", "NT", "LAST", "KC", "NE", "FH", "FC", "LN_EPS"))
    X, ident, identb, iota_row, iota_i, iota_p, ones, acc = (v[k] for k in ("X", "ident", "identb", "iota_row", "iota_i", "iota_p", "ones", "acc"))
    sem, sb, pb, waits_passed = v["sem"], v["sb"], v["pb"], v["waits_passed"]
    w1, w2, wr, br, b1, b2, ln_g, ln_b, out = (v[k] for k in ("w1", "w2", "wr", "br", "b1", "b2", "ln_g", "ln_b", "out"))
    SG = 256
    ST = SG // P
    EG = (2 * NT * P + NE * (SG - 1)) // SG
    EG += EG % 2
    in_slots = nc.dram_tensor("in_slots", [EG * SG, D], FP32).ap()
    out_slots = nc.dram_tensor("out_slots", [EG * SG, D], FP32).ap()

    with ExitStack() as s:
        mean1, rstd1, mean2, rstd2 = (sb(s, n, [P, NT]) for n in ("mean1", "rstd1", "mean2", "rstd2"))
        slot_of = sb(s, "slot_of", [P, NT, 2])
        weight = sb(s, "weight", [P, NT, 2])
        expert_of = sb(s, "expert_of", [1, EG], I32)
        gains = sb(s, "gains", [P, 2, NE * KC])
        b1t = sb(s, "b1t", [P, NE * FC])
        b2_all = sb(s, "b2_all", [P, NE * D])

        with ExitStack() as s2:
            stats = sb(s2, "f_stats", [P, NT, 6])
            tmp, sig = (sb(s2, n, [P, NT]) for n in ("f_tmp", "f_sig"))
            u_tile = sb(s2, "u_tile", [P, 2, D])
            ut = sb(s2, "ut", [P, 2, KC, P])
            wr_sb = sb(s2, "wr_sb", [P, KC, NE])
            br_sb = sb(s2, "br_sb", [1, NE])
            prob, sel, sel2, rest, pos = (sb(s2, n, [P, NT, NE]) for n in ("prob", "sel", "sel2", "rest", "pos"))
            red = sb(s2, "red", [P, NT])
            order = sb(s2, "order", [P, NE])
            tri = sb(s2, "f_tri", [P, P])
            count, before, start, groups_f = (sb(s2, n, [P, NE]) for n in ("f_count", "f_before", "f_start", "f_groups"))
            zero8 = sb(s2, "zero8", [P, NE])
            groups_i = sb(s2, "f_groups_i", [P, NE], I32)
            reached = sb(s2, "f_reached", [1, EG, NE])
            gno = sb(s2, "gno", [1, EG, NE])
            expert_f = sb(s2, "expert_f", [1, EG])
            zero = sb(s2, "zero", [P, 14, D])
            gb_rows = sb(s2, "gb_rows", [NE * KC, 2, P])
            b1_rows = sb(s2, "b1_rows", [NE * FC, P])
            ps_u = [pb(s2, f"ps_u{i}", [P, 512]) for i in range(2)]
            ps_l = [pb(s2, f"ps_l{i}", [P, 512]) for i in range(2)]
            ps_w = pb(s2, "ps_w", [P, 512])
            ps_s = pb(s2, "ps_s", [P, 512])
            names = ("f_loaded", "zeroed", "slots_cleared", "f_chain", "f_moments", "f_sigma", "u_made", "u_turned", "ut_kept", "logits_done",
                     "logits_kept", "logits_shifted", "prob_made", "counted", "count_summed", "weights_turned")
            S = {n: sem(n) for n in names}
            block = s2.enter_context(nc.Block())
            FILL = 14 * P

            @block.sync
            def _(sp):
                ld = S["f_loaded"]
                sp.dma_start(wr_sb[:], wr.rearrange("(k p) e -> p k e", p=P)).then_inc(ld, 16)
                sp.dma_start(br_sb[:], br.rearrange("(a e) -> a e", a=1)).then_inc(ld, 16)
                sp.dma_start(b2_all[:], b2.rearrange("e c -> (e c)").rearrange("(a c) -> a c", a=1).broadcast_to([P, NE * D])).then_inc(ld, 16)
                sp.dma_start(gb_rows[:, 0, :], ln_g.rearrange("e (k p) -> (e k) p", p=P)).then_inc(ld, 16)
                sp.dma_start(gb_rows[:, 1, :], ln_b.rearrange("e (k p) -> (e k) p", p=P)).then_inc(ld, 16)
                sp.dma_start(b1_rows[:], b1.rearrange("e (k p) -> (e k) p", p=P)).then_inc(ld, 16)
                sp.wait_ge(S["zeroed"], 1)
                rows = in_slots.shape[0]
                assert rows % P == 0
                n = 0
                for r in range(0, rows, FILL):
                    m = min(FILL, rows - r)
                    sp.dma_start(in_slots[r:r + m, :].rearrange("(p t) c -> p t c", p=P), zero[:, 0:m // P, :]).then_inc(S["slots_cleared"], 16)
                    n += 16
                sp.wait_ge(S["slots_cleared"], n)

            @block.gpsimd
            def _(pool):
                pool.memset(zero[:], 0.0).then_inc(S["zeroed"], 1)
                pool.iota(order[:], pattern=[[-1, NE]], base=NE, channel_multiplier=0, allow_small_or_imprecise_dtypes=True).then_inc(S["zeroed"], 1)
                pool.iota(gno[:], pattern=[[1, EG], [0, NE]], base=0, channel_multiplier=0, allow_small_or_imprecise_dtypes=True).then_inc(S["zeroed"], 1)
                pool.memset(zero8[:], 0.0).then_inc(S["zeroed"], 1)

            @block.scalar
            def _(act):
                def sigma(n):
                    act.wait_ge(S["f_moments"], n)
                    act.activation(sig[:], tmp[:], ACT.Sqrt).then_inc(S["f_sigma"], 1)

                sigma(1)

                def tile(i, u):
                    t = i * 2 + u
                    act.wait_ge(S["u_turned"], t + 1)
                    if not isinstance(i, int) or i > 0:
                        act.wait_ge(S["logits_done"], t - 1)
                    act.activation(ut[:, u, :, :], ps_u[u][:, 0:D].rearrange("p (k c) -> p k c", k=KC), ACT.Copy).then_inc(S["ut_kept"], 1)

                def pair(i):
                    tile(i, 0)
                    tile(i, 1)

                first_then_rest(act, NT // 2, pair)
                tile(NT // 2, 0)
                sigma(2)
                act.wait_ge(S["logits_shifted"], 1)
                act.activation(prob[:], prob[:], ACT.Exp).then_inc(S["prob_made"], 1)

            @block.vector
            def _(dve):
                c = Chain(dve, S["f_chain"])

                def moments(mean, rstd, n):
                    c.link(dve.tensor_tensor(mean, stats[:, :, 1], stats[:, :, 4], ALU.add))
                    c.link(dve.tensor_tensor(rstd, stats[:, :, 1], stats[:, :, 4], ALU.subtract))
                    c.link(dve.tensor_tensor(tmp[:], stats[:, :, 2], stats[:, :, 5], ALU.add))
                    c.link(dve.tensor_scalar(mean, mean, 0.5, None, ALU.mult))
                    c.link(dve.scalar_tensor_tensor(rstd, rstd, 0.25, rstd, ALU.mult, ALU.mult))
                    c.link(dve.scalar_tensor_tensor(tmp[:], tmp[:], 1.0 / D, rstd, ALU.mult, ALU.add))
                    c.publish(dve.tensor_scalar(tmp[:], tmp[:], LN_EPS, None, ALU.add), S["f_moments"], n)
                    dve.wait_ge(S["f_sigma"], n)
                    c.link(dve.reciprocal(rstd, sig[:]))

                with dve.Fori(0, NT) as t:
                    c.turn(t, 1)
                    c.link(dve.bn_stats(stats[:, bass.ds(t, 1), :].rearrange("p a c -> p (a c)"), X[:, bass.ds(t, 1), :].rearrange("p a c -> p (a c)")))
                c.done(NT)
                c.straight()
                moments(mean1[:], rstd1[:], 1)
                c.link(dve.tensor_scalar(tri[:], iota_row[:], iota_p[:], None, ALU.is_gt))
                c.done(1)

                def keep_logits(t, u):
                    dve.wait_ge(S["logits_done"], t + 1)
                    dve.tensor_scalar(prob[:, bass.ds(t, 1), :].rearrange("p a c -> p (a c)"), ps_l[u][:, 0:NE], 1.0, None, ALU.mult).then_inc(S["logits_kept"], 1)

                def tile(i, u):
                    t = i * 2 + u
                    later = not isinstance(i, int) or i > 0
                    tt = bass.ds(t, 1)
                    if later:
                        dve.wait_ge(S["u_turned"], t - 1)
                    c.turn(t, 1)
                    c.publish(dve.tensor_scalar(u_tile[:, u, :], X[:, tt, :].rearrange("p a c -> p (a c)"), mean1[:, tt], rstd1[:, tt],
                                               ALU.subtract, ALU.mult), S["u_made"], t + 1)
                    c.link(dve.bn_stats(stats[:, tt, :].rearrange("p a c -> p (a c)"), u_tile[:, u, :]))
                    if later:
                        keep_logits(t - 2, u)

                def pair(i):
                    tile(i, 0)
                    tile(i, 1)

                first_then_rest(dve, NT // 2, pair)
                tile(NT // 2, 0)
                keep_logits(NT - 2, 1)
                keep_logits(NT - 1, 0)
                c.done(NT)
                dve.wait_ge(S["logits_kept"], NT)
                c.straight()
                moments(mean2[:], rstd2[:], 2)

                def each(a):
                    return a.unsqueeze(2).broadcast_to([P, NT, NE])

                orders = order[:].unsqueeze(1).broadcast_to([P, NT, NE])
                c.link(dve.tensor_reduce(red[:], prob[:], AX, ALU.max))
                c.publish(dve.tensor_tensor(prob[:], prob[:], each(red[:]), ALU.subtract), S["logits_shifted"], 1)
                dve.wait_ge(S["prob_made"], 1)
                dve.wait_ge(S["zeroed"], 4)

                def choose(values, chosen, top):
                    c.link(dve.tensor_reduce(top, values, AX, ALU.max))
                    c.link(dve.tensor_tensor(chosen, values, each(top), ALU.is_equal))
                    c.link(dve.tensor_tensor(chosen, chosen, orders, ALU.mult))
                    c.link(dve.tensor_reduce(red[:], chosen, AX, ALU.max))
                    c.link(dve.tensor_tensor(chosen, each(red[:]), orders, ALU.is_equal))

                choose(prob[:], sel[:], weight[:, :, 0])
                c.link(dve.scalar_tensor_tensor(rest[:], sel[:], -2.0, prob[:], ALU.mult, ALU.add))
                choose(rest[:], sel2[:], weight[:, :, 1])
                c.link(dve.tensor_tensor(red[:], weight[:, :, 0], weight[:, :, 1], ALU.add))
                c.link(dve.reciprocal(red[:], red[:]))
                c.link(dve.tensor_tensor(weight[:], weight[:], red[:].unsqueeze(2).broadcast_to([P, NT, 2]), ALU.mult))
                c.link(dve.tensor_tensor(rest[:], sel[:], sel2[:], ALU.add))
                c.publish(dve.tensor_reduce(count[:], rest[:].rearrange("p t e -> p e t"), AX, ALU.add), S["counted"], 1)
                dve.wait_ge(S["count_summed"], 1)
                c.link(dve.tensor_scalar(groups_i[:], ps_s[:, 16:16 + NE], float(SG - 1), None, ALU.add))
                c.link(dve.tensor_single_scalar(groups_i[:], groups_i[:], SG.bit_length() - 1, ALU.logical_shift_right))
                c.link(dve.tensor_copy(groups_f[:], groups_i[:]))
                c.link(dve.tensor_tensor_scan(start[:], groups_f[:], zero8[:], 0.0, ALU.add, ALU.add))
                c.link(dve.tensor_tensor(start[:], start[:], groups_f[:], ALU.subtract))
                c.link(dve.scalar_tensor_tensor(before[:], start[:], float(SG), ps_s[:, 0:NE], ALU.mult, ALU.add))
                for e in range(NE):
                    ins = dve.tensor_tensor_scan(pos[:, :, e], rest[:, :, e], rest[:, :, e], before[:, e:e + 1], ALU.add, ALU.max)
                c.link(ins)
                for n, chosen in enumerate((sel, sel2)):
                    c.link(dve.tensor_tensor(chosen[:], chosen[:], pos[:], ALU.mult))
                    c.link(dve.tensor_reduce(slot_of[:, :, n], chosen[:], AX, ALU.add))
                c.link(dve.tensor_scalar(slot_of[:], slot_of[:], -1.0, None, ALU.add))
                c.link(dve.tensor_tensor(reached[:], gno[:], start[0:1, :].unsqueeze(1).broadcast_to([1, EG, NE]), ALU.is_ge))
                c.link(dve.tensor_reduce(expert_f[:], reached[:], AX, ALU.add))
                c.link(dve.tensor_scalar(expert_of[:], expert_f[:], -1.0, None, ALU.add))
                dve.wait_ge(S["weights_turned"], 1)
                dve.tensor_copy(gains[:].rearrange("p a c -> p (a c)"), ps_w[:, 0:2 * NE * KC])
                c.link(dve.tensor_copy(b1t[:], ps_w[:, 128:128 + NE * FC]))
                c.done(1)

            @block.tensor
            def _(pe):
                pe.wait_ge(S["f_loaded"], 96)
                for n in range(2):
                    pe.transpose(ps_w[:, n * NE * KC:(n + 1) * NE * KC], gb_rows[:, n, :], ident[0:NE * KC, 0:NE * KC])
                pe.transpose(ps_w[:, 128:128 + NE * FC], b1_rows[:], ident[0:NE * FC, 0:NE * FC]).then_inc(S["weights_turned"], 1)

                def tile(i, u):
                    t = i * 2 + u
                    pe.wait_ge(S["u_made"], t + 1)
                    if not isinstance(i, int) or i > 0:
                        pe.wait_ge(S["ut_kept"], t - 1)
                    for k in range(KC):
                        ins = pe.transpose(ps_u[u][:, k * P:(k + 1) * P], u_tile[:, u, k * P:(k + 1) * P], ident[:])
                    ins.then_inc(S["u_turned"], 1)
                    if u > 0 or not isinstance(i, int) or i > 0:
                        products(t - 1, 1 - u)

                def products(t, u):
                    pe.wait_ge(S["ut_kept"], t + 1)
                    if not isinstance(t, int) or t > 1:
                        pe.wait_ge(S["logits_kept"], t - 1)
                    for k in range(KC):
                        pe.matmul(ps_l[u][:, 0:NE], ut[:, u, k, :], wr_sb[:, k, :], start=(k == 0), stop=False)
                    pe.matmul(ps_l[u][:, 0:NE], ones[0:1, :], br_sb[:], start=False, stop=True).then_inc(S["logits_done"], 1)

                def pair(i):
                    tile(i, 0)
                    tile(i, 1)

                first_then_rest(pe, NT // 2, pair)
                tile(NT // 2, 0)
                products(NT - 1, 0)
                pe.wait_ge(S["counted"], 1)
                pe.matmul(ps_s[:, 0:NE], tri[:], count[:], start=True, stop=True)
                pe.matmul(ps_s[:, 16:16 + NE], ones[:], count[:], start=True, stop=True).then_inc(S["count_summed"], 1)

        with ExitStack() as s2:
            u_tile = sb(s2, "d_u", [P, 2, D])
            v_tile = sb(s2, "d_v", [P, 2, D])
            slot_tile = sb(s2, "d_slot", [P, 2, 2], I32)
            S = {n: sem(n) for n in ("d_normed", "d_ready", "dispatched0", "dispatched1")}
            block = s2.enter_context(nc.Block())

            @block.vector
            def _(dve):
                def tile(i, u):
                    t = i * 2 + u
                    tt = bass.ds(t, 1)
                    if not isinstance(i, int) or i > 0:
                        dve.wait_ge(S["d_ready"], t - 1)
                    dve.tensor_scalar(u_tile[:, u, :], X[:, tt, :].rearrange("p a c -> p (a c)"), mean1[:, tt], rstd1[:, tt],
                                      ALU.subtract, ALU.mult).then_inc(S["d_normed"], 1)
                    if not isinstance(i, int) or i > 0:
                        dve.wait_ge(S[f"dispatched{u}"], i * 32)
                    dve.tensor_scalar(slot_tile[:, u, :], slot_of[:, tt, :].rearrange("p a c -> p (a c)"), 1.0, None, ALU.mult)
                    dve.wait_ge(S["d_normed"], t + 1)
                    dve.tensor_scalar(v_tile[:, u, :], u_tile[:, u, :], mean2[:, tt], rstd2[:, tt], ALU.subtract, ALU.mult).then_inc(S["d_ready"], 1)

                def pair(i):
                    tile(i, 0)
                    tile(i, 1)

                first_then_rest(dve, NT // 2, pair)
                tile(NT // 2, 0)

            @block.gpsimd
            def _(pool):
                def tile(i, u):
                    pool.wait_ge(S["d_ready"], i * 2 + u + 1)
                    pool.sem_inc(waits_passed, 1)
                    for n in range(2):
                        pool.indirect_dma_start(in_slots, bass.IndirectOffsetOnAxis(slot_tile[:, u, n:n + 1], 0), v_tile[:, u, :],
                                                None).then_inc(S[f"dispatched{u}"], 16)

                with pool.Fori(0, NT // 2) as i:
                    tile(i, 0)
                    tile(i, 1)
                tile(NT // 2, 0)
                pool.wait_ge(S["dispatched0"], 32 * ((NT + 1) // 2))
                pool.wait_ge(S["dispatched1"], 32 * (NT // 2))

        with ExitStack() as s2:
            work = acc[:, :, :].rearrange("p t c -> p (t c)")
            taken = [0]

            def carve(shape, names, **sizes):
                width = 1
                for n in shape:
                    width *= n
                view = work[:, taken[0]:taken[0] + width]
                taken[0] += width
                return view.rearrange(f"p ({names}) -> p {names}", **sizes)

            w1_full = carve([KC, FH], "k f", k=KC)
            w2_full = carve([2, FC, D], "u f c", u=2, f=FC)
            hid_full = carve([FC, SG], "f t", f=FC)
            xt_full = carve([KC, SG], "k t", k=KC)
            slot_in = carve([2, ST, D], "u j c", u=2, j=ST)
            slot_out = carve([2, ST, D], "u j c", u=2, j=ST)
            hid = sb(s2, "hid", [P, 2, FC, SG], FP32R)
            w1_parts = sb(s2, "w1_parts", [P, 2, 2, KC, FH], FP32R)
            w2_parts = sb(s2, "w2_parts", [P, 2, 2, FC, D], FP32R)
            xt = sb(s2, "xt", [P, 2, 2, KC, SG], FP32R)
            PASSES = ((0, 0), (0, 1), (1, 0))
            PF = FC // 2
            HB = 4
            ps_x = [pb(s2, f"ps_x{i}", [P, KC, SG]) for i in range(2)]
            ps_h = [pb(s2, f"ps_h{i}", [P, 512]) for i in range(HB)]
            ps_y = [pb(s2, f"ps_y{i}", [P, ST, D]) for i in range(2)]
            S = {n: sem(n) for n in ("w1_in", "w2_in0", "w2_in1", "slots_in0", "slots_in1", "x_turned", "xt_full_made", "xt_lead_made", "xt_rest_made", "hidden_done",
                                     "gelu_done", "hid_lead_made", "hid_rest_made", "w1_lead_made", "w1_rest_made", "w2_lead_made", "w2_rest_made",
                                     "out_done", "out_kept", "slots_out0", "slots_out1")}
            block = s2.enter_context(nc.Block())

            def turns(engine, step):
                def turn(i):
                    step(i, 0)
                    step(i, 1)
                turn(0)
                with engine.Fori(1, EG // 2 - 1) as i:
                    turn(i)
                turn(EG // 2 - 1)

            def wait(engine, name, value):
                if not isinstance(value, int) or value > 0:
                    engine.wait_ge(S[name], value)

            in_view = in_slots.rearrange("(g j p) c -> p g j c", j=ST, p=P)
            out_view = out_slots.rearrange("(g j p) c -> p g j c", j=ST, p=P)
            w1_view = w1.rearrange("e (k p) f -> p e k f", p=P)
            w2_view = w2.rearrange("e (k p) c -> p e k c", p=P)

            def exists(g):
                return not isinstance(g, int) or 0 <= g < EG

            @block.sync
            def _(sp):
                def step(i, u):
                    g = i * 2 + u
                    e = sp.value_load(expert_of[0:1, bass.ds(g, 1)], min_val=0, max_val=NE - 1)
                    wait(sp, "x_turned", g - 1)
                    sp.sem_inc(waits_passed, 1)
                    sp.dma_start(slot_in[:, u, :, :], in_view[:, bass.ds(g, 1), :, :].rearrange("p a j c -> p (a j) c")).then_inc(S[f"slots_in{u}"], 16)
                    wait(sp, "w2_rest_made", (g - 1) * 2)
                    wait(sp, "w2_lead_made", (g - 1) * 2)
                    sp.sem_inc(waits_passed, 1)
                    sp.dma_start(w2_full[:, u, :, :], w2_view[:, bass.ds(e, 1), :, :].rearrange("p a k c -> p (a k) c")).then_inc(S[f"w2_in{u}"], 16)
                    wait(sp, "w1_rest_made", g * KC)
                    wait(sp, "w1_lead_made", g * KC)
                    sp.sem_inc(waits_passed, 1)
                    sp.dma_start(w1_full, w1_view[:, bass.ds(e, 1), :, :].rearrange("p a k f -> p (a k) f")).then_inc(S["w1_in"], 16)
                turns(sp, step)

            def halves(n):
                return slice(n * FC // 2, (n + 1) * FC // 2)

            @block.gpsimd
            def _(pool):
                def put_out(i, u):
                    g = i * 2 + u
                    wait(pool, "out_kept", g + 1)
                    pool.dma_start(out_view[:, bass.ds(g, 1), :, :].rearrange("p a j c -> p (a j) c"), slot_out[:, u, :, :]).then_inc(S[f"slots_out{u}"], 16)

                turns(pool, put_out)
                for u in range(2):
                    pool.wait_ge(S[f"slots_out{u}"], 16 * (EG // 2))

            @block.scalar
            def _(act):
                def w1_leads(g, u):
                    wait(act, "w1_in", (g + 1) * 16)
                    wait(act, "hidden_done", (g - 1) * FC)
                    for k in range(KC):
                        act.activation(w1_parts[:, u, 0, k, :], w1_full[:, k, :], ACT.Copy).then_inc(S["w1_lead_made"], 1)

                w1_leads(0, 0)

                def step(i, u):
                    g = i * 2 + u
                    e = act.value_load(expert_of[0:1, bass.ds(g, 1)], min_val=0, max_val=NE - 1)
                    wait(act, "x_turned", g + 1)
                    wait(act, "xt_rest_made", g)
                    wait(act, "xt_lead_made", g)
                    for k in range(KC):
                        ins = act.activation(xt_full[:, k, :], ps_x[u][:, k, :], ACT.Identity, bias=gains[:, 1, bass.ds(e * KC + k, 1)],
                                             scale=gains[:, 0, bass.ds(e * KC + k, 1)])
                    ins.then_inc(S["xt_full_made"], 1)
                    wait(act, "xt_full_made", g + 1)
                    wait(act, "hidden_done", (g - 1) * FC)
                    act.activation(xt[:, u, 0, :, :], xt_full, ACT.Copy).then_inc(S["xt_lead_made"], 1)
                    wait(act, "out_done", g)
                    wait(act, "hid_rest_made", g * PF)
                    wait(act, "hid_lead_made", g * PF)
                    for p in range(PF + 1):
                        for f in (2 * p, 2 * p + 1):
                            if f < FC:
                                wait(act, "hidden_done", g * FC + f + 1)
                                act.activation(hid_full[:, f, :], ps_h[f % HB][:, 0:SG], ACT.Gelu, bias=b1t[:, bass.ds(e * FC + f, 1)]).then_inc(S["gelu_done"], 1)
                        if p == 0:
                            continue
                        p -= 1
                        wait(act, "gelu_done", g * FC + 2 * p + 2)
                        act.activation(hid[:, 0, 2 * p:2 * p + 2, :], hid_full[:, 2 * p:2 * p + 2, :], ACT.Copy).then_inc(S["hid_lead_made"], 1)
                    if exists(g + 1):
                        w1_leads(g + 1, 1 - u)
                turns(act, step)

            @block.vector
            def _(dve):
                def w1_rest(g, u, k):
                    wait(dve, "w1_lead_made", g * KC + k + 1)
                    wait(dve, "w1_in", (g + 1) * 16)
                    wait(dve, "hidden_done", (g - 1) * FC)
                    dve.tensor_tensor(w1_parts[:, u, 1, k, :], w1_full[:, k, :], w1_parts[:, u, 0, k, :], ALU.subtract).then_inc(S["w1_rest_made"], 1)

                def w2_lead(i, u, n):
                    g = i * 2 + u
                    wait(dve, f"w2_in{u}", (i + 1) * 16)
                    wait(dve, "out_done", g - 1)
                    dve.tensor_copy(w2_parts[:, u, 0, halves(n), :], w2_full[:, u, halves(n), :]).then_inc(S["w2_lead_made"], 1)

                def w2_rest(g, u, n):
                    wait(dve, "w2_lead_made", g * 2 + n + 1)
                    dve.tensor_tensor(w2_parts[:, u, 1, halves(n), :], w2_full[:, u, halves(n), :], w2_parts[:, u, 0, halves(n), :],
                                      ALU.subtract).then_inc(S["w2_rest_made"], 1)

                def keep_out(i, u):
                    g = i * 2 + u
                    e = dve.value_load(expert_of[0:1, bass.ds(g, 1)], min_val=0, max_val=NE - 1)
                    wait(dve, f"slots_out{u}", i * 16)
                    wait(dve, "out_done", g + 1)
                    dve.tensor_tensor(slot_out[:, u, :, :], ps_y[u][:], b2_all[:, bass.ds(e * D, D)].unsqueeze(1).broadcast_to([P, ST, D]),
                                      ALU.add).then_inc(S["out_kept"], 1)

                for k in range(KC):
                    w1_rest(0, 0, k)
                for n in range(2):
                    w2_lead(0, 0, n)
                    w2_rest(0, 0, n)

                def step(i, u):
                    g = i * 2 + u
                    wait(dve, "xt_lead_made", g + 1)
                    wait(dve, "hidden_done", (g - 1) * FC)
                    dve.tensor_tensor(xt[:, u, 1, :, :], xt_full, xt[:, u, 0, :, :], ALU.subtract).then_inc(S["xt_rest_made"], 1)
                    if exists(g - 1):
                        keep_out(i - (1 - u), 1 - u)
                    if exists(g + 1):
                        for n in range(2):
                            w2_lead(i + (u + 1) // 2, 1 - u, n)
                            w2_rest(g + 1, 1 - u, n)
                    for p in range(PF):
                        wait(dve, "hid_lead_made", g * PF + p + 1)
                        wait(dve, "out_done", g)
                        pair = slice(2 * p, 2 * p + 2)
                        dve.tensor_tensor(hid[:, 1, pair, :], hid_full[:, pair, :], hid[:, 0, pair, :], ALU.subtract).then_inc(S["hid_rest_made"], 1)
                    if exists(g + 1):
                        for k in range(KC):
                            w1_rest(g + 1, 1 - u, k)
                turns(dve, step)
                keep_out(EG // 2 - 1, 1)

            @block.tensor
            def _(pe):
                def turn_slots(i, u):
                    wait(pe, f"slots_in{u}", i * 16 + 16)
                    wait(pe, "xt_full_made", i * 2 + u - 1)
                    for k in range(KC):
                        for j in range(ST):
                            ins = pe.transpose(ps_x[u][:, k, j * P:(j + 1) * P], slot_in[:, u, j, k * P:(k + 1) * P], ident[:])
                    ins.then_inc(S["x_turned"], 1)

                turn_slots(0, 0)

                def step(i, u):
                    g = i * 2 + u
                    wait(pe, "w1_rest_made", (g + 1) * KC)
                    wait(pe, "xt_rest_made", g + 1)
                    for f in range(FC):
                        wait(pe, "gelu_done", g * FC + f + 1 - HB)
                        for n, (a, b) in enumerate(PASSES):
                            for k in range(KC):
                                ins = pe.matmul(ps_h[f % HB][:, 0:SG], w1_parts[:, u, a, k, f * P:(f + 1) * P], xt[:, u, b, k, :],
                                                start=(n == 0 and k == 0), stop=(n == 2 and k == KC - 1))
                        ins.then_inc(S["hidden_done"], 1)
                    if not isinstance(g, int) or g + 1 < EG:
                        turn_slots(i + (u + 1) // 2, (u + 1) % 2)
                    wait(pe, "w2_rest_made", (g + 1) * 2)
                    wait(pe, "out_kept", g - 1)
                    for j in range(ST):
                        for f in range(FC):
                            if j == 0 and f % 2 == 0:
                                wait(pe, "hid_rest_made", g * PF + f // 2 + 1)
                            for n, (a, b) in enumerate(PASSES):
                                ins = pe.matmul(ps_y[u][:, j, :], hid[:, a, f, j * P:(j + 1) * P], w2_parts[:, u, b, f, :],
                                                start=(f == 0 and n == 0), stop=(f == FC - 1 and n == 2))
                    ins.then_inc(S["out_done"], 1)
                turns(pe, step)

        with ExitStack() as s2:
            CB = 4
            slot_all = sb(s2, "c_slot", [P, NT, 2], I32)
            slot_tile = sb(s2, "c_slots", [P, CB, 2], I32)
            y = sb(s2, "c_y", [P, CB, 2, D])
            S = {n: sem(n) for n in ["c_chain", "combined", "c_ready", "stored", "c_staged"] + [f"c_in{u}" for u in range(CB)]}
            block = s2.enter_context(nc.Block())
            TURNS = NT // CB

            def wait(engine, name, value):
                if not isinstance(value, int) or value > 0:
                    engine.wait_ge(S[name], value)

            def turns(engine, step):
                def turn(i):
                    for u in range(CB):
                        step(i, u)
                first_then_rest(engine, TURNS, turn)
                for u in range(NT - TURNS * CB):
                    step(TURNS, u)

            @block.scalar
            def _(act):
                def step(i, u):
                    wait(act, f"c_in{u}", i * 32)
                    act.activation(slot_tile[:, u, :], slot_of[:, bass.ds(i * CB + u, 1), :].rearrange("p a c -> p (a c)"), ACT.Copy).then_inc(S["c_staged"], 1)
                turns(act, step)

            @block.gpsimd
            def _(pool):
                def step(i, u):
                    wait(pool, "c_staged", i * CB + u + 1)
                    wait(pool, "combined", (i - 1) * CB + u + 1)
                    pool.sem_inc(waits_passed, 1)
                    for n in range(2):
                        pool.indirect_dma_start(y[:, u, n, :], None, out_slots, bass.IndirectOffsetOnAxis(slot_tile[:, u, n:n + 1], 0)).then_inc(S[f"c_in{u}"], 16)
                turns(pool, step)

            @block.vector
            def _(dve):
                def step(i, u):
                    t = i * CB + u
                    xt_ = X[:, bass.ds(t, 1), :].rearrange("p a c -> p (a c)")
                    wait(dve, f"c_in{u}", i * 32 + 32)
                    dve.scalar_tensor_tensor(xt_, y[:, u, 0, :], weight[:, bass.ds(t, 1), 0], xt_, ALU.mult, ALU.add).then_inc(S["c_chain"], 1)
                    dve.wait_ge(S["c_chain"], t + 1)
                    dve.scalar_tensor_tensor(xt_, y[:, u, 1, :], weight[:, bass.ds(t, 1), 1], xt_, ALU.mult, ALU.add).then_inc(S["combined"], 1)
                turns(dve, step)

            @block.sync
            def _(sp):
                n = 0
                for t0 in range(0, NT - 1, 8):
                    m = min(8, NT - 1 - t0)
                    sp.wait_ge(S["combined"], t0 + m)
                    sp.dma_start(out[t0 * P:(t0 + m) * P, :].rearrange("(t p) f -> p t f", p=P), X[:, t0:t0 + m, :]).then_inc(S["stored"], 16)
                    n += 16
                sp.wait_ge(S["combined"], NT)
                sp.dma_start(out[(NT - 1) * P:N, :], X[0:LAST, NT - 1, :]).then_inc(S["stored"], 16)
                sp.wait_ge(S["stored"], n + 16)


_INS = ["x", "src", "dst", "L0_gnn_W", "L0_gnn_a_l", "L0_gnn_a_r", "L0_mix_w_qkv", "L0_mix_mem_kv", "L0_mix_w_out", "L0_mix_b_out",
        "L0_mix_g_out", "L0_mix_g_pre", "L0_ffn_Wr", "L0_ffn_br", "L0_ffn_ln_g", "L0_ffn_ln_b", "L0_ffn_W1", "L0_ffn_b1", "L0_ffn_W2",
        "L0_ffn_b2"]
_OUTS = [((6250, 256), "float32")]


def kernel(**inputs):
    import numpy as _np
    import concourse.bacc as _bacc
    from concourse import mybir as _mybir
    from concourse.bass_utils import run_bass_kernel_spmd as _run

    nc = _bacc.Bacc("TRN2", target_bir_lowering=False, num_devices=1)
    arrays, args = {}, []
    for name in _INS:
        a = _np.ascontiguousarray(inputs[name])
        arrays[f"in_{name}_dram"] = a
        args.append(nc.dram_tensor(f"in_{name}_dram", a.shape, _mybir.dt.from_np(a.dtype), kind="ExternalInput").ap())
    for i, (shape, dtype) in enumerate(_OUTS):
        dt = _mybir.dt.from_np(_np.dtype(dtype))
        args.append(nc.dram_tensor(f"out_{i}_dram", shape, dt, kind="ExternalOutput").ap())
    gps_layer_kernel(nc, *args)
    r = _run(nc, [arrays], core_ids=[0])
    return r.results[0]["out_0_dram"]
```
